# Optimizing a Trainium2 kernel written in Bass

```python
import numpy as np
import jax
import jax.numpy as jnp

def _softmax(x, axis=-1):
    return jax.nn.softmax(x, axis=axis)

def _gelu(x):
    return jax.nn.gelu(x, approximate=True)

def _silu(x):
    return jax.nn.silu(x)

def _sigmoid(x):
    return jax.nn.sigmoid(x)

def _layernorm(x, axis=-1, eps=1e-05):
    m = jnp.mean(x, axis=axis, keepdims=True)
    v = jnp.var(x, axis=axis, keepdims=True)
    return (x - m) / jnp.sqrt(v + eps)

def _scatter_add(tgt, idx, src, axis=0):
    return tgt.at[idx].add(src)

def _segment_sum(src, seg, n):
    return jax.ops.segment_sum(src, seg, n)
kernel_name = 'mk_decoder_preln_d4_seqx_r4_12c58d'

def setup_inputs(seed: int=0):
    np.random.seed(seed)
    _w = jnp.asarray

    def _rec_inputs():
        import jax
        import jax.numpy as jnp
        _rk = jax.random.key(seed)
        x = -0.0002928 + 1 * jax.random.normal(jax.random.fold_in(_rk, 1), (16, 128, 256), jnp.float32)
        _lenS = 128 - jax.random.randint(jax.random.fold_in(_rk, 7), (16,), 0, max(1, 128 // 4) + 1, jnp.int32)
        _lenS2 = 128 - jax.random.randint(jax.random.fold_in(_rk, 8), (16,), 0, max(1, 128 // 4) + 1, jnp.int32)
        _ctx_1024P = jax.random.normal(jax.random.fold_in(_rk, 11), (16, 16, 256), jnp.float32)
        _ctx_1024c = jax.random.dirichlet(jax.random.fold_in(_rk, 511), 0.3 * jnp.ones((16,), jnp.float32), (16, 128))
        _ctx_1024t = jnp.einsum('bsk,bkd->bsd', _ctx_1024c, _ctx_1024P)
        _ctx_1024t = _ctx_1024t * jax.lax.rsqrt(jnp.mean(jnp.square(_ctx_1024t)) + 1e-12) * 0.953939
        ctx_1024 = -1.39393e-06 + 0.999914 * (_ctx_1024t + 0.3 * jax.random.normal(jax.random.fold_in(_rk, 611), (16, 128, 256), jnp.float32))
        _validS = jnp.arange(128)[None, :] < _lenS[:, None]
        _validS2 = jnp.arange(128)[None, :] < _lenS2[:, None]
        _causal = jnp.tril(jnp.ones((128, 128), dtype=bool))
        mask_Bx1xSxS2_ik1 = jnp.where(jnp.broadcast_to(_validS2[:, None, None, :], (16, 1, 128, 128)), 1, 0).astype(jnp.int32)
        mask_BxSxS2_if1 = jnp.where(jnp.ones((16, 128, 128), dtype=bool), 1, 0).astype(jnp.int32)
        return (x, ctx_1024, mask_Bx1xSxS2_ik1, mask_BxSxS2_if1)
    x, ctx_1024, mask_Bx1xSxS2_ik1, mask_BxSxS2_if1 = _rec_inputs()

    def _L0_attn_setup():
        import jax, jax.numpy as jnp
        import numpy as np
        B, L, IN_DIM = (4, 512, 256)
        H, D = (16, 64)
        OUT_DIM = 256
        key = jax.random.key(seed)
        k1, k2, k3 = jax.random.split(key, 3)
        inputs = jax.random.normal(k1, (B, L, IN_DIM), dtype=jnp.float32)
        W_qkv = jax.random.normal(k2, (IN_DIM, 3 * H * D), dtype=jnp.float32) * IN_DIM ** (-0.5)
        W_out = jax.random.normal(k3, (H * D, OUT_DIM), dtype=jnp.float32) * (H * D) ** (-0.5)
        return {'inputs': inputs, 'W_qkv': W_qkv, 'W_out': W_out}
    _L0_attn_all = _L0_attn_setup()
    _L0_attn_in = {k: v for k, v in _L0_attn_all.items() if k in ('W_qkv', 'W_out')}
    del _L0_attn_all

    def _L0_xattn_setup():
        import jax, jax.numpy as jnp
        import numpy as np
        B, NQ, NKV = (2, 512, 512)
        DIM, CTX_DIM = (256, 256)
        HEADS, DIM_HEAD = (16, 64)
        INNER = HEADS * DIM_HEAD
        SCALE = DIM_HEAD ** (-0.5)
        key = jax.random.key(seed)
        ks = jax.random.split(key, 6)
        x = jax.random.normal(ks[0], (B, NQ, DIM), dtype=jnp.float32)
        context = jax.random.normal(ks[1], (B, NKV, CTX_DIM), dtype=jnp.float32)
        Wq = jax.random.normal(ks[2], (DIM, INNER), dtype=jnp.float32) / np.sqrt(DIM)
        Wkv = jax.random.normal(ks[3], (CTX_DIM, 2 * INNER), dtype=jnp.float32) / np.sqrt(CTX_DIM)
        Wout = jax.random.normal(ks[4], (INNER, DIM), dtype=jnp.float32) / np.sqrt(INNER)
        bout = jax.random.normal(ks[5], (DIM,), dtype=jnp.float32) * 0.01
        return {'x': x, 'context': context, 'Wq': Wq, 'Wkv': Wkv, 'Wout': Wout, 'bout': bout}
    _L0_xattn_all = _L0_xattn_setup()
    _L0_xattn_in = {k: v for k, v in _L0_xattn_all.items() if k in ('Wq', 'Wkv', 'Wout', 'bout')}
    del _L0_xattn_all

    def _L0_ffn_setup():
        import jax, jax.numpy as jnp
        import numpy as np
        N_EMBED = 256
        FFN_HIDDEN = 1024
        NUM_EXPERTS = 8
        TOP_K = 2
        key = jax.random.key(seed)
        ks = jax.random.split(key, 8)
        d, f, E = (N_EMBED, FFN_HIDDEN, NUM_EXPERTS)
        s_d = 1.0 / np.sqrt(d)
        s_f = 1.0 / np.sqrt(f)
        return {'x': jax.random.normal(ks[0], (2, 512, d), dtype=jnp.float32), 'Wg': jax.random.uniform(ks[1], (d, E), jnp.float32, -s_d, s_d), 'bg': jax.random.uniform(ks[2], (E,), jnp.float32, -s_d, s_d), 'W1': jax.random.uniform(ks[3], (E, d, f), jnp.float32, -s_d, s_d), 'b1': jax.random.uniform(ks[4], (E, f), jnp.float32, -s_d, s_d), 'W2': jax.random.uniform(ks[5], (E, f, d), jnp.float32, -s_f, s_f), 'b2': jax.random.uniform(ks[6], (E, d), jnp.float32, -s_f, s_f)}
    _L0_ffn_all = _L0_ffn_setup()
    _L0_ffn_in = {k: v for k, v in _L0_ffn_all.items() if k in ('Wg', 'bg', 'W1', 'b1', 'W2', 'b2')}
    del _L0_ffn_all

    def _L1_attn_setup():
        import jax, jax.numpy as jnp
        import numpy as np
        import math
        D_MODEL = 256
        N_HEADS = 16
        HEAD_DIM = D_MODEL // N_HEADS
        FEAT = 16
        WINDOW = 64
        EPS_NORM = 1e-06
        EPS_LIN = 1e-06
        CHUNK = 128

        def rmsnorm(x, w):
            return x * jax.lax.rsqrt(jnp.mean(x * x, axis=-1, keepdims=True) + EPS_NORM) * w

        def taylor_feature_map(x):
            d = x.shape[-1]
            iu, ju = jnp.triu_indices(d)
            scale = jnp.where(iu == ju, 0.5, 1.0 / math.sqrt(2.0)).astype(x.dtype)
            quad = x[..., iu] * x[..., ju] * scale
            ones = jnp.ones(x.shape[:-1] + (1,), dtype=x.dtype)
            return jnp.concatenate([ones, x, quad], axis=-1)

        def linear_attention_causal(q_phi, k_phi, v):
            B, T, H, F = q_phi.shape
            D = v.shape[-1]
            Nc = T // CHUNK
            qc = q_phi.reshape(B, Nc, CHUNK, H, F).transpose(1, 0, 2, 3, 4)
            kc = k_phi.reshape(B, Nc, CHUNK, H, F).transpose(1, 0, 2, 3, 4)
            vc = v.reshape(B, Nc, CHUNK, H, D).transpose(1, 0, 2, 3, 4)
            causal = jnp.tril(jnp.ones((CHUNK, CHUNK), dtype=q_phi.dtype))

            def step(carry, inp):
                kv, ksum = carry
                qb, kb, vb = inp
                A = jnp.einsum('bchf,bshf->bhcs', qb, kb) * causal
                y = jnp.einsum('bhcs,bshd->bchd', A, vb) + jnp.einsum('bchf,bhfd->bchd', qb, kv)
                z = jnp.einsum('bhcs->bch', A) + jnp.einsum('bchf,bhf->bch', qb, ksum)
                kv = kv + jnp.einsum('bshf,bshd->bhfd', kb, vb)
                ksum = ksum + kb.sum(axis=1)
                return ((kv, ksum), y / (z[..., None] + EPS_LIN))
            kv0 = jnp.zeros((B, H, F, D), dtype=q_phi.dtype)
            ks0 = jnp.zeros((B, H, F), dtype=q_phi.dtype)
            _, ys = jax.lax.scan(step, (kv0, ks0), (qc, kc, vc))
            return ys.transpose(1, 0, 2, 3, 4).reshape(B, T, H, D)

        def sliding_window_attention(q, k, v):
            B, T, H, D = q.shape
            scale = 1.0 / math.sqrt(D)
            t = jnp.arange(T)
            allowed = (t[None, :] <= t[:, None]) & (t[None, :] >= t[:, None] - WINDOW)
            scores = jnp.einsum('bqhd,bkhd->bhqk', q, k) * scale
            scores = jnp.where(allowed[None, None], scores, -jnp.inf)
            attn = jax.nn.softmax(scores, axis=-1)
            out = jnp.einsum('bhqk,bkhd->bqhd', attn, v)
            return out.reshape(B, T, H * D)
        key = jax.random.key(seed)
        ks = jax.random.split(key, 7)
        B, T = (2, 512)
        s = 0.02
        return {'x': jax.random.normal(ks[0], (B, T, D_MODEL), jnp.float32), 'norm_w': jnp.ones((D_MODEL,), jnp.float32), 'Wq': jax.random.normal(ks[1], (D_MODEL, D_MODEL), jnp.float32) * s, 'Wk': jax.random.normal(ks[2], (D_MODEL, D_MODEL), jnp.float32) * s, 'Wv': jax.random.normal(ks[3], (D_MODEL, D_MODEL), jnp.float32) * s, 'Wqf': jax.random.normal(ks[4], (HEAD_DIM, FEAT), jnp.float32) * s, 'Wkf': jax.random.normal(ks[5], (HEAD_DIM, FEAT), jnp.float32) * s, 'Wout': jax.random.normal(ks[6], (2 * D_MODEL, D_MODEL), jnp.float32) * s}
    _L1_attn_all = _L1_attn_setup()
    _L1_attn_in = {k: v for k, v in _L1_attn_all.items() if k in ('norm_w', 'Wq', 'Wk', 'Wv', 'Wqf', 'Wkf', 'Wout')}
    del _L1_attn_all

    def _L1_xattn_setup():
        import jax, jax.numpy as jnp
        import numpy as np
        D_MODEL = 256
        H = 16
        D_K = D_MODEL // H
        B = 2
        S = 512

        def _split_heads(x):
            b, s, _ = x.shape
            return x.reshape(b, s, H, D_K).transpose(0, 2, 1, 3)
        key = jax.random.key(seed)
        ks = jax.random.split(key, 13)
        scale = 1.0 / np.sqrt(D_MODEL)
        inp = {'Q': jax.random.normal(ks[0], (B, S, D_MODEL), jnp.float32), 'K': jax.random.normal(ks[1], (B, S, D_MODEL), jnp.float32), 'V': jax.random.normal(ks[2], (B, S, D_MODEL), jnp.float32), 'mask': jax.random.randint(ks[3], (B, 1, S, S), 0, 2, jnp.int32), 'WQ_w': jax.random.normal(ks[4], (D_MODEL, D_MODEL), jnp.float32) * scale, 'WQ_b': jax.random.normal(ks[5], (D_MODEL,), jnp.float32) * scale, 'WK_w': jax.random.normal(ks[6], (D_MODEL, D_MODEL), jnp.float32) * scale, 'WK_b': jax.random.normal(ks[7], (D_MODEL,), jnp.float32) * scale, 'WV_w': jax.random.normal(ks[8], (D_MODEL, D_MODEL), jnp.float32) * scale, 'WV_b': jax.random.normal(ks[9], (D_MODEL,), jnp.float32) * scale, 'WO_w': jax.random.normal(ks[10], (D_MODEL, D_MODEL), jnp.float32) * scale, 'WO_b': jax.random.normal(ks[11], (D_MODEL,), jnp.float32) * scale}
        return inp
    _L1_xattn_all = _L1_xattn_setup()
    _L1_xattn_in = {k: v for k, v in _L1_xattn_all.items() if k in ('WQ_w', 'WQ_b', 'WK_w', 'WK_b', 'WV_w', 'WV_b', 'WO_w', 'WO_b')}
    del _L1_xattn_all

    def _L1_ffn_setup():
        import jax, jax.numpy as jnp
        import numpy as np
        B, S, D, F, E, K = (2, 512, 256, 1024, 8, 2)
        key = jax.random.key(seed)
        ks = jax.random.split(key, 5)
        x = jax.random.normal(ks[0], (B, S, D), dtype=jnp.float32)
        Wg = jax.random.normal(ks[1], (D, E), dtype=jnp.float32) * 0.02
        W1 = jax.random.normal(ks[2], (E, D, F), dtype=jnp.float32) * 0.02
        b1 = jnp.zeros((E, F), dtype=jnp.float32)
        W2 = jax.random.normal(ks[3], (E, F, D), dtype=jnp.float32) * 0.02
        b2 = jnp.zeros((E, D), dtype=jnp.float32)
        return {'x': x, 'Wg': Wg, 'W1': W1, 'b1': b1, 'W2': W2, 'b2': b2}
    _L1_ffn_all = _L1_ffn_setup()
    _L1_ffn_in = {k: v for k, v in _L1_ffn_all.items() if k in ('Wg', 'W1', 'b1', 'W2', 'b2')}
    del _L1_ffn_all

    def _L2_attn_setup():
        import jax, jax.numpy as jnp
        import numpy as np
        D_MODEL = 256
        N_HEADS = 16
        ORDER = 6
        P2 = 2 * ORDER - 1
        EPS_CLAMP = 1e-06
        EPS_DEN = 1e-07

        def _beta_np():
            j = np.arange(ORDER, dtype=np.float32)
            alpha = (j + 1.0) ** (-1.5)
            tail = np.flip(np.cumsum(np.flip(alpha)))
            beta = np.concatenate([np.zeros(1, np.float32), tail[1:].astype(np.float32), np.zeros(ORDER - 1, np.float32)])
            return beta / beta.sum()

        def _cheb(x):
            T = [jnp.ones_like(x), x]
            for _ in range(2, P2):
                T.append(2.0 * x * T[-1] - T[-2])
            return jnp.stack(T, axis=3)
        key = jax.random.key(seed)
        k1, k2, k3 = jax.random.split(key, 3)
        B, S, D = (2, 256, D_MODEL)
        x = jax.random.normal(k1, (B, S, D), dtype=jnp.float32)
        W_in = jax.random.normal(k2, (3 * D, D), dtype=jnp.float32) * 0.02
        W_out = jax.random.normal(k3, (D, D), dtype=jnp.float32) * 0.02
        return {'x': x, 'W_in': W_in, 'W_out': W_out}
    _L2_attn_all = _L2_attn_setup()
    _L2_attn_in = {k: v for k, v in _L2_attn_all.items() if k in ('W_in', 'W_out')}
    del _L2_attn_all

    def _L2_xattn_setup():
        import jax, jax.numpy as jnp
        import numpy as np
        HIDDEN = 256
        N_HEADS = 16
        HEAD_DIM = HIDDEN // N_HEADS
        SCALE = HEAD_DIM ** (-0.5)
        B, QL, KVL = (2, 512, 1024)
        key = jax.random.key(seed)
        ks = jax.random.split(key, 7)
        s = 0.02
        return {'query_states': jax.random.normal(ks[0], (B, QL, HIDDEN), jnp.float32), 'key_states': jax.random.normal(ks[1], (B, KVL, HIDDEN), jnp.float32), 'value_states': jax.random.normal(ks[2], (B, KVL, HIDDEN), jnp.float32), 'Wq': jax.random.normal(ks[3], (HIDDEN, HIDDEN), jnp.float32) * s, 'Wk': jax.random.normal(ks[4], (HIDDEN, HIDDEN), jnp.float32) * s, 'Wv': jax.random.normal(ks[5], (HIDDEN, HIDDEN), jnp.float32) * s, 'Wo': jax.random.normal(ks[6], (HIDDEN, HIDDEN), jnp.float32) * s}
    _L2_xattn_all = _L2_xattn_setup()
    _L2_xattn_in = {k: v for k, v in _L2_xattn_all.items() if k in ('Wq', 'Wk', 'Wv', 'Wo')}
    del _L2_xattn_all

    def _L2_ffn_setup():
        import jax, jax.numpy as jnp
        import numpy as np
        B, S, D, DO = (4, 512, 256, 256)
        E, K = (20, 2)
        key = jax.random.key(seed)
        ks = jax.random.split(key, 6)
        sc_d = 1.0 / np.sqrt(D)
        sc_h = 1.0 / np.sqrt(D // 4)
        return {'x': jax.random.normal(ks[0], (B, S, D), jnp.float32), 'wg1': jax.random.normal(ks[1], (D, D // 4), jnp.float32) * sc_d, 'bg1': jnp.zeros((D // 4,), jnp.float32), 'wg2': jax.random.normal(ks[2], (D // 4, 2 * E), jnp.float32) * sc_h, 'bg2': jnp.zeros((2 * E,), jnp.float32), 'We': jax.random.normal(ks[3], (E, D, DO), jnp.float32) * sc_d, 'be': jnp.zeros((E, DO), jnp.float32)}
    _L2_ffn_all = _L2_ffn_setup()
    _L2_ffn_in = {k: v for k, v in _L2_ffn_all.items() if k in ('wg1', 'bg1', 'wg2', 'bg2', 'We', 'be')}
    del _L2_ffn_all

    def _L3_attn_setup():
        import math
        import jax, jax.numpy as jnp
        import numpy as np
        D_MODEL = 256
        N_HEADS = 16
        D_HEAD = D_MODEL // N_HEADS

        def get_alibi_slopes(n_heads: int) -> np.ndarray:

            def pow2_slopes(n):
                start = 2 ** (-2 ** (-(math.log2(n) - 3)))
                return np.array([start * start ** i for i in range(n)], dtype=np.float32)
            if math.log2(n_heads).is_integer():
                return pow2_slopes(n_heads)
            closest = 2 ** math.floor(math.log2(n_heads))
            slopes = pow2_slopes(closest)
            extra = pow2_slopes(2 * closest)[0::2][:n_heads - closest]
            return np.concatenate([slopes, extra], axis=0)
        key = jax.random.key(seed)
        ks = jax.random.split(key, 9)
        B, S, D = (2, 512, D_MODEL)
        scale = 1.0 / math.sqrt(D)
        inp = {'x': jax.random.normal(ks[0], (B, S, D), dtype=jnp.float32), 'Wq': jax.random.normal(ks[1], (D, D), dtype=jnp.float32) * scale, 'bq': jnp.zeros((D,), dtype=jnp.float32), 'Wk': jax.random.normal(ks[2], (D, D), dtype=jnp.float32) * scale, 'bk': jnp.zeros((D,), dtype=jnp.float32), 'Wv': jax.random.normal(ks[3], (D, D), dtype=jnp.float32) * scale, 'bv': jnp.zeros((D,), dtype=jnp.float32), 'Wo': jax.random.normal(ks[4], (D, D), dtype=jnp.float32) * scale, 'bo': jnp.zeros((D,), dtype=jnp.float32)}
        return inp
    _L3_attn_all = _L3_attn_setup()
    _L3_attn_in = {k: v for k, v in _L3_attn_all.items() if k in ('Wq', 'bq', 'Wk', 'bk', 'Wv', 'bv', 'Wo', 'bo')}
    del _L3_attn_all

    def _L3_xattn_setup():
        import jax, jax.numpy as jnp
        import numpy as np
        N_HEADS = 16
        D_MODEL = 256
        HEAD_DIM = D_MODEL // N_HEADS
        B, S = (2, 512)
        key = jax.random.key(seed)
        ks = jax.random.split(key, 10)
        scale = 1.0 / np.sqrt(D_MODEL)
        inp = {'query_tokens': jax.random.normal(ks[0], (B, S, D_MODEL), dtype=jnp.float32), 'key_or_value_tokens': jax.random.normal(ks[1], (B, S, D_MODEL), dtype=jnp.float32), 'mask': jnp.ones((B, S, S), dtype=jnp.int32), 'Wq': jax.random.normal(ks[2], (D_MODEL, D_MODEL), dtype=jnp.float32) * scale, 'bq': jnp.zeros((D_MODEL,), dtype=jnp.float32), 'Wk': jax.random.normal(ks[3], (D_MODEL, D_MODEL), dtype=jnp.float32) * scale, 'bk': jnp.zeros((D_MODEL,), dtype=jnp.float32), 'Wv': jax.random.normal(ks[4], (D_MODEL, D_MODEL), dtype=jnp.float32) * scale, 'bv': jnp.zeros((D_MODEL,), dtype=jnp.float32), 'Wo': jax.random.normal(ks[5], (D_MODEL, D_MODEL), dtype=jnp.float32) * scale, 'bo': jnp.zeros((D_MODEL,), dtype=jnp.float32)}
        return inp
    _L3_xattn_all = _L3_xattn_setup()
    _L3_xattn_in = {k: v for k, v in _L3_xattn_all.items() if k in ('Wq', 'bq', 'Wk', 'bk', 'Wv', 'bv', 'Wo', 'bo')}
    del _L3_xattn_all

    def _L3_ffn_setup():
        import jax, jax.numpy as jnp
        import numpy as np
        DIM = 256
        DEPTH = 2
        HEADS = 8
        DIM_HEAD = 64
        WINDOW = 128
        INNER = HEADS * DIM_HEAD
        HID = int(DIM * 4 * 2 / 3)
        B, N = (2, 2048)
        QK_SCALE = 8.0

        def shift_token(t):
            t1, t2 = jnp.split(t, 2, axis=-1)
            t2 = jnp.pad(t2, ((0, 0), (1, 0), (0, 0)))[:, :-1]
            return jnp.concatenate([t1, t2], axis=-1)

        def l2norm(t):
            return t / jnp.clip(jnp.linalg.norm(t, axis=-1, keepdims=True), 1e-12)

        def rotate_half(x):
            x1, x2 = jnp.split(x, 2, axis=-1)
            return jnp.concatenate([-x2, x1], axis=-1)

        def rotary_xpos(q, k):
            n = q.shape[-2]
            half_idx = jnp.arange(0, DIM_HEAD, 2, dtype=jnp.float32)
            inv_freq = 1.0 / 10000.0 ** (half_idx / DIM_HEAD)
            t = jnp.arange(n, dtype=jnp.float32)
            freqs = t[:, None] * inv_freq[None, :]
            freqs = jnp.concatenate([freqs, freqs], axis=-1)
            base = (half_idx + 0.4 * DIM_HEAD) / (1.4 * DIM_HEAD)
            power = (t - n // 2) / float(WINDOW // 2)
            scale = base[None, :] ** power[:, None]
            scale = jnp.concatenate([scale, scale], axis=-1)
            cos, sin = (jnp.cos(freqs), jnp.sin(freqs))
            q = q * cos * scale + rotate_half(q) * sin * scale
            k = k * cos / scale + rotate_half(k) * sin / scale
            return (q, k)

        def local_attention(q, k, v):
            b, h, n, d = q.shape
            w = n // WINDOW
            bq = q.reshape(b, h, w, WINDOW, d) * QK_SCALE
            bk = k.reshape(b, h, w, WINDOW, d)
            bv = v.reshape(b, h, w, WINDOW, d)

            def look_around(t):
                p = jnp.pad(t, ((0, 0), (0, 0), (1, 0), (0, 0), (0, 0)))
                return jnp.concatenate([p[:, :, :w], p[:, :, 1:]], axis=3)
            bk, bv = (look_around(bk), look_around(bv))
            bt = jnp.arange(n).reshape(w, WINDOW)
            btp = jnp.pad(bt, ((1, 0), (0, 0)), constant_values=-1)
            btk = jnp.concatenate([btp[:w], btp[1:]], axis=1)
            sim = jnp.einsum('bhwid,bhwjd->bhwij', bq, bk)
            i = bt[:, :, None]
            j = btk[:, None, :]
            mask = (i < j) | (i > j + WINDOW) | (j == -1)
            sim = jnp.where(mask, -jnp.finfo(sim.dtype).max, sim)
            attn = jax.nn.softmax(sim, axis=-1)
            out = jnp.einsum('bhwij,bhwjd->bhwid', attn, bv)
            return out.reshape(b, h, n, d)

        def _layer(x, wqkv, qs, ksc, wo, lg, lb, w1, b1, w2, b2):
            b, n, _ = x.shape
            h = shift_token(x)
            qkv = h @ wqkv
            q, k, v = jnp.split(qkv, 3, axis=-1)
            to_heads = lambda t: t.reshape(b, n, HEADS, DIM_HEAD).transpose(0, 2, 1, 3)
            q, k, v = (to_heads(q), to_heads(k), to_heads(v))
            q = l2norm(q) * qs
            k = l2norm(k) * ksc
            q, k = rotary_xpos(q, k)
            o = local_attention(q, k, v)
            o = o.transpose(0, 2, 1, 3).reshape(b, n, INNER)
            x = x + o @ wo
            h = shift_token(x)
            mu = h.mean(-1, keepdims=True)
            var = h.var(-1, keepdims=True)
            h = (h - mu) / jnp.sqrt(var + 1e-05) * lg + lb
            h = h @ w1 + b1
            a, g = jnp.split(h, 2, axis=-1)
            h = a * jax.nn.gelu(g, approximate=False)
            x = x + h @ w2 + b2
            return x
        key = jax.random.key(seed)
        ks = jax.random.split(key, 6)
        return {'x': jax.random.normal(ks[0], (B, N, DIM), jnp.float32), 'wqkv': jax.random.normal(ks[1], (DEPTH, DIM, 3 * INNER), jnp.float32) * 0.02, 'q_scale': jnp.ones((DEPTH, DIM_HEAD), jnp.float32), 'k_scale': jnp.ones((DEPTH, DIM_HEAD), jnp.float32), 'wo': jax.random.normal(ks[2], (DEPTH, INNER, DIM), jnp.float32) * 0.02, 'ln_g': jnp.ones((DEPTH, DIM), jnp.float32), 'ln_b': jnp.zeros((DEPTH, DIM), jnp.float32), 'w1': jax.random.normal(ks[3], (DEPTH, DIM, 2 * HID), jnp.float32) * 0.02, 'b1': jnp.zeros((DEPTH, 2 * HID), jnp.float32), 'w2': jax.random.normal(ks[4], (DEPTH, HID, DIM), jnp.float32) * 0.02, 'b2': jnp.zeros((DEPTH, DIM), jnp.float32)}
    _L3_ffn_all = _L3_ffn_setup()
    _L3_ffn_in = {k: v for k, v in _L3_ffn_all.items() if k in ('wqkv', 'q_scale', 'k_scale', 'wo', 'ln_g', 'ln_b', 'w1', 'b1', 'w2', 'b2')}
    del _L3_ffn_all
    return {'x': x, 'ctx_1024': ctx_1024, 'mask_Bx1xSxS2_ik1': mask_Bx1xSxS2_ik1, 'mask_BxSxS2_if1': mask_BxSxS2_if1, 'L0_attn_W_qkv': _L0_attn_in['W_qkv'], 'L0_attn_W_out': _L0_attn_in['W_out'], 'L0_xattn_Wq': _L0_xattn_in['Wq'], 'L0_xattn_Wkv': _L0_xattn_in['Wkv'], 'L0_xattn_Wout': _L0_xattn_in['Wout'], 'L0_xattn_bout': _L0_xattn_in['bout'], 'L0_ffn_Wg': _L0_ffn_in['Wg'], 'L0_ffn_bg': _L0_ffn_in['bg'], 'L0_ffn_W1': _L0_ffn_in['W1'], 'L0_ffn_b1': _L0_ffn_in['b1'], 'L0_ffn_W2': _L0_ffn_in['W2'], 'L0_ffn_b2': _L0_ffn_in['b2'], 'L1_attn_norm_w': _L1_attn_in['norm_w'], 'L1_attn_Wq': _L1_attn_in['Wq'], 'L1_attn_Wk': _L1_attn_in['Wk'], 'L1_attn_Wv': _L1_attn_in['Wv'], 'L1_attn_Wqf': _L1_attn_in['Wqf'], 'L1_attn_Wkf': _L1_attn_in['Wkf'], 'L1_attn_Wout': _L1_attn_in['Wout'], 'L1_xattn_WQ_w': _L1_xattn_in['WQ_w'], 'L1_xattn_WQ_b': _L1_xattn_in['WQ_b'], 'L1_xattn_WK_w': _L1_xattn_in['WK_w'], 'L1_xattn_WK_b': _L1_xattn_in['WK_b'], 'L1_xattn_WV_w': _L1_xattn_in['WV_w'], 'L1_xattn_WV_b': _L1_xattn_in['WV_b'], 'L1_xattn_WO_w': _L1_xattn_in['WO_w'], 'L1_xattn_WO_b': _L1_xattn_in['WO_b'], 'L1_ffn_Wg': _L1_ffn_in['Wg'], 'L1_ffn_W1': _L1_ffn_in['W1'], 'L1_ffn_b1': _L1_ffn_in['b1'], 'L1_ffn_W2': _L1_ffn_in['W2'], 'L1_ffn_b2': _L1_ffn_in['b2'], 'L2_attn_W_in': _L2_attn_in['W_in'], 'L2_attn_W_out': _L2_attn_in['W_out'], 'L2_xattn_Wq': _L2_xattn_in['Wq'], 'L2_xattn_Wk': _L2_xattn_in['Wk'], 'L2_xattn_Wv': _L2_xattn_in['Wv'], 'L2_xattn_Wo': _L2_xattn_in['Wo'], 'L2_ffn_wg1': _L2_ffn_in['wg1'], 'L2_ffn_bg1': _L2_ffn_in['bg1'], 'L2_ffn_wg2': _L2_ffn_in['wg2'], 'L2_ffn_bg2': _L2_ffn_in['bg2'], 'L2_ffn_We': _L2_ffn_in['We'], 'L2_ffn_be': _L2_ffn_in['be'], 'L3_attn_Wq': _L3_attn_in['Wq'], 'L3_attn_bq': _L3_attn_in['bq'], 'L3_attn_Wk': _L3_attn_in['Wk'], 'L3_attn_bk': _L3_attn_in['bk'], 'L3_attn_Wv': _L3_attn_in['Wv'], 'L3_attn_bv': _L3_attn_in['bv'], 'L3_attn_Wo': _L3_attn_in['Wo'], 'L3_attn_bo': _L3_attn_in['bo'], 'L3_xattn_Wq': _L3_xattn_in['Wq'], 'L3_xattn_bq': _L3_xattn_in['bq'], 'L3_xattn_Wk': _L3_xattn_in['Wk'], 'L3_xattn_bk': _L3_xattn_in['bk'], 'L3_xattn_Wv': _L3_xattn_in['Wv'], 'L3_xattn_bv': _L3_xattn_in['bv'], 'L3_xattn_Wo': _L3_xattn_in['Wo'], 'L3_xattn_bo': _L3_xattn_in['bo'], 'L3_ffn_wqkv': _L3_ffn_in['wqkv'], 'L3_ffn_q_scale': _L3_ffn_in['q_scale'], 'L3_ffn_k_scale': _L3_ffn_in['k_scale'], 'L3_ffn_wo': _L3_ffn_in['wo'], 'L3_ffn_ln_g': _L3_ffn_in['ln_g'], 'L3_ffn_ln_b': _L3_ffn_in['ln_b'], 'L3_ffn_w1': _L3_ffn_in['w1'], 'L3_ffn_b1': _L3_ffn_in['b1'], 'L3_ffn_w2': _L3_ffn_in['w2'], 'L3_ffn_b2': _L3_ffn_in['b2']}

def reference(x, ctx_1024, mask_Bx1xSxS2_ik1, mask_BxSxS2_if1, L0_attn_W_qkv, L0_attn_W_out, L0_xattn_Wq, L0_xattn_Wkv, L0_xattn_Wout, L0_xattn_bout, L0_ffn_Wg, L0_ffn_bg, L0_ffn_W1, L0_ffn_b1, L0_ffn_W2, L0_ffn_b2, L1_attn_norm_w, L1_attn_Wq, L1_attn_Wk, L1_attn_Wv, L1_attn_Wqf, L1_attn_Wkf, L1_attn_Wout, L1_xattn_WQ_w, L1_xattn_WQ_b, L1_xattn_WK_w, L1_xattn_WK_b, L1_xattn_WV_w, L1_xattn_WV_b, L1_xattn_WO_w, L1_xattn_WO_b, L1_ffn_Wg, L1_ffn_W1, L1_ffn_b1, L1_ffn_W2, L1_ffn_b2, L2_attn_W_in, L2_attn_W_out, L2_xattn_Wq, L2_xattn_Wk, L2_xattn_Wv, L2_xattn_Wo, L2_ffn_wg1, L2_ffn_bg1, L2_ffn_wg2, L2_ffn_bg2, L2_ffn_We, L2_ffn_be, L3_attn_Wq, L3_attn_bq, L3_attn_Wk, L3_attn_bk, L3_attn_Wv, L3_attn_bv, L3_attn_Wo, L3_attn_bo, L3_xattn_Wq, L3_xattn_bq, L3_xattn_Wk, L3_xattn_bk, L3_xattn_Wv, L3_xattn_bv, L3_xattn_Wo, L3_xattn_bo, L3_ffn_wqkv, L3_ffn_q_scale, L3_ffn_k_scale, L3_ffn_wo, L3_ffn_ln_g, L3_ffn_ln_b, L3_ffn_w1, L3_ffn_b1, L3_ffn_w2, L3_ffn_b2):
    import jax
    import jax.numpy as jnp

    def _L0_attn_ref(inputs, W_qkv, W_out):
        import jax, jax.numpy as jnp
        import numpy as np
        B, L, IN_DIM = (4, 512, 256)
        H, D = (16, 64)
        OUT_DIM = 256
        b, l, _ = inputs.shape
        qkv = inputs @ W_qkv
        q, k, v = jnp.split(qkv, 3, axis=-1)
        q = q.reshape(b, l, H, D)
        k = k.reshape(b, l, H, D)
        v = v.reshape(b, l, H, D)
        score = jnp.einsum('bihd,bjhd->bijh', q, k) / D ** 0.5
        mask = jnp.tril(jnp.ones((l, l), dtype=score.dtype))[None, :, :, None]
        masked_score = score * mask + 1e+30 * (mask - 1.0)
        wmat = jax.nn.softmax(masked_score, axis=2)
        out = jnp.einsum('bijh,bjhd->bihd', wmat, v).reshape(b, l, H * D)
        return out @ W_out

    def _L0_xattn_ref(x, context, Wq, Wkv, Wout, bout):
        import jax, jax.numpy as jnp
        import numpy as np
        B, NQ, NKV = (2, 512, 512)
        DIM, CTX_DIM = (256, 256)
        HEADS, DIM_HEAD = (16, 64)
        INNER = HEADS * DIM_HEAD
        SCALE = DIM_HEAD ** (-0.5)
        q = x @ Wq
        kv = context @ Wkv
        k, v = jnp.split(kv, 2, axis=-1)

        def split_heads(t):
            return t.reshape(t.shape[0], t.shape[1], HEADS, DIM_HEAD).transpose(0, 2, 1, 3)
        q, k, v = (split_heads(q), split_heads(k), split_heads(v))
        dots = jnp.einsum('bhqd,bhkd->bhqk', q, k) * SCALE
        attn = jax.nn.softmax(dots, axis=-1)
        out = jnp.einsum('bhqk,bhkd->bhqd', attn, v)
        out = out.transpose(0, 2, 1, 3).reshape(out.shape[0], out.shape[2], INNER)
        return out @ Wout + bout

    def _L0_ffn_ref(x, Wg, bg, W1, b1, W2, b2):
        import jax, jax.numpy as jnp
        import numpy as np
        N_EMBED = 256
        FFN_HIDDEN = 1024
        NUM_EXPERTS = 8
        TOP_K = 2
        gate_scores = jax.nn.softmax(x @ Wg + bg, axis=-1)
        topk_scores, topk_idx = jax.lax.top_k(gate_scores, TOP_K)
        topk_scores = topk_scores / (jnp.sum(topk_scores, axis=-1, keepdims=True) + 1e-08)
        onehot = jax.nn.one_hot(topk_idx, NUM_EXPERTS, dtype=x.dtype)
        combine_w = jnp.einsum('bsk,bske->bse', topk_scores, onehot)
        output = jnp.zeros_like(x)
        for e in range(NUM_EXPERTS):
            h = jax.nn.gelu(x @ W1[e] + b1[e])
            y = h @ W2[e] + b2[e]
            output = output + y * combine_w[..., e:e + 1]
        return output

    def _L1_attn_ref(x, norm_w, Wq, Wk, Wv, Wqf, Wkf, Wout):
        import jax, jax.numpy as jnp
        import numpy as np
        import math
        D_MODEL = 256
        N_HEADS = 16
        HEAD_DIM = D_MODEL // N_HEADS
        FEAT = 16
        WINDOW = 64
        EPS_NORM = 1e-06
        EPS_LIN = 1e-06
        CHUNK = 128

        def rmsnorm(x, w):
            return x * jax.lax.rsqrt(jnp.mean(x * x, axis=-1, keepdims=True) + EPS_NORM) * w

        def taylor_feature_map(x):
            d = x.shape[-1]
            iu, ju = jnp.triu_indices(d)
            scale = jnp.where(iu == ju, 0.5, 1.0 / math.sqrt(2.0)).astype(x.dtype)
            quad = x[..., iu] * x[..., ju] * scale
            ones = jnp.ones(x.shape[:-1] + (1,), dtype=x.dtype)
            return jnp.concatenate([ones, x, quad], axis=-1)

        def linear_attention_causal(q_phi, k_phi, v):
            B, T, H, F = q_phi.shape
            D = v.shape[-1]
            Nc = T // CHUNK
            qc = q_phi.reshape(B, Nc, CHUNK, H, F).transpose(1, 0, 2, 3, 4)
            kc = k_phi.reshape(B, Nc, CHUNK, H, F).transpose(1, 0, 2, 3, 4)
            vc = v.reshape(B, Nc, CHUNK, H, D).transpose(1, 0, 2, 3, 4)
            causal = jnp.tril(jnp.ones((CHUNK, CHUNK), dtype=q_phi.dtype))

            def step(carry, inp):
                kv, ksum = carry
                qb, kb, vb = inp
                A = jnp.einsum('bchf,bshf->bhcs', qb, kb) * causal
                y = jnp.einsum('bhcs,bshd->bchd', A, vb) + jnp.einsum('bchf,bhfd->bchd', qb, kv)
                z = jnp.einsum('bhcs->bch', A) + jnp.einsum('bchf,bhf->bch', qb, ksum)
                kv = kv + jnp.einsum('bshf,bshd->bhfd', kb, vb)
                ksum = ksum + kb.sum(axis=1)
                return ((kv, ksum), y / (z[..., None] + EPS_LIN))
            kv0 = jnp.zeros((B, H, F, D), dtype=q_phi.dtype)
            ks0 = jnp.zeros((B, H, F), dtype=q_phi.dtype)
            _, ys = jax.lax.scan(step, (kv0, ks0), (qc, kc, vc))
            return ys.transpose(1, 0, 2, 3, 4).reshape(B, T, H, D)

        def sliding_window_attention(q, k, v):
            B, T, H, D = q.shape
            scale = 1.0 / math.sqrt(D)
            t = jnp.arange(T)
            allowed = (t[None, :] <= t[:, None]) & (t[None, :] >= t[:, None] - WINDOW)
            scores = jnp.einsum('bqhd,bkhd->bhqk', q, k) * scale
            scores = jnp.where(allowed[None, None], scores, -jnp.inf)
            attn = jax.nn.softmax(scores, axis=-1)
            out = jnp.einsum('bhqk,bkhd->bqhd', attn, v)
            return out.reshape(B, T, H * D)
        B, T, _ = x.shape
        h = rmsnorm(x, norm_w)
        q = (h @ Wq).reshape(B, T, N_HEADS, HEAD_DIM)
        k = (h @ Wk).reshape(B, T, N_HEADS, HEAD_DIM)
        v = (h @ Wv).reshape(B, T, N_HEADS, HEAD_DIM)
        q_phi = taylor_feature_map(q @ Wqf)
        k_phi = taylor_feature_map(k @ Wkf)
        lin = linear_attention_causal(q_phi, k_phi, v).reshape(B, T, D_MODEL)
        win = sliding_window_attention(q, k, v)
        out = jnp.concatenate([lin, win], axis=-1) @ Wout
        return x + out

    def _L1_xattn_ref(Q, K, V, mask, WQ_w, WQ_b, WK_w, WK_b, WV_w, WV_b, WO_w, WO_b):
        import jax, jax.numpy as jnp
        import numpy as np
        D_MODEL = 256
        H = 16
        D_K = D_MODEL // H
        B = 2
        S = 512

        def _split_heads(x):
            b, s, _ = x.shape
            return x.reshape(b, s, H, D_K).transpose(0, 2, 1, 3)
        q = _split_heads(Q @ WQ_w.T + WQ_b)
        k = _split_heads(K @ WK_w.T + WK_b)
        v = _split_heads(V @ WV_w.T + WV_b)
        scores = jnp.einsum('bhqd,bhkd->bhqk', q, k) / jnp.sqrt(jnp.float32(D_K))
        scores = jnp.where(mask == 0, jnp.float32(1e-09), scores)
        attn = jax.nn.softmax(scores, axis=-1)
        out = jnp.einsum('bhqk,bhkd->bhqd', attn, v)
        out = out.transpose(0, 2, 1, 3).reshape(Q.shape[0], -1, D_MODEL)
        return out @ WO_w.T + WO_b

    def _L1_ffn_ref(x, Wg, W1, b1, W2, b2):
        import jax, jax.numpy as jnp
        import numpy as np
        B, S, D, F, E, K = (2, 512, 256, 1024, 8, 2)
        b, s, d = x.shape
        e = Wg.shape[1]
        T = b * s
        C = 2 * K * T // e
        xt = x.reshape(T, d)
        logits = xt.astype(jnp.float32) @ Wg.astype(jnp.float32)
        gates = jax.nn.softmax(logits, axis=-1)
        idx1 = jnp.argmax(gates, axis=-1)
        mask1 = jax.nn.one_hot(idx1, e, dtype=gates.dtype)
        gate1 = jnp.sum(gates * mask1, axis=-1)
        logits2 = jnp.where(mask1 > 0, -jnp.inf, logits)
        idx2 = jnp.argmax(logits2, axis=-1)
        mask2 = jax.nn.one_hot(idx2, e, dtype=gates.dtype)
        gate2 = jnp.sum(gates * mask2, axis=-1)
        denom = gate1 + gate2 + 1e-09
        w1 = gate1 / denom
        w2 = gate2 / denom
        p1 = jnp.cumsum(mask1, axis=0) - mask1
        pos1 = jnp.sum(p1 * mask1, axis=-1).astype(jnp.int32)
        off = jnp.sum(mask1, axis=0)
        p2 = jnp.cumsum(mask2, axis=0) - mask2 + off[None, :]
        pos2 = jnp.sum(p2 * mask2, axis=-1).astype(jnp.int32)
        keep1 = (pos1 < C).astype(xt.dtype)
        keep2 = (pos2 < C).astype(xt.dtype)
        pos1 = jnp.clip(pos1, 0, C - 1)
        pos2 = jnp.clip(pos2, 0, C - 1)
        xe = jnp.zeros((e, C, d), dtype=xt.dtype)
        xe = xe.at[idx1, pos1].add(xt * keep1[:, None])
        xe = xe.at[idx2, pos2].add(xt * keep2[:, None])
        h = jax.nn.gelu(jnp.einsum('ecd,edf->ecf', xe, W1) + b1[:, None, :], approximate=False)
        ye = jnp.einsum('ecf,efd->ecd', h, W2) + b2[:, None, :]
        out = ye[idx1, pos1] * (w1 * keep1)[:, None] + ye[idx2, pos2] * (w2 * keep2)[:, None]
        return out.reshape(b, s, d)

    def _L2_attn_ref(x, W_in, W_out):
        import jax, jax.numpy as jnp
        import numpy as np
        D_MODEL = 256
        N_HEADS = 16
        ORDER = 6
        P2 = 2 * ORDER - 1
        EPS_CLAMP = 1e-06
        EPS_DEN = 1e-07

        def _beta_np():
            j = np.arange(ORDER, dtype=np.float32)
            alpha = (j + 1.0) ** (-1.5)
            tail = np.flip(np.cumsum(np.flip(alpha)))
            beta = np.concatenate([np.zeros(1, np.float32), tail[1:].astype(np.float32), np.zeros(ORDER - 1, np.float32)])
            return beta / beta.sum()

        def _cheb(x):
            T = [jnp.ones_like(x), x]
            for _ in range(2, P2):
                T.append(2.0 * x * T[-1] - T[-2])
            return jnp.stack(T, axis=3)
        B, S, D = x.shape
        H, Dh = (N_HEADS, D // N_HEADS)
        qkv = jnp.einsum('bsd,ed->bse', x, W_in)
        q, k, v = jnp.split(qkv, 3, axis=-1)
        q = q.reshape(B, S, H, Dh).transpose(0, 2, 1, 3)
        k = k.reshape(B, S, H, Dh).transpose(0, 2, 1, 3)
        v = v.reshape(B, S, H, Dh).transpose(0, 2, 1, 3)
        inv_sqrt_d = 1.0 / jnp.sqrt(jnp.float32(Dh))
        xq = jnp.clip(q * inv_sqrt_d, -1.0 + EPS_CLAMP, 1.0 - EPS_CLAMP)
        xk = jnp.clip(k * inv_sqrt_d, -1.0 + EPS_CLAMP, 1.0 - EPS_CLAMP)
        Tq = _cheb(xq)
        Tk = _cheb(xk)
        beta = jnp.asarray(_beta_np())
        Tv = Tk * v[:, :, :, None, :]
        kv_prefix = jnp.cumsum(Tv, axis=2)
        ks_prefix = jnp.cumsum(Tk.sum(axis=-1), axis=2)
        kv_beta = kv_prefix * beta[None, None, None, :, None]
        k_beta = ks_prefix * beta[None, None, None, :]
        num = (Tq * kv_beta).sum(axis=3)
        den = (Tq.sum(axis=-1) * k_beta).sum(axis=3)
        out_h = num / (den[..., None] + EPS_DEN)
        out = out_h.transpose(0, 2, 1, 3).reshape(B, S, H * Dh)
        return jnp.einsum('bsd,ed->bse', out, W_out)

    def _L2_xattn_ref(query_states, key_states, value_states, Wq, Wk, Wv, Wo):
        import jax, jax.numpy as jnp
        import numpy as np
        HIDDEN = 256
        N_HEADS = 16
        HEAD_DIM = HIDDEN // N_HEADS
        SCALE = HEAD_DIM ** (-0.5)
        B, QL, KVL = (2, 512, 1024)
        b, ql, _ = query_states.shape
        kvl = key_states.shape[1]
        q = query_states @ Wq.T
        k = key_states @ Wk.T
        v = value_states @ Wv.T
        q = q.reshape(b, ql, N_HEADS, HEAD_DIM).transpose(0, 2, 1, 3)
        k = k.reshape(b, kvl, N_HEADS, HEAD_DIM).transpose(0, 2, 1, 3)
        v = v.reshape(b, kvl, N_HEADS, HEAD_DIM).transpose(0, 2, 1, 3)
        scores = jnp.einsum('bhqd,bhkd->bhqk', q, k) * SCALE
        attn = jax.nn.softmax(scores, axis=-1)
        out = jnp.einsum('bhqk,bhkd->bhqd', attn, v)
        out = out.transpose(0, 2, 1, 3).reshape(b, ql, HIDDEN)
        return out @ Wo.T

    def _L2_ffn_ref(x, wg1, bg1, wg2, bg2, We, be):
        import jax, jax.numpy as jnp
        import numpy as np
        B, S, D, DO = (4, 512, 256, 256)
        E, K = (20, 2)
        Bv, Sv, Dv = x.shape
        xf = x.reshape(-1, Dv)
        h = jax.nn.gelu(xf @ wg1 + bg1, approximate=False)
        logits = (xf @ 0.0 + (h @ wg2 + bg2))[:, :E] if False else (h @ wg2 + bg2)[:, :E]
        probs = jax.nn.softmax(logits, axis=-1)
        top_vals, top_idx = jax.lax.top_k(probs, K)
        N = xf.shape[0]
        gates = jnp.zeros((N, E), xf.dtype).at[jnp.arange(N)[:, None], top_idx].set(top_vals)

        def body(y, eb):
            We_e, be_e, g_e = eb
            return (y + g_e[:, None] * (xf @ We_e + be_e), None)
        y0 = jnp.zeros((N, be.shape[-1]), xf.dtype)
        y, _ = jax.lax.scan(body, y0, (We, be, gates.T))
        return y.reshape(Bv, Sv, -1)

    def _L3_attn_ref(x, Wq, bq, Wk, bk, Wv, bv, Wo, bo):
        import math
        import jax, jax.numpy as jnp
        import numpy as np
        D_MODEL = 256
        N_HEADS = 16
        D_HEAD = D_MODEL // N_HEADS

        def get_alibi_slopes(n_heads: int) -> np.ndarray:

            def pow2_slopes(n):
                start = 2 ** (-2 ** (-(math.log2(n) - 3)))
                return np.array([start * start ** i for i in range(n)], dtype=np.float32)
            if math.log2(n_heads).is_integer():
                return pow2_slopes(n_heads)
            closest = 2 ** math.floor(math.log2(n_heads))
            slopes = pow2_slopes(closest)
            extra = pow2_slopes(2 * closest)[0::2][:n_heads - closest]
            return np.concatenate([slopes, extra], axis=0)
        B, S, D = x.shape
        H, Dh = (N_HEADS, D_HEAD)
        q = (x @ Wq.T + bq).reshape(B, S, H, Dh).transpose(0, 2, 1, 3)
        k = (x @ Wk.T + bk).reshape(B, S, H, Dh).transpose(0, 2, 1, 3)
        v = (x @ Wv.T + bv).reshape(B, S, H, Dh).transpose(0, 2, 1, 3)
        scores = jnp.einsum('bhqd,bhkd->bhqk', q, k) / math.sqrt(Dh)
        slopes = jnp.asarray(get_alibi_slopes(H), dtype=scores.dtype)
        pos = jnp.arange(S, dtype=scores.dtype)
        pos_diff = pos[None, :] - pos[:, None]
        alibi = slopes[:, None, None] * pos_diff[None, :, :]
        scores = scores + alibi[None]
        causal = jnp.tril(jnp.ones((S, S), dtype=bool))
        scores = jnp.where(causal[None, None], scores, -jnp.inf)
        weights = jax.nn.softmax(scores, axis=-1)
        y = jnp.einsum('bhqk,bhkd->bhqd', weights, v)
        y = y.transpose(0, 2, 1, 3).reshape(B, S, D)
        return y @ Wo.T + bo

    def _L3_xattn_ref(query_tokens, key_or_value_tokens, mask, Wq, bq, Wk, bk, Wv, bv, Wo, bo):
        import jax, jax.numpy as jnp
        import numpy as np
        N_HEADS = 16
        D_MODEL = 256
        HEAD_DIM = D_MODEL // N_HEADS
        B, S = (2, 512)
        b, s, d = query_tokens.shape
        h, dh = (N_HEADS, HEAD_DIM)

        def proj(x, W, bias):
            y = jnp.einsum('bsd,ed->bse', x, W) + bias
            return y.reshape(b, -1, h, dh).transpose(0, 2, 1, 3)
        q = proj(query_tokens, Wq, bq)
        k = proj(key_or_value_tokens, Wk, bk)
        v = proj(key_or_value_tokens, Wv, bv)
        scores = jnp.einsum('bhqd,bhkd->bhqk', q, k) / jnp.sqrt(jnp.float32(dh))
        scores = jnp.where(mask[:, None, :, :] == 0, jnp.float32(-1000000000.0), scores)
        attn = jax.nn.softmax(scores, axis=-1)
        out = jnp.einsum('bhqk,bhkd->bhqd', attn, v)
        out = out.transpose(0, 2, 1, 3).reshape(b, s, d)
        return jnp.einsum('bsd,ed->bse', out, Wo) + bo

    def _L3_ffn_ref(x, wqkv, q_scale, k_scale, wo, ln_g, ln_b, w1, b1, w2, b2):
        import jax, jax.numpy as jnp
        import numpy as np
        DIM = 256
        DEPTH = 2
        HEADS = 8
        DIM_HEAD = 64
        WINDOW = 128
        INNER = HEADS * DIM_HEAD
        HID = int(DIM * 4 * 2 / 3)
        B, N = (2, 2048)
        QK_SCALE = 8.0

        def shift_token(t):
            t1, t2 = jnp.split(t, 2, axis=-1)
            t2 = jnp.pad(t2, ((0, 0), (1, 0), (0, 0)))[:, :-1]
            return jnp.concatenate([t1, t2], axis=-1)

        def l2norm(t):
            return t / jnp.clip(jnp.linalg.norm(t, axis=-1, keepdims=True), 1e-12)

        def rotate_half(x):
            x1, x2 = jnp.split(x, 2, axis=-1)
            return jnp.concatenate([-x2, x1], axis=-1)

        def rotary_xpos(q, k):
            n = q.shape[-2]
            half_idx = jnp.arange(0, DIM_HEAD, 2, dtype=jnp.float32)
            inv_freq = 1.0 / 10000.0 ** (half_idx / DIM_HEAD)
            t = jnp.arange(n, dtype=jnp.float32)
            freqs = t[:, None] * inv_freq[None, :]
            freqs = jnp.concatenate([freqs, freqs], axis=-1)
            base = (half_idx + 0.4 * DIM_HEAD) / (1.4 * DIM_HEAD)
            power = (t - n // 2) / float(WINDOW // 2)
            scale = base[None, :] ** power[:, None]
            scale = jnp.concatenate([scale, scale], axis=-1)
            cos, sin = (jnp.cos(freqs), jnp.sin(freqs))
            q = q * cos * scale + rotate_half(q) * sin * scale
            k = k * cos / scale + rotate_half(k) * sin / scale
            return (q, k)

        def local_attention(q, k, v):
            b, h, n, d = q.shape
            w = n // WINDOW
            bq = q.reshape(b, h, w, WINDOW, d) * QK_SCALE
            bk = k.reshape(b, h, w, WINDOW, d)
            bv = v.reshape(b, h, w, WINDOW, d)

            def look_around(t):
                p = jnp.pad(t, ((0, 0), (0, 0), (1, 0), (0, 0), (0, 0)))
                return jnp.concatenate([p[:, :, :w], p[:, :, 1:]], axis=3)
            bk, bv = (look_around(bk), look_around(bv))
            bt = jnp.arange(n).reshape(w, WINDOW)
            btp = jnp.pad(bt, ((1, 0), (0, 0)), constant_values=-1)
            btk = jnp.concatenate([btp[:w], btp[1:]], axis=1)
            sim = jnp.einsum('bhwid,bhwjd->bhwij', bq, bk)
            i = bt[:, :, None]
            j = btk[:, None, :]
            mask = (i < j) | (i > j + WINDOW) | (j == -1)
            sim = jnp.where(mask, -jnp.finfo(sim.dtype).max, sim)
            attn = jax.nn.softmax(sim, axis=-1)
            out = jnp.einsum('bhwij,bhwjd->bhwid', attn, bv)
            return out.reshape(b, h, n, d)

        def _layer(x, wqkv, qs, ksc, wo, lg, lb, w1, b1, w2, b2):
            b, n, _ = x.shape
            h = shift_token(x)
            qkv = h @ wqkv
            q, k, v = jnp.split(qkv, 3, axis=-1)
            to_heads = lambda t: t.reshape(b, n, HEADS, DIM_HEAD).transpose(0, 2, 1, 3)
            q, k, v = (to_heads(q), to_heads(k), to_heads(v))
            q = l2norm(q) * qs
            k = l2norm(k) * ksc
            q, k = rotary_xpos(q, k)
            o = local_attention(q, k, v)
            o = o.transpose(0, 2, 1, 3).reshape(b, n, INNER)
            x = x + o @ wo
            h = shift_token(x)
            mu = h.mean(-1, keepdims=True)
            var = h.var(-1, keepdims=True)
            h = (h - mu) / jnp.sqrt(var + 1e-05) * lg + lb
            h = h @ w1 + b1
            a, g = jnp.split(h, 2, axis=-1)
            h = a * jax.nn.gelu(g, approximate=False)
            x = x + h @ w2 + b2
            return x
        for l in range(DEPTH):
            x = _layer(x, wqkv[l], q_scale[l], k_scale[l], wo[l], ln_g[l], ln_b[l], w1[l], b1[l], w2[l], b2[l])
        return x
    x = x + _L0_attn_ref(_layernorm(x, axis=-1), L0_attn_W_qkv, L0_attn_W_out)
    x = x + _L0_xattn_ref(_layernorm(x, axis=-1), ctx_1024, L0_xattn_Wq, L0_xattn_Wkv, L0_xattn_Wout, L0_xattn_bout)
    x = x + _L0_ffn_ref(_layernorm(x, axis=-1), L0_ffn_Wg, L0_ffn_bg, L0_ffn_W1, L0_ffn_b1, L0_ffn_W2, L0_ffn_b2)
    x = x + _L1_attn_ref(_layernorm(x, axis=-1), L1_attn_norm_w, L1_attn_Wq, L1_attn_Wk, L1_attn_Wv, L1_attn_Wqf, L1_attn_Wkf, L1_attn_Wout)
    x = x + _L1_xattn_ref(_layernorm(x, axis=-1), ctx_1024, ctx_1024, mask_Bx1xSxS2_ik1, L1_xattn_WQ_w, L1_xattn_WQ_b, L1_xattn_WK_w, L1_xattn_WK_b, L1_xattn_WV_w, L1_xattn_WV_b, L1_xattn_WO_w, L1_xattn_WO_b)
    x = x + _L1_ffn_ref(_layernorm(x, axis=-1), L1_ffn_Wg, L1_ffn_W1, L1_ffn_b1, L1_ffn_W2, L1_ffn_b2)
    x = x + _L2_attn_ref(_layernorm(x, axis=-1), L2_attn_W_in, L2_attn_W_out)
    x = x + _L2_xattn_ref(_layernorm(x, axis=-1), ctx_1024, ctx_1024, L2_xattn_Wq, L2_xattn_Wk, L2_xattn_Wv, L2_xattn_Wo)
    x = x + _L2_ffn_ref(_layernorm(x, axis=-1), L2_ffn_wg1, L2_ffn_bg1, L2_ffn_wg2, L2_ffn_bg2, L2_ffn_We, L2_ffn_be)
    x = x + _L3_attn_ref(_layernorm(x, axis=-1), L3_attn_Wq, L3_attn_bq, L3_attn_Wk, L3_attn_bk, L3_attn_Wv, L3_attn_bv, L3_attn_Wo, L3_attn_bo)
    x = x + _L3_xattn_ref(_layernorm(x, axis=-1), ctx_1024, mask_BxSxS2_if1, L3_xattn_Wq, L3_xattn_bq, L3_xattn_Wk, L3_xattn_bk, L3_xattn_Wv, L3_xattn_bv, L3_xattn_Wo, L3_xattn_bo)
    x = x + _L3_ffn_ref(_layernorm(x, axis=-1), L3_ffn_wqkv, L3_ffn_q_scale, L3_ffn_k_scale, L3_ffn_wo, L3_ffn_ln_g, L3_ffn_ln_b, L3_ffn_w1, L3_ffn_b1, L3_ffn_w2, L3_ffn_b2)
    return x

_drawn_inputs = setup_inputs


def setup_inputs(seed=0):
    import zlib

    import numpy as np

    out = dict(_drawn_inputs(seed))
    spreads = {'L1_attn_norm_w': (1.0, 0.6),
     'L1_ffn_b1': (0.0, 0.577),
     'L1_ffn_b2': (0.0, 0.1),
     'L2_ffn_bg1': (0.0, 0.327),
     'L2_ffn_bg2': (0.0, 0.278),
     'L2_ffn_be': (0.0, 0.8),
     'L3_attn_bq': (0.0, 0.8),
     'L3_attn_bk': (0.0, 2.0),
     'L3_attn_bv': (0.0, 0.1),
     'L3_attn_bo': (0.0, 0.1),
     'L3_xattn_bq': (0.0, 0.8),
     'L3_xattn_bk': (0.0, 2.0),
     'L3_xattn_bv': (0.0, 0.1),
     'L3_xattn_bo': (0.0, 0.1),
     'L3_ffn_q_scale': (1.0, 0.6),
     'L3_ffn_k_scale': (1.0, 0.6),
     'L3_ffn_ln_g': (1.0, 0.6),
     'L3_ffn_ln_b': (0.0, 0.8),
     'L3_ffn_b1': (0.0, 0.8),
     'L3_ffn_b2': (0.0, 0.524)}
    factors = {'L0_xattn_bout': 4.055,
     'L0_ffn_b1': 5.728,
     'L0_ffn_b2': 4.244,
     'L1_attn_Wq': 8.0,
     'L1_attn_Wk': 8.0,
     'L1_attn_Wqf': 8.0,
     'L1_attn_Wkf': 8.0,
     'L1_xattn_WQ_b': 6.498,
     'L1_xattn_WK_b': 8.0,
     'L2_attn_W_in': 8.0,
     'L2_attn_W_out': 8.0,
     'L2_xattn_Wq': 8.0,
     'L2_xattn_Wk': 8.0,
     'L3_ffn_w1': 3.991,
     'L3_ffn_w2': 3.977}
    for name, (base, spread) in spreads.items():
        noise = np.random.default_rng([zlib.crc32(name.encode()), seed]).standard_normal(out[name].shape)
        drawn = base * np.exp(spread * noise) if base else spread * noise
        out[name] = jnp.asarray(drawn.astype(out[name].dtype))
    for name, factor in factors.items():
        out[name] = (out[name] * factor).astype(out[name].dtype)
    return out
```

```python
from contextlib import ExitStack
import math

import numpy as np

import concourse.bass as bass
from concourse import mybir

F32 = mybir.dt.float32
I32 = mybir.dt.int32
ALU = mybir.AluOpType
ACT = mybir.ActivationFunctionType
AX = mybir.AxisListType

B, S, D = 16, 128, 256
P = 128
KD = D // P
LN_EPS = 1e-5
NEG = -1e30

L3_HID = -(-int(D * 4 * 2 / 3) // P) * P
START = 8

SUBLAYERS = range(12)


class Signal:

    def __init__(self, sem):
        self.sem, self.base = sem, START

    def at(self, n):
        return self.base + n

    def passed(self, n):
        self.base += n


class Chain:

    def __init__(self, eng, counted, start):
        self.eng, self.counted, self.start, self.n = eng, counted, start, 0

    def __call__(self, ins):
        self.n += 1
        ins.then_inc(self.counted.sem, 1)
        self.eng.wait_ge(self.counted.sem, self.counted.at(self.start + self.n))


class Core:

    def __init__(self, nc, ctx):
        self.nc, self.ctx = nc, ctx
        self.sig = {}
        self.loaded = self.count("loaded")
        self.stored = self.count("stored")
        self.xn_ready = self.count("xn_ready")
        self.xt_ps = self.count("xt_ps")
        self.xT_ready = self.count("xT_ready")
        self.ctx_ready = self.count("ctx_ready")
        self.k_ps = self.count("k_ps")
        self.q_ready = self.count("q_ready")
        self.k_ready = self.count("k_ready")
        self.v_ps = self.count("v_ps")
        self.v_ready = self.count("v_ready")
        self.km_ready = self.count("km_ready")
        self.s_ps = self.count("s_ps")
        self.e_ready = self.count("e_ready")
        self.p_ready = self.count("p_ready")
        self.pt_ps = self.count("pt_ps")
        self.pT_ready = self.count("pT_ready")
        self.pv_done = self.count("pv_done")
        self.o_ready = self.count("o_ready")
        self.ot_ps = self.count("ot_ps")
        self.oT_ready = self.count("oT_ready")
        self.y_ps = self.count("y_ps")
        self.x_added = self.count("x_added")
        self.chain_v = self.count("chain_v")
        self.chain_p = self.count("chain_p")
        self.stats_ready = self.count("stats_ready")
        self.std_ready = self.count("std_ready")
        self.h_ps = self.count("h_ps")
        self.h_ready = self.count("h_ready")
        self.l_ps = self.count("l_ps")
        self.l_ready = self.count("l_ready")
        self.c_ps = self.count("c_ps")
        self.c_ready = self.count("c_ready")
        self.shifted = self.count("shifted")
        self.comb_ready = self.count("comb_ready")
        self.cT_ps = self.count("cT_ps")
        self.cT_ready = self.count("cT_ready")
        self.a_ready = self.count("a_ready")
        self.xs_ready = self.count("xs_ready")
        self.w_loaded = [self.count(f"w_loaded{i}") for i in range(2)]
        sb = self.sb
        self.x = sb(ctx, "x_res", [P, B, D])
        self.ctxT = sb(ctx, "ctxT", [P, KD, B * S])
        self.ident = sb(ctx, "ident", [P, P])
        self.causal_add = sb(ctx, "causal_add", [P, P])
        self.stats = sb(ctx, "stats", [P, B, 2, 6])
        self.mv = sb(ctx, "mv", [P, B, 2])
        self.std = sb(ctx, "std", [P, B])
        self.rstd = sb(ctx, "rstd", [P, B])
        self.bank = [ctx.enter_context(nc.psum_tensor(f"bank{i}", [P, 512], F32)) for i in range(8)]

    def count(self, name):
        self.sig[name] = Signal(self.ctx.enter_context(self.nc.semaphore("s_" + name)))
        return self.sig[name]

    def sb(self, ctx, name, shape, dt=F32):
        return ctx.enter_context(self.nc.sbuf_tensor(name, shape, dt))

    def passed(self, **counts):
        for name, n in counts.items():
            self.sig[name].passed(n)


def m_parity(g, quads, t):
    return (g * quads + t) % 2


def token_tile(t, b):
    return t[:, :, bass.ds(b * S, S)]


def heads_of(ap, h):
    return ap.rearrange("p (h d) -> p h d", h=h)


def load(c, pairs):
    with c.nc.Block() as block:
        @block.sync
        def _(sp):
            for dst, src in pairs:
                sp.dma_start(dst, src).then_inc(c.loaded.sem, 16)
            sp.wait_ge(c.loaded.sem, c.loaded.at(16 * len(pairs)))
    c.passed(loaded=16 * len(pairs))


def layernorm_stats(c, halves, eps=LN_EPS, rms_eps=None):
    nc, n = c.nc, len(halves)
    with nc.Block() as block:
        @block.vector
        def _(dve):
            with dve.Fori(0, B) as b:
                for k, half in enumerate(halves):
                    last = nc.vector.bn_stats(c.stats[:, b, k, :], half[:, b, :])
                last.then_inc(c.stats_ready.sem, 1)
            dve.wait_ge(c.stats_ready.sem, c.stats_ready.at(B))
            chain = Chain(dve, c.chain_v, 0)
            for b in range(B):
                last = nc.vector.bn_aggr(c.mv[:, b, :], c.stats[:, b, 0:n, :])
            chain(last)
            chain(nc.vector.tensor_scalar(c.std[:, :], c.mv[:, :, 1], eps, None, ALU.add))
            if rms_eps is not None:
                chain(nc.vector.scalar_tensor_tensor(out=c.std[:, :], in0=c.std[:, :], scalar=rms_eps,
                                                     in1=c.mv[:, :, 1], op0=ALU.mult, op1=ALU.add))
            nc.vector.tensor_copy(c.rstd[:, :], c.std[:, :]).then_inc(c.stats_ready.sem, 1)
            dve.wait_ge(c.std_ready.sem, c.std_ready.at(1))
            chain(nc.vector.reciprocal(c.rstd[:, :], c.std[:, :]))

        @block.scalar
        def _(act):
            act.wait_ge(c.stats_ready.sem, c.stats_ready.at(B + 1))
            nc.scalar.activation(c.std[:, :], c.rstd[:, :], ACT.Sqrt).then_inc(c.std_ready.sem, 1)
    c.passed(stats_ready=B + 1, std_ready=1, chain_v=3 + (rms_eps is not None))


def attention(c, name, groups, quads, dh, weights, *, ctx_kv=False, norm_w=None, q_scale, q_bias=None,
              k_bias=None, v_bias=None, y_bias=None, lin_group=None, mask_of=None,
              xin=None, rotary=None, into=None):
    nc = c.nc
    H = 4 * quads
    T = groups * quads
    per_block = P // dh
    wq, wk, wv, wo = weights
    into = c.x if into is None else into
    bank_m, bank_v, bank_o, bank_y = c.bank[0], c.bank[1], c.bank[6], c.bank[7]
    bank_s, bank_t = c.bank[2:4], c.bank[4:6]
    with ExitStack() as ctx:
        sb = lambda n, shape: c.sb(ctx, f"{name}_{n}", shape)
        xn, xT, q, k = sb("xn", [P, D]), sb("xT", [P, KD, S]), sb("q", [P, KD, S]), sb("k", [P, KD, S])
        kv_src = sb("ctx", [P, KD, S]) if ctx_kv else xT
        km = sb("km", [P, quads, 4, S])
        v = sb("v", [P, H, dh + 1])
        E = [sb(f"E{i}", [P, 4, S]) for i in range(2)]
        Pr = [sb(f"P{i}", [P, 4, S]) for i in range(2)]
        PT = [sb(f"PT{i}", [P, 4, S]) for i in range(2)]
        mx = [sb(f"mx{i}", [P, 4]) for i in range(2)]
        rden = sb("rden", [P, H])
        o, oT = sb("o", [P, D]), sb("oT", [P, KD, S])
        yb = sb("yb", [P, D])
        hm = c.hm16 if dh == 16 else c.hm64

        vector_steps = (y_bias is not None) + (xin is not None) + 4 * (rotary is not None)
        qk = [[sb(f"rot{a}{n}", [P, H * groups, dh]) for n in range(2)] for a in range(2)] if rotary else None

        def rotate(eng, chain, a, i):
            n = H * groups
            t, r = qk[a]
            per_token = lambda m: m.unsqueeze(1).to_broadcast([P, n, m.shape[1]])
            src = heads_of(rotary.QK[:, i, a * n * dh:(a + 1) * n * dh], n)
            eng.wait_ge(c.v_ps.sem, c.v_ps.at(i * groups))
            chain(eng.tensor_tensor(t[:, :, :], src, rotary.rnorm[:, i, a * n:(a + 1) * n].unsqueeze(2)
                                    .to_broadcast([P, n, dh]), ALU.mult))
            chain(eng.tensor_tensor(t[:, :, :], t[:, :, :], per_token(rotary.scale[:, a, :]), ALU.mult))
            half = dh // 2
            eng.tensor_tensor(r[:, :, 0:half], t[:, :, half:], per_token(rotary.sin[:, a, 0:half]), ALU.mult)
            chain(eng.tensor_tensor(r[:, :, half:], t[:, :, 0:half], per_token(rotary.sin[:, a, half:]), ALU.mult))
            chain(eng.tensor_tensor(t[:, :, :], t[:, :, :], per_token(rotary.cos[:, a, :]), ALU.mult))
            eng.tensor_tensor(r[:, :, :], r[:, :, :], t[:, :, :], ALU.add).then_inc(c.xn_ready.sem, 1)

        for g in range(groups):
            masks = sum(a is not None for a in mask_of(g, 0, 0))
            vector_steps += quads * (masks - 1) + 2 if g == lin_group else quads * (masks + 1) + 1

        with nc.Block() as block:
            @block.vector
            def _(dve):
                nc.vector.memset(v[:, :, :], 1.0).then_inc(c.chain_v.sem, 1)
                dve.wait_ge(c.chain_v.sem, c.chain_v.at(1))

                def prepare(i):
                    dve.wait_ge(c.xt_ps.sem, c.xt_ps.at(i))
                    nc.vector.tensor_scalar(xn[:, :], c.x[:, i, :], c.mv[:, i, 0:1], c.rstd[:, bass.ds(i, 1)],
                                            ALU.subtract, ALU.mult).then_inc(c.xn_ready.sem, 1)

                with dve.Fori(0, B) as i:
                    chain = Chain(dve, c.chain_v, 1 + i * vector_steps)
                    if rotary:
                        rotate(nc.vector, chain, 1, i)
                    else:
                        prepare(i)
                    for g in range(groups):
                        n = i * groups + g
                        dve.wait_ge(c.v_ps.sem, c.v_ps.at(n + 1))
                        dve.wait_ge(c.s_ps.sem, c.s_ps.at(n * quads))
                        for j in range(KD):
                            src = bank_v[:, D + j * S:D + (j + 1) * S]
                            if q_bias is not None:
                                last = nc.vector.tensor_scalar(q[:, j, :], src, q_bias[:, j:j + 1], q_scale[g],
                                                               ALU.add, ALU.mult)
                            else:
                                last = nc.vector.tensor_scalar(q[:, j, :], src, q_scale[g], None, ALU.mult)
                        last.then_inc(c.q_ready.sem, 1)
                        vd = v[:, :, 0:dh]
                        vs = heads_of(bank_v[:, 0:D], H)
                        if not rotary:
                            dve.wait_ge(c.pv_done.sem, c.pv_done.at(n * quads))
                        if rotary:
                            pass
                        elif v_bias is not None:
                            nc.vector.tensor_tensor(vd, vs, heads_of(v_bias[:, :], H), ALU.add)\
                                .then_inc(c.v_ready.sem, 1)
                        else:
                            nc.vector.tensor_copy(vd, vs).then_inc(c.v_ready.sem, 1)
                        for t in range(quads):
                            m = n * quads + t
                            lin = g == lin_group
                            e = E[m_parity(g, quads, t)]
                            s = bank_s[m_parity(g, quads, t)][:, :].rearrange("p (h k) -> p h k", h=4)
                            dve.wait_ge(c.s_ps.sem, c.s_ps.at(m + 1))
                            dve.wait_ge(c.p_ready.sem, c.p_ready.at(m - 1))
                            mul, plus = mask_of(g, t, i)
                            src = s
                            if mul is not None:
                                chain(nc.vector.tensor_tensor(e[:, :, :], src, mul, ALU.mult))
                                src = e[:, :, :]
                            if plus is not None:
                                ins = nc.vector.tensor_tensor(e[:, :, :], src, plus, ALU.add)
                                if lin:
                                    ins.then_inc(c.e_ready.sem, 1)
                                    continue
                                chain(ins)
                                src = e[:, :, :]
                            most = mx[m_parity(g, quads, t)]
                            chain(nc.vector.tensor_reduce(most[:, :], src, AX.X, ALU.max))
                            nc.vector.tensor_tensor(e[:, :, :], src, most[:, :].unsqueeze(2).to_broadcast([P, 4, S]),
                                                    ALU.subtract).then_inc(c.e_ready.sem, 1)
                        dve.wait_ge(c.pv_done.sem, c.pv_done.at((n + 1) * quads))
                        po = bank_o[:, 0:H * (dh + 1)].rearrange("p (h d) -> p h d", h=H)
                        if g == lin_group:
                            chain(nc.vector.tensor_scalar(rden[:, :], po[:, :, dh], 1e-6, None, ALU.add))
                            chain(nc.vector.reciprocal(rden[:, :], rden[:, :]))
                        else:
                            chain(nc.vector.reciprocal(rden[:, :], po[:, :, dh]))
                        dve.wait_ge(c.ot_ps.sem, c.ot_ps.at(n))
                        nc.vector.tensor_tensor(heads_of(o[:, :], H), po[:, :, 0:dh],
                                                rden[:, :].unsqueeze(2).to_broadcast([P, H, dh]), ALU.mult)\
                            .then_inc(c.o_ready.sem, 1)
                    dve.wait_ge(c.y_ps.sem, c.y_ps.at((i + 1) * groups))
                    y = bank_y[:, 0:D]
                    if y_bias is not None:
                        chain(nc.vector.tensor_tensor(yb[:, :], y, y_bias[:, :], ALU.add))
                        y = yb[:, :]
                    if xin is not None:
                        chain(nc.vector.tensor_tensor(yb[:, :], y, xin[:, i, :], ALU.add))
                        y = yb[:, :]
                    nc.vector.tensor_tensor(into[:, i, :], into[:, i, :], y, ALU.add).then_inc(c.x_added.sem, 1)
                    assert chain.n == vector_steps, chain.n

            @block.gpsimd
            def _(pool):
                with pool.Fori(0, B) as i:
                    if rotary:
                        rotate(nc.gpsimd, Chain(pool, c.chain_p, i * 4), 0, i)
                    if ctx_kv:
                        pool.wait_ge(c.v_ps.sem, c.v_ps.at(i * groups))
                        nc.gpsimd.tensor_copy(kv_src[:, :, :], token_tile(c.ctxT, i)).then_inc(c.ctx_ready.sem, 1)
                    for g in range(groups):
                        n = i * groups + g
                        pool.wait_ge(c.k_ready.sem, c.k_ready.at(n + 1))
                        for t in range(quads):
                            pool.wait_ge(c.s_ps.sem, c.s_ps.at((n - 1) * quads + t + 1))
                            if dh == 16:
                                j, h0 = t // 2, 4 * (t % 2)
                                nc.gpsimd.tensor_tensor(
                                    km[:, t, :, :], k[:, j, :].unsqueeze(1).to_broadcast([P, 4, S]),
                                    hm[:, h0:h0 + 4].unsqueeze(2).to_broadcast([P, 4, S]), ALU.mult)\
                                    .then_inc(c.km_ready.sem, 1)
                            else:
                                for j in range(KD):
                                    last = nc.gpsimd.tensor_tensor(
                                        km[:, t, 2 * j:2 * j + 2, :], k[:, j, :].unsqueeze(1).to_broadcast([P, 2, S]),
                                        hm[:, 0:2].unsqueeze(2).to_broadcast([P, 2, S]), ALU.mult)
                                last.then_inc(c.km_ready.sem, 1)

            @block.scalar
            def _(act):
                with act.Fori(0, B) as i:
                    if not rotary:
                        act.wait_ge(c.xt_ps.sem, c.xt_ps.at(i + 1))
                        act.wait_ge(c.v_ps.sem, c.v_ps.at(i * groups))
                        for j in range(KD):
                            src = bank_m[:, j * S:(j + 1) * S]
                            if norm_w is not None:
                                last = nc.scalar.activation(xT[:, j, :], src, ACT.Identity, scale=norm_w[:, j:j + 1])
                            else:
                                last = nc.scalar.copy(xT[:, j, :], src)
                        last.then_inc(c.xT_ready.sem, 1)
                    for g in range(groups):
                        n = i * groups + g
                        act.wait_ge(c.k_ps.sem, c.k_ps.at(n + 1))
                        act.wait_ge(c.km_ready.sem, c.km_ready.at(n * quads))
                        for j in range(KD):
                            src = bank_m[:, j * S:(j + 1) * S]
                            if k_bias is not None:
                                last = nc.scalar.activation(k[:, j, :], src, ACT.Identity, bias=k_bias[:, j:j + 1])
                            else:
                                last = nc.scalar.copy(k[:, j, :], src)
                        last.then_inc(c.k_ready.sem, 1)

                        def weights_of(t):
                            m = n * quads + t
                            par = m_parity(g, quads, t)
                            act.wait_ge(c.e_ready.sem, c.e_ready.at(m + 1))
                            act.wait_ge(c.pt_ps.sem, c.pt_ps.at(m - 1))
                            if g == lin_group:
                                nc.scalar.activation(Pr[par][:, :, :], E[par][:, :, :], ACT.Square, bias=c.one[:, :],
                                                     scale=0.5).then_inc(c.p_ready.sem, 1)
                            else:
                                nc.scalar.activation(Pr[par][:, :, :], E[par][:, :, :], ACT.Exp)\
                                    .then_inc(c.p_ready.sem, 1)

                        def transposed(t):
                            m = n * quads + t
                            par = m_parity(g, quads, t)
                            act.wait_ge(c.pt_ps.sem, c.pt_ps.at(m + 1))
                            act.wait_ge(c.pv_done.sem, c.pv_done.at(m - 1))
                            nc.scalar.copy(PT[par][:, :, :],
                                           bank_t[par][:, :].rearrange("p (h q) -> p h q", h=4))\
                                .then_inc(c.pT_ready.sem, 1)

                        weights_of(0)
                        for t in range(1, quads):
                            weights_of(t)
                            transposed(t - 1)
                        transposed(quads - 1)
                        act.wait_ge(c.ot_ps.sem, c.ot_ps.at(n + 1))
                        act.wait_ge(c.y_ps.sem, c.y_ps.at(n))
                        nc.scalar.copy(oT[:, :, :], bank_m[:, 0:D].rearrange("p (j q) -> p j q", j=KD))\
                            .then_inc(c.oT_ready.sem, 1)

            @block.tensor
            def _(pe):
                with pe.Fori(0, B) as i:
                    if rotary:
                        pe.wait_ge(c.xn_ready.sem, c.xn_ready.at(2 * (i + 1)))
                    else:
                        pe.wait_ge(c.xn_ready.sem, c.xn_ready.at(i + 1))
                        pe.wait_ge(c.oT_ready.sem, c.oT_ready.at(i * groups))
                        for j in range(KD):
                            last = nc.tensor.transpose(bank_m[:, j * S:(j + 1) * S], xn[:, j * P:(j + 1) * P],
                                                       c.ident[:, :])
                        last.then_inc(c.xt_ps.sem, 1)
                        pe.wait_ge(c.xT_ready.sem, c.xT_ready.at(i + 1))
                    if ctx_kv:
                        pe.wait_ge(c.ctx_ready.sem, c.ctx_ready.at(i + 1))
                    for g in range(groups):
                        n = i * groups + g
                        pe.wait_ge(c.oT_ready.sem, c.oT_ready.at(n))
                        if rotary:
                            q_rot, k_rot = (qk[a][1][:, :, :].rearrange("p h d -> p (h d)") for a in range(2))
                            for j in range(KD):
                                col = g * D + j * P
                                last = nc.tensor.transpose(bank_m[:, j * S:(j + 1) * S], k_rot[:, col:col + P],
                                                           c.ident[:, :])
                            last.then_inc(c.k_ps.sem, 1)
                            pe.wait_ge(c.q_ready.sem, c.q_ready.at(n))
                            for j in range(KD):
                                col = g * D + j * P
                                last = nc.tensor.transpose(bank_v[:, D + j * S:D + (j + 1) * S],
                                                           q_rot[:, col:col + P], c.ident[:, :])
                            last.then_inc(c.v_ps.sem, 1)
                        else:
                            for j in range(KD):
                                for kd in range(KD):
                                    last = nc.tensor.matmul(bank_m[:, j * S:(j + 1) * S],
                                                            wk[:, kd, g * D + j * P:g * D + (j + 1) * P],
                                                            kv_src[:, kd, :], start=kd == 0, stop=kd == KD - 1)
                            last.then_inc(c.k_ps.sem, 1)
                            pe.wait_ge(c.v_ready.sem, c.v_ready.at(n))
                            for j in range(KD):
                                for kd in range(KD):
                                    nc.tensor.matmul(bank_v[:, D + j * S:D + (j + 1) * S],
                                                     wq[:, kd, g * D + j * P:g * D + (j + 1) * P],
                                                     xT[:, kd, :], start=kd == 0, stop=kd == KD - 1)
                            for kd in range(KD):
                                last = nc.tensor.matmul(bank_v[:, 0:D], kv_src[:, kd, :],
                                                        wv[:, kd, g * D:(g + 1) * D],
                                                        start=kd == 0, stop=kd == KD - 1)
                            last.then_inc(c.v_ps.sem, 1)
                        pe.wait_ge(c.q_ready.sem, c.q_ready.at(n + 1))

                        def scores(t):
                            m = n * quads + t
                            pe.wait_ge(c.km_ready.sem, c.km_ready.at(m + 1))
                            pe.wait_ge(c.e_ready.sem, c.e_ready.at(m - 1))
                            s = bank_s[m_parity(g, quads, t)]
                            if dh == 16:
                                last = nc.tensor.matmul(s[:, :], q[:, t // 2, :],
                                                        km[:, t, :, :].rearrange("p h k -> p (h k)"),
                                                        start=True, stop=True)
                            else:
                                for j in range(KD):
                                    last = nc.tensor.matmul(s[:, j * D:(j + 1) * D], q[:, j, :],
                                                            km[:, t, 2 * j:2 * j + 2, :].rearrange("p h k -> p (h k)"),
                                                            start=True, stop=True)
                            last.then_inc(c.s_ps.sem, 1)

                        def transposes(t):
                            m = n * quads + t
                            par = m_parity(g, quads, t)
                            pe.wait_ge(c.p_ready.sem, c.p_ready.at(m + 1))
                            pe.wait_ge(c.pT_ready.sem, c.pT_ready.at(m - 1))
                            for h in range(4):
                                last = nc.tensor.transpose(bank_t[par][:, h * S:(h + 1) * S], Pr[par][:, h, :],
                                                           c.ident[:, :])
                            last.then_inc(c.pt_ps.sem, 1)

                        def values(t):
                            m = n * quads + t
                            par = m_parity(g, quads, t)
                            if t == 0 and not rotary:
                                pe.wait_ge(c.v_ready.sem, c.v_ready.at(n + 1))
                            if t == 0:
                                pe.wait_ge(c.o_ready.sem, c.o_ready.at(n))
                            pe.wait_ge(c.pT_ready.sem, c.pT_ready.at(m + 1))
                            for h in range(4):
                                hh = 4 * t + h
                                last = nc.tensor.matmul(bank_o[:, hh * (dh + 1):(hh + 1) * (dh + 1)],
                                                        PT[par][:, h, :],
                                                        rotary.V[:, i, g * H + hh, :] if rotary else v[:, hh, :],
                                                        start=True, stop=True)
                            last.then_inc(c.pv_done.sem, 1)

                        scores(0)
                        for t in range(quads):
                            if t + 1 < quads:
                                scores(t + 1)
                            transposes(t)
                            if t:
                                values(t - 1)
                        values(quads - 1)
                        pe.wait_ge(c.o_ready.sem, c.o_ready.at(n + 1))
                        pe.wait_ge(c.k_ready.sem, c.k_ready.at(n + 1))
                        for j in range(KD):
                            last = nc.tensor.transpose(bank_m[:, j * S:(j + 1) * S], o[:, j * P:(j + 1) * P],
                                                       c.ident[:, :])
                        last.then_inc(c.ot_ps.sem, 1)
                        pe.wait_ge(c.oT_ready.sem, c.oT_ready.at(n + 1))
                        if g == 0:
                            pe.wait_ge(c.x_added.sem, c.x_added.at(i))
                        for j in range(KD):
                            last = nc.tensor.matmul(bank_y[:, 0:D], oT[:, j, :], wo[:, g * KD + j, :],
                                                    start=(g == 0 and j == 0),
                                                    stop=(g == groups - 1 and j == KD - 1))
                        last.then_inc(c.y_ps.sem, 1)
    own = rotary is None
    c.passed(chain_v=1 + B * vector_steps, chain_p=0 if own else 4 * B, xn_ready=B if own else 2 * B,
             xt_ps=B * own, xT_ready=B * own, ctx_ready=B * ctx_kv,
             k_ps=B * groups, q_ready=B * groups, k_ready=B * groups, v_ps=B * groups, v_ready=B * groups * own,
             km_ready=B * T, s_ps=B * T, e_ready=B * T, p_ready=B * T, pt_ps=B * T, pT_ready=B * T, pv_done=B * T,
             o_ready=B * groups, ot_ps=B * groups, oT_ready=B * groups, y_ps=B * groups, x_added=B)


def per_head(ap):
    return ap.unsqueeze(1).to_broadcast([P, 4, S])


def no_mask(g, t, i):
    return None, None


def l0_attn(c, w):
    with ExitStack() as ctx:
        wqkv = c.sb(ctx, "l0a_wqkv", [P, KD, 3072])
        wo = c.sb(ctx, "l0a_wo", [P, 8, D])
        load(c, [(wqkv[:, :, :], w["L0_attn_W_qkv"]), (wo[:, :, :], w["L0_attn_W_out"])])
        layernorm_stats(c, [c.x])
        attention(c, "l0a", 4, 1, 64, (wqkv[:, :, 0:1024], wqkv[:, :, 1024:2048], wqkv[:, :, 2048:3072], wo),
                  q_scale=[0.125] * 4, mask_of=lambda g, t, i: (None, per_head(c.causal_add[:, :])))


def l0_xattn(c, w):
    with ExitStack() as ctx:
        wq = c.sb(ctx, "l0x_wq", [P, KD, 1024])
        wkv = c.sb(ctx, "l0x_wkv", [P, KD, 2048])
        wo = c.sb(ctx, "l0x_wo", [P, 8, D])
        bo = c.sb(ctx, "l0x_bo", [P, D])
        load(c, [(wq[:, :, :], w["L0_xattn_Wq"]), (wkv[:, :, :], w["L0_xattn_Wkv"]),
                 (wo[:, :, :], w["L0_xattn_Wout"]), (bo[:, :], w["L0_xattn_bout"])])
        layernorm_stats(c, [c.x])
        attention(c, "l0x", 4, 1, 64, (wq, wkv[:, :, 0:1024], wkv[:, :, 1024:2048], wo), ctx_kv=True,
                  q_scale=[0.125] * 4, y_bias=bo, mask_of=no_mask)


def xattn_masked(c, w, name, mask, fill, names):
    q, qb, k, kb, v, vb, o, ob = names
    with ExitStack() as ctx:
        ws = [c.sb(ctx, f"{name}_w{i}", [P, KD, D]) for i in range(4)]
        qkb = [c.sb(ctx, f"{name}_b{i}", [P, KD]) for i in range(2)]
        vob = [c.sb(ctx, f"{name}_bb{i}", [P, D]) for i in range(2)]
        mi = c.sb(ctx, f"{name}_mi", [P, B, S], I32)
        keep = c.sb(ctx, f"{name}_keep", [P, B, S])
        put = c.sb(ctx, f"{name}_put", [P, B, S])
        load(c, [(ws[0][:, :, :], w[q]), (ws[1][:, :, :], w[k]), (ws[2][:, :, :], w[v]), (ws[3][:, :, :], w[o]),
                 (qkb[0][:, :], w[qb]), (qkb[1][:, :], w[kb]), (vob[0][:, :], w[vb]), (vob[1][:, :], w[ob]),
                 (mi[:, :, :], w[mask])])
        layernorm_stats(c, [c.x])
        with c.nc.Block() as block:
            @block.vector
            def _(dve):
                chain = Chain(dve, c.chain_v, 0)
                chain(c.nc.vector.tensor_scalar(keep[:, :, :], mi[:, :, :], 0.0, None, ALU.not_equal))
                chain(c.nc.vector.tensor_scalar(put[:, :, :], keep[:, :, :], -fill, fill, ALU.mult, ALU.add))
        c.passed(chain_v=2)
        attention(c, name, 1, 4, 16, ws, ctx_kv=True, q_scale=[0.25], q_bias=qkb[0], k_bias=qkb[1], v_bias=vob[0],
                  y_bias=vob[1], mask_of=lambda g, t, i: (per_head(keep[:, i, :]), per_head(put[:, i, :])))


def l1_xattn(c, w):
    n = "L1_xattn_W"
    xattn_masked(c, w, "l1x", "mask_Bx1xSxS2_ik1", 1e-9,
                 [n + "Q_w", n + "Q_b", n + "K_w", n + "K_b", n + "V_w", n + "V_b", n + "O_w", n + "O_b"])


def l3_xattn(c, w):
    n = "L3_xattn_"
    xattn_masked(c, w, "l3x", "mask_BxSxS2_if1", -1e9,
                 [n + "Wq", n + "bq", n + "Wk", n + "bk", n + "Wv", n + "bv", n + "Wo", n + "bo"])


def l2_xattn(c, w):
    with ExitStack() as ctx:
        ws = [c.sb(ctx, f"l2x_w{i}", [P, KD, D]) for i in range(4)]
        load(c, [(ws[i][:, :, :], w["L2_xattn_W" + n]) for i, n in enumerate("qkvo")])
        layernorm_stats(c, [c.x])
        attention(c, "l2x", 1, 4, 16, ws, ctx_kv=True, q_scale=[0.25], mask_of=no_mask)


def l3_attn(c, w):
    with ExitStack() as ctx:
        ws = [c.sb(ctx, f"l3a_w{i}", [P, KD, D]) for i in range(4)]
        qkb = [c.sb(ctx, f"l3a_b{i}", [P, KD]) for i in range(2)]
        vob = [c.sb(ctx, f"l3a_bb{i}", [P, D]) for i in range(2)]
        alibi = c.sb(ctx, "l3a_alibi", [P, 16, S])
        n = "L3_attn_"
        load(c, [(ws[i][:, :, :], w[n + "W" + m]) for i, m in enumerate("qkvo")]
             + [(qkb[0][:, :], w[n + "bq"]), (qkb[1][:, :], w[n + "bk"]), (vob[0][:, :], w[n + "bv"]),
                (vob[1][:, :], w[n + "bo"]), (alibi[:, :, :], w["alibi"])])
        layernorm_stats(c, [c.x])
        attention(c, "l3a", 1, 4, 16, ws, q_scale=[0.25], q_bias=qkb[0], k_bias=qkb[1], v_bias=vob[0],
                  y_bias=vob[1], mask_of=lambda g, t, i: (None, alibi[:, 4 * t:4 * t + 4, :]))


def l1_attn(c, w):
    nc = c.nc
    with ExitStack() as ctx:
        wq, wk, wv = (c.sb(ctx, f"l1a_w{n}", [P, KD, 2 * D]) for n in "qkv")
        wo = c.sb(ctx, "l1a_wo", [P, 4, D])
        wT = c.sb(ctx, "l1a_wT", [P, 2, KD, D])
        feat = c.sb(ctx, "l1a_feat", [P, 2, KD, D])
        norm_w = c.sb(ctx, "l1a_norm", [P, KD])
        xin = c.sb(ctx, "l1a_xin", [P, B, D])
        causal, c2, window = (c.sb(ctx, f"l1a_m{i}", [P, S]) for i in range(3))
        a = "L1_attn_"
        load(c, [(wq[:, :, D:], w[a + "Wq"]), (wk[:, :, D:], w[a + "Wk"]), (wv[:, :, 0:D], w[a + "Wv"]),
                 (wv[:, :, D:], w[a + "Wv"]), (wo[:, :, :], w[a + "Wout"]), (wT[:, 0, :, :], w[a + "WqT"]),
                 (wT[:, 1, :, :], w[a + "WkT"]), (feat[:, 0, :, :], w[a + "Wqf"]), (feat[:, 1, :, :], w[a + "Wkf"]),
                 (norm_w[:, :], w[a + "norm_w"]), (causal[:, :], w["causal"]), (c2[:, :], w["causal_minus2"]),
                 (window[:, :], w["window_add"])])
        layernorm_stats(c, [c.x])
        with nc.Block() as block:
            @block.tensor
            def _(pe):
                for a in range(2):
                    for j in range(KD):
                        for m in range(KD):
                            last = nc.tensor.matmul(c.bank[a][:, j * D:(j + 1) * D], wT[:, a, m, j * P:(j + 1) * P],
                                                    feat[:, a, m, :], start=m == 0, stop=m == KD - 1)
                    last.then_inc(c.h_ps.sem, 1)

            @block.scalar
            def _(act):
                for a, dst in enumerate((wq, wk)):
                    act.wait_ge(c.h_ps.sem, c.h_ps.at(a + 1))
                    nc.scalar.copy(dst[:, :, 0:D], c.bank[a][:, :].rearrange("p (j n) -> p j n", j=KD))

            @block.vector
            def _(dve):
                with dve.Fori(0, B) as i:
                    nc.vector.tensor_scalar(xin[:, i, :], c.x[:, i, :], c.mv[:, i, 0:1], c.rstd[:, bass.ds(i, 1)],
                                            ALU.subtract, ALU.mult)
        c.passed(h_ps=2)
        layernorm_stats(c, [c.x], rms_eps=1e-6)
        attention(c, "l1a", 2, 4, 16, (wq, wk, wv, wo), norm_w=norm_w, q_scale=[1.0, 0.25], lin_group=0, xin=xin,
                  mask_of=lambda g, t, i: ((per_head(causal[:, :]), per_head(c2[:, :])) if g == 0
                                           else (None, per_head(window[:, :]))))


def first_largest(nc, chain, vals, rev, mx, tmp, mask):
    bc = mx.unsqueeze(2).to_broadcast(list(vals.shape))
    chain(nc.vector.tensor_reduce(mx, vals, AX.X, ALU.max))
    chain(nc.vector.tensor_tensor(tmp, vals, bc, ALU.is_equal))
    chain(nc.vector.tensor_tensor(tmp, tmp, rev, ALU.mult))
    chain(nc.vector.tensor_reduce(mx, tmp, AX.X, ALU.max))
    chain(nc.vector.tensor_tensor(mask, tmp, bc, ALU.is_equal))


def route(c, name, E, xnT, comb, wg, *, g_bias=None, hidden=None, renorm_eps=None, capacity=None):
    nc = c.nc
    layernorm_stats(c, [c.x])
    with ExitStack() as ctx:
        sb = lambda n, shape: c.sb(ctx, f"{name}_{n}", shape)
        xn, xT = sb("xn", [P, D]), sb("xT", [P, KD, S])
        lg, pr, tmp, m1, m2 = (sb(n, [P, B, E]) for n in ("lg", "pr", "tmp", "m1", "m2"))
        r = [sb(f"r{i}", [P, B]) for i in range(3)]
        rev = sb("rev", [P, E])
        bg = sb("bg", [P, E])
        hT = sb("hT", [64, S]) if hidden else None
        load(c, [(rev[:, :], c.w[f"rev{E}"])] + ([(bg[:, :], g_bias)] if g_bias is not None else []))
        bank_x, bank_l, bank_h = c.bank[0], c.bank[1], c.bank[2]
        with nc.Block() as block:
            @block.vector
            def _(dve):
                with dve.Fori(0, B) as i:
                    dve.wait_ge(c.xt_ps.sem, c.xt_ps.at(i))
                    nc.vector.tensor_scalar(xn[:, :], c.x[:, i, :], c.mv[:, i, 0:1], c.rstd[:, bass.ds(i, 1)],
                                            ALU.subtract, ALU.mult).then_inc(c.xn_ready.sem, 1)
                    dve.wait_ge(c.l_ps.sem, c.l_ps.at(i + 1))
                    nc.vector.tensor_copy(lg[:, i, :], bank_l[:, 0:E]).then_inc(c.l_ready.sem, 1)

            @block.tensor
            def _(pe):
                with pe.Fori(0, B) as i:
                    pe.wait_ge(c.xn_ready.sem, c.xn_ready.at(i + 1))
                    for j in range(KD):
                        last = nc.tensor.transpose(bank_x[:, j * S:(j + 1) * S], xn[:, j * P:(j + 1) * P],
                                                   c.ident[:, :])
                    last.then_inc(c.xt_ps.sem, 1)
                    pe.wait_ge(c.xT_ready.sem, c.xT_ready.at(i + 1))
                    if hidden:
                        pe.wait_ge(c.h_ready.sem, c.h_ready.at(i))
                        for j in range(KD):
                            last = nc.tensor.matmul(bank_h[0:64, 0:S], hidden[0][:, j, :], xT[:, j, :],
                                                    start=j == 0, stop=j == KD - 1)
                        last.then_inc(c.h_ps.sem, 1)
                        pe.wait_ge(c.h_ready.sem, c.h_ready.at(i + 1))
                    pe.wait_ge(c.l_ready.sem, c.l_ready.at(i))
                    if hidden:
                        last = nc.tensor.matmul(bank_l[:, 0:E], hT[:, :], wg[:, 0:E], start=True, stop=True)
                    else:
                        for j in range(KD):
                            last = nc.tensor.matmul(bank_l[:, 0:E], xT[:, j, :], wg[:, j, :],
                                                    start=j == 0, stop=j == KD - 1)
                    last.then_inc(c.l_ps.sem, 1)

            @block.scalar
            def _(act):
                with act.Fori(0, B) as i:
                    act.wait_ge(c.xt_ps.sem, c.xt_ps.at(i + 1))
                    act.wait_ge(c.l_ps.sem, c.l_ps.at(i))
                    src = bank_x[:, 0:D].rearrange("p (j t) -> p j t", j=KD)
                    nc.scalar.copy(token_tile(xnT, i), src)
                    nc.scalar.copy(xT[:, :, :], src).then_inc(c.xT_ready.sem, 1)
                    if hidden:
                        act.wait_ge(c.h_ps.sem, c.h_ps.at(i + 1))
                        nc.scalar.activation(hT[:, :], bank_h[0:64, 0:S], ACT.Gelu, bias=hidden[1][:, 0:1])\
                            .then_inc(c.h_ready.sem, 1)
        c.passed(xn_ready=B, xt_ps=B, xT_ready=B, l_ps=B, l_ready=B, h_ps=B * bool(hidden), h_ready=B * bool(hidden))

        steps = [0]
        full = lambda a: a.unsqueeze(2).to_broadcast([P, B, E])
        with nc.Block() as block:
            @block.vector
            def _(dve):
                chain = Chain(dve, c.chain_v, 0)
                v = nc.vector
                L, Q, W, M1, M2 = (a[:, :, :] for a in (lg, pr, tmp, m1, m2))
                R = [a[:, :] for a in r]
                rv = rev[:, :].unsqueeze(1).to_broadcast([P, B, E])
                if g_bias is not None:
                    chain(v.tensor_tensor(L, L, bg[:, :].unsqueeze(1).to_broadcast([P, B, E]), ALU.add))
                chain(v.tensor_reduce(R[0], L, AX.X, ALU.max))
                v.tensor_tensor(Q, L, full(R[0]), ALU.subtract).then_inc(c.e_ready.sem, 1)
                dve.wait_ge(c.p_ready.sem, c.p_ready.at(1))
                chain(v.tensor_reduce(R[0], Q, AX.X, ALU.add))
                chain(v.reciprocal(R[1], R[0]))
                chain(v.tensor_tensor(Q, Q, full(R[1]), ALU.mult))
                vals = L if capacity else Q
                first_largest(nc, chain, vals, rv, R[0], W, M1)
                chain(v.scalar_tensor_tensor(out=L, in0=M1, scalar=NEG if capacity else -4.0, in1=vals,
                                             op0=ALU.mult, op1=ALU.add))
                first_largest(nc, chain, L, rv, R[0], W, M2)
                if renorm_eps is not None:
                    chain(v.tensor_tensor(W, M1, M2, ALU.add))
                    chain(v.tensor_tensor(W, W, Q, ALU.mult))
                    chain(v.tensor_reduce(R[0], W, AX.X, ALU.add))
                    chain(v.tensor_scalar(R[0], R[0], renorm_eps, None, ALU.add))
                    chain(v.reciprocal(R[1], R[0]))
                    chain(v.tensor_tensor(Q, Q, full(R[1]), ALU.mult))
                if capacity:
                    chain(v.tensor_copy(W, M1))
                    nc.vector.tensor_copy(L, M2).then_inc(c.a_ready.sem, 1)
                    dve.wait_ge(c.c_ps.sem, c.c_ps.at(1))
                    before = sb("before", [P, 2, B + 1, E])
                    place = sb("place", [P, B, E])
                    chain(v.memset(before[:, 0, 0, :], 0.0))
                    for a in range(2):
                        tot = c.bank[4 + a][:, 0:B * E].rearrange("p (b e) -> p b e", b=B)
                        if a:
                            chain(v.tensor_copy(before[:, 1, 0, :], before[:, 0, B, :]))
                        for b in range(B):
                            chain(v.tensor_tensor(before[:, a, b + 1, :], before[:, a, b, :], tot[:, b, :], ALU.add))
                        within = c.bank[2 + a][:, 0:B * E].rearrange("p (b e) -> p b e", b=B)
                        chain(v.tensor_tensor(place[:, :, :], within, before[:, a, 0:B, :], ALU.add))
                        chain(v.tensor_scalar(place[:, :, :], place[:, :, :], float(capacity), None, ALU.is_lt))
                        M = (M1, M2)[a]
                        chain(v.tensor_tensor(M, M, place[:, :, :], ALU.mult))
                chain(v.tensor_tensor(W, M1, M2, ALU.add))
                chain(v.tensor_tensor(comb[:, :, :], Q, W, ALU.mult))
                steps[0] = chain.n

            @block.scalar
            def _(act):
                act.wait_ge(c.e_ready.sem, c.e_ready.at(1))
                nc.scalar.activation(pr[:, :, :], pr[:, :, :], ACT.Exp).then_inc(c.p_ready.sem, 1)

            if capacity:
                @block.tensor
                def _(pe):
                    pe.wait_ge(c.a_ready.sem, c.a_ready.at(1))
                    for a, m in enumerate((m1, m2)):
                        flat = m[:, :, :].rearrange("p b e -> p (b e)")
                        nc.tensor.matmul(c.bank[2 + a][:, 0:B * E], c.earlier[:, :], flat, start=True, stop=True)
                        last = nc.tensor.matmul(c.bank[4 + a][:, 0:B * E], c.ones[:, :], flat, start=True, stop=True)
                    last.then_inc(c.c_ps.sem, 1)
        c.passed(e_ready=1, p_ready=1, chain_v=steps[0], a_ready=bool(capacity), c_ps=bool(capacity))


def add_output_bias(c, name, E, comb, bias):
    nc = c.nc
    with ExitStack() as ctx:
        cs, cT = c.sb(ctx, f"{name}_cs", [P, E]), c.sb(ctx, f"{name}_cT", [E, S])
        b2 = c.sb(ctx, f"{name}_b2", [E, D])
        load(c, [(b2[:, :], bias)])
        with nc.Block() as block:
            @block.gpsimd
            def _(pool):
                with pool.Fori(0, B) as i:
                    pool.wait_ge(c.cT_ps.sem, c.cT_ps.at(i))
                    nc.gpsimd.tensor_copy(cs[:, :], comb[:, i, :]).then_inc(c.comb_ready.sem, 1)

            @block.tensor
            def _(pe):
                with pe.Fori(0, B) as i:
                    pe.wait_ge(c.comb_ready.sem, c.comb_ready.at(i + 1))
                    nc.tensor.transpose(c.bank[0][0:E, 0:S], cs[:, :], c.ident[:, :]).then_inc(c.cT_ps.sem, 1)
                    pe.wait_ge(c.cT_ready.sem, c.cT_ready.at(i + 1))
                    pe.wait_ge(c.x_added.sem, c.x_added.at(i))
                    nc.tensor.matmul(c.bank[1][:, 0:D], cT[:, :], b2[:, :], start=True, stop=True)\
                        .then_inc(c.y_ps.sem, 1)

            @block.scalar
            def _(act):
                with act.Fori(0, B) as i:
                    act.wait_ge(c.cT_ps.sem, c.cT_ps.at(i + 1))
                    act.wait_ge(c.y_ps.sem, c.y_ps.at(i))
                    nc.scalar.copy(cT[:, :], c.bank[0][0:E, 0:S]).then_inc(c.cT_ready.sem, 1)

            @block.vector
            def _(dve):
                with dve.Fori(0, B) as i:
                    dve.wait_ge(c.y_ps.sem, c.y_ps.at(i + 1))
                    nc.vector.tensor_tensor(c.x[:, i, :], c.x[:, i, :], c.bank[1][:, 0:D], ALU.add)\
                        .then_inc(c.x_added.sem, 1)
    c.passed(comb_ready=B, cT_ps=B, cT_ready=B, y_ps=B, x_added=B)


def expert_mlps(c, name, w, gelu, capacity, renorm_eps, g_bias):
    nc, E, F = c.nc, 8, 1024
    FC = F // P
    TB, TW = 4, 512
    TT = TW // P
    with ExitStack() as ctx:
        sb = lambda n, shape: c.sb(ctx, f"{name}_{n}", shape)
        xnT, comb = sb("xnT", [P, KD, B * S]), sb("comb", [P, B, E])
        wg, b1 = sb("wg", [P, KD, E]), sb("b1", [P, E, FC])
        w1 = [sb(f"w1_{i}", [P, KD, F]) for i in range(2)]
        w2 = [sb(f"w2_{i}", [P, FC, D]) for i in range(2)]
        hT = sb("hT", [P, FC, TW])
        load(c, [(wg[:, :, :], w[name + "_Wg"]), (b1[:, :, :], w[name + "_b1"])])
        route(c, name, E, xnT, comb, wg, g_bias=g_bias, renorm_eps=renorm_eps, capacity=capacity)
        add_output_bias(c, name, E, comb, w[name + "_b2"])
        banks_h, banks_y = c.bank[0:4], c.bank[4:8]
        with nc.Block() as block:
            @block.sync
            def _(sp):
                for e in range(E):
                    if e >= 2:
                        sp.wait_ge(c.y_ps.sem, c.y_ps.at((e - 1) * TB * TT))
                    sp.dma_start(w1[e % 2][:, :, :], w[name + "_W1"][e]).then_inc(c.w_loaded[e % 2].sem, 16)
                    sp.dma_start(w2[e % 2][:, :, :], w[name + "_W2"][e]).then_inc(c.w_loaded[e % 2].sem, 16)

            @block.tensor
            def _(pe):
                with pe.Fori(0, E // 2) as pair:
                    for par in range(2):
                        with pe.Fori(0, TB) as tb:
                            pe.wait_ge(c.w_loaded[par].sem, c.w_loaded[par].at(pair * 32 + 32))
                            n = (pair * 2 + par) * TB + tb
                            for f in range(FC):
                                pe.wait_ge(c.h_ready.sem, c.h_ready.at(n * FC + f - 3))
                                for kd in range(KD):
                                    last = nc.tensor.matmul(banks_h[f % 4][:, :], w1[par][:, kd, f * P:(f + 1) * P],
                                                            xnT[:, kd, bass.ds(tb * TW, TW)],
                                                            start=kd == 0, stop=kd == KD - 1)
                                last.then_inc(c.h_ps.sem, 1)
                            for tt in range(TT):
                                pe.wait_ge(c.x_added.sem, c.x_added.at(n * TT + tt - 3))
                                for f in range(FC):
                                    if tt == 0:
                                        pe.wait_ge(c.h_ready.sem, c.h_ready.at(n * FC + f + 1))
                                    last = nc.tensor.matmul(banks_y[tt][:, 0:D], hT[:, f, tt * P:(tt + 1) * P],
                                                            w2[par][:, f, :], start=f == 0, stop=f == FC - 1)
                                last.then_inc(c.y_ps.sem, 1)

            @block.scalar
            def _(act):
                with act.Fori(0, E) as e:
                    with act.Fori(0, TB) as tb:
                        n = e * TB + tb
                        for f in range(FC):
                            act.wait_ge(c.h_ps.sem, c.h_ps.at(n * FC + f + 1))
                            if f == 0:
                                act.wait_ge(c.y_ps.sem, c.y_ps.at(n * TT))
                            nc.scalar.activation(hT[:, f, :], banks_h[f % 4][:, :], gelu,
                                                 bias=b1[:, bass.ds(e, 1), f]).then_inc(c.h_ready.sem, 1)

            @block.vector
            def _(dve):
                with dve.Fori(0, E) as e:
                    with dve.Fori(0, TB) as tb:
                        n = e * TB + tb
                        for tt in range(TT):
                            dve.wait_ge(c.y_ps.sem, c.y_ps.at(n * TT + tt + 1))
                            b = tb * TT + tt
                            dve.wait_ge(c.x_added.sem, c.x_added.at(n * TT + tt - 3))
                            nc.vector.scalar_tensor_tensor(out=c.x[:, b, :], in0=banks_y[tt][:, 0:D],
                                                           scalar=comb[:, b, bass.ds(e, 1)], in1=c.x[:, b, :],
                                                           op0=ALU.mult, op1=ALU.add).then_inc(c.x_added.sem, 1)
        n = E * TB
        c.passed(h_ps=n * FC, h_ready=n * FC, y_ps=n * TT, x_added=n * TT)
        for s in c.w_loaded:
            s.passed(16 * E)


def l0_ffn(c, w):
    expert_mlps(c, "L0_ffn", w, ACT.Gelu_apprx_tanh, None, 1e-8, w["L0_ffn_bg"])


def l1_ffn(c, w):
    expert_mlps(c, "L1_ffn", w, ACT.Gelu, 2 * 2 * B * S // 8, 1e-9, None)


def l2_ffn(c, w):
    nc, E = c.nc, 20
    with ExitStack() as ctx:
        sb = lambda n, shape: c.sb(ctx, f"l2f_{n}", shape)
        xnT, comb = sb("xnT", [P, KD, B * S]), sb("comb", [P, B, E])
        wg1, bg1, wg2 = sb("wg1", [P, KD, 64]), sb("bg1", [64, 1]), sb("wg2", [64, 2 * E])
        we = sb("we", [P, KD, E, D])
        xs = sb("xs", [P, KD, S])
        load(c, [(wg1[:, :, :], w["L2_ffn_wg1"]), (bg1[:, :], w["L2_ffn_bg1"]), (wg2[:, :], w["L2_ffn_wg2"]),
                 (we[:, :, :, :], w["L2_ffn_We"])])
        route(c, "l2f", E, xnT, comb, wg2, g_bias=w["L2_ffn_bg2"], hidden=(wg1, bg1))
        add_output_bias(c, "l2f", E, comb, w["L2_ffn_be"])
        PAIRS = E // 2
        with nc.Block() as block:
            @block.gpsimd
            def _(pool):
                with pool.Fori(0, B) as i:
                    pool.wait_ge(c.y_ps.sem, c.y_ps.at(i * PAIRS))
                    nc.gpsimd.tensor_copy(xs[:, :, :], token_tile(xnT, i)).then_inc(c.xs_ready.sem, 1)

            @block.tensor
            def _(pe):
                with pe.Fori(0, B) as i:
                    pe.wait_ge(c.xs_ready.sem, c.xs_ready.at(i + 1))
                    for e in range(PAIRS):
                        pe.wait_ge(c.x_added.sem, c.x_added.at(2 * (i * PAIRS + e - 4)))
                        for kd in range(KD):
                            last = nc.tensor.matmul(c.bank[e % 5][:, :], xs[:, kd, :],
                                                    we[:, kd, 2 * e:2 * e + 2, :].rearrange("p a n -> p (a n)"),
                                                    start=kd == 0, stop=kd == KD - 1)
                        last.then_inc(c.y_ps.sem, 1)

            @block.vector
            def _(dve):
                with dve.Fori(0, B) as i:
                    for e in range(E):
                        dve.wait_ge(c.y_ps.sem, c.y_ps.at(i * PAIRS + e // 2 + 1))
                        dve.wait_ge(c.x_added.sem, c.x_added.at(i * E + e))
                        nc.vector.scalar_tensor_tensor(out=c.x[:, i, :],
                                                       in0=c.bank[e // 2 % 5][:, (e % 2) * D:(e % 2 + 1) * D],
                                                       scalar=comb[:, i, e:e + 1], in1=c.x[:, i, :],
                                                       op0=ALU.mult, op1=ALU.add).then_inc(c.x_added.sem, 1)
        c.passed(xs_ready=B, y_ps=B * PAIRS, x_added=B * E)


def l2_attn(c, w):
    nc, NP, H, W = c.nc, 5, 16, D + 16
    j = np.arange(6, dtype=np.float32)
    tail = np.flip(np.cumsum(np.flip((j + 1.0) ** (-1.5))))
    beta = tail[1:].astype(np.float32)
    beta = beta / beta.sum()
    lo, hi = -1.0 + 1e-6, 1.0 - 1e-6
    with ExitStack() as ctx:
        sb = lambda n, shape: c.sb(ctx, f"l2a_{n}", shape)
        win, wo = sb("win", [P, KD, 3 * D]), sb("wo", [P, KD, D])
        xn, xT, v = sb("xn", [P, D]), sb("xT", [P, KD, S]), sb("v", [P, D])
        TQ, TK, R, CS = (sb(n, [P, NP, W]) for n in ("TQ", "TK", "R", "CS"))
        tmp = [sb(f"tmp{i}", [P, D]) for i in range(2)]
        nd, rden = sb("nd", [P, W]), sb("rden", [P, H])
        o, oT = sb("o", [P, D]), sb("oT", [P, KD, S])
        load(c, [(win[:, :, :], w["L2_attn_W_in"]), (wo[:, :, :], w["L2_attn_W_out"])])
        layernorm_stats(c, [c.x])
        bank_m, bank_qk, bank_v, bank_c = c.bank[0], c.bank[1], c.bank[2], c.bank[3:8]
        KV = 14

        with nc.Block() as block:
            @block.vector
            def _(dve):
                with dve.Fori(0, B) as i:
                    chain = Chain(dve, c.chain_v, i * KV)
                    v_ = nc.vector
                    dve.wait_ge(c.xt_ps.sem, c.xt_ps.at(i))
                    v_.tensor_scalar(xn[:, :], c.x[:, i, :], c.mv[:, i, 0:1], c.rstd[:, bass.ds(i, 1)],
                                     ALU.subtract, ALU.mult).then_inc(c.xn_ready.sem, 1)
                    dve.wait_ge(c.k_ps.sem, c.k_ps.at(i + 1))
                    for a, T in enumerate((TQ, TK)):
                        last = v_.tensor_scalar(T[:, 0, 0:D], bank_qk[:, a * D:(a + 1) * D], 0.25, hi,
                                                ALU.mult, ALU.min)
                    last.then_inc(c.k_ready.sem, 1)
                    dve.wait_ge(c.k_ready.sem, c.k_ready.at(i + 1))
                    for T in (TQ, TK):
                        last = v_.tensor_scalar(T[:, 0, 0:D], T[:, 0, 0:D], lo, None, ALU.max)
                    chain(last)
                    for p in range(1, NP):
                        for a, T in enumerate((TQ, TK)):
                            last = v_.scalar_tensor_tensor(out=tmp[a][:, :], in0=T[:, 0, 0:D], scalar=2.0,
                                                           in1=T[:, p - 1, 0:D], op0=ALU.mult, op1=ALU.mult)
                        chain(last)
                        for a, T in enumerate((TQ, TK)):
                            if p == 1:
                                last = v_.tensor_scalar(T[:, 1, 0:D], tmp[a][:, :], -1.0, None, ALU.add)
                            else:
                                last = v_.tensor_tensor(T[:, p, 0:D], tmp[a][:, :], T[:, p - 2, 0:D], ALU.subtract)
                        chain(last)
                    dve.wait_ge(c.v_ready.sem, c.v_ready.at(i + 1))
                    dve.wait_ge(c.c_ps.sem, c.c_ps.at(i * NP))
                    v_.tensor_tensor(R[:, :, 0:D], TK[:, :, 0:D], v[:, :].unsqueeze(1).to_broadcast([P, NP, D]),
                                     ALU.mult)
                    v_.tensor_reduce(R[:, :, D:W], TK[:, :, 0:D].rearrange("p n (h d) -> p n h d", h=H), AX.X,
                                     ALU.add).then_inc(c.a_ready.sem, 1)
                    chain(v_.tensor_reduce(TQ[:, :, D:W], TQ[:, :, 0:D].rearrange("p n (h d) -> p n h d", h=H),
                                           AX.X, ALU.add))
                    dve.wait_ge(c.c_ready.sem, c.c_ready.at((i + 1) * NP))
                    chain(v_.tensor_tensor(TQ[:, :, :], TQ[:, :, :], CS[:, :, :], ALU.mult))
                    chain(v_.tensor_reduce(nd[:, :], TQ[:, :, :].rearrange("p n f -> p f n"), AX.X, ALU.add))
                    chain(v_.tensor_scalar(nd[:, D:W], nd[:, D:W], 1e-7, None, ALU.add))
                    chain(v_.reciprocal(rden[:, :], nd[:, D:W]))
                    dve.wait_ge(c.ot_ps.sem, c.ot_ps.at(i))
                    v_.tensor_tensor(heads_of(o[:, :], H), heads_of(nd[:, 0:D], H),
                                     rden[:, :].unsqueeze(2).to_broadcast([P, H, 16]), ALU.mult)\
                        .then_inc(c.o_ready.sem, 1)
                    dve.wait_ge(c.y_ps.sem, c.y_ps.at(i + 1))
                    v_.tensor_tensor(c.x[:, i, :], c.x[:, i, :], bank_v[:, D:2 * D], ALU.add)\
                        .then_inc(c.x_added.sem, 1)
                    assert chain.n == KV, chain.n

            @block.scalar
            def _(act):
                with act.Fori(0, B) as i:
                    act.wait_ge(c.xt_ps.sem, c.xt_ps.at(i + 1))
                    act.wait_ge(c.v_ps.sem, c.v_ps.at(i))
                    nc.scalar.copy(xT[:, :, :], bank_m[:, 0:D].rearrange("p (j t) -> p j t", j=KD))\
                        .then_inc(c.xT_ready.sem, 1)
                    act.wait_ge(c.v_ps.sem, c.v_ps.at(i + 1))
                    act.wait_ge(c.a_ready.sem, c.a_ready.at(i))
                    nc.scalar.copy(v[:, :], bank_v[:, 0:D]).then_inc(c.v_ready.sem, 1)
                    for p in range(NP):
                        act.wait_ge(c.c_ps.sem, c.c_ps.at(i * NP + p + 1))
                        if p == 0:
                            act.wait_ge(c.o_ready.sem, c.o_ready.at(i))
                        nc.scalar.mul(CS[:, p, :], bank_c[p][:, 0:W], float(beta[p])).then_inc(c.c_ready.sem, 1)
                    act.wait_ge(c.ot_ps.sem, c.ot_ps.at(i + 1))
                    act.wait_ge(c.y_ps.sem, c.y_ps.at(i))
                    nc.scalar.copy(oT[:, :, :], bank_m[:, 0:D].rearrange("p (j q) -> p j q", j=KD))\
                        .then_inc(c.oT_ready.sem, 1)

            @block.tensor
            def _(pe):
                with pe.Fori(0, B) as i:
                    pe.wait_ge(c.xn_ready.sem, c.xn_ready.at(i + 1))
                    pe.wait_ge(c.oT_ready.sem, c.oT_ready.at(i))
                    for k in range(KD):
                        last = nc.tensor.transpose(bank_m[:, k * S:(k + 1) * S], xn[:, k * P:(k + 1) * P],
                                                   c.ident[:, :])
                    last.then_inc(c.xt_ps.sem, 1)
                    pe.wait_ge(c.xT_ready.sem, c.xT_ready.at(i + 1))
                    pe.wait_ge(c.k_ready.sem, c.k_ready.at(i))
                    for kd in range(KD):
                        last = nc.tensor.matmul(bank_qk[:, :], xT[:, kd, :], win[:, kd, 0:2 * D],
                                                start=kd == 0, stop=kd == KD - 1)
                    last.then_inc(c.k_ps.sem, 1)
                    pe.wait_ge(c.x_added.sem, c.x_added.at(i))
                    for kd in range(KD):
                        last = nc.tensor.matmul(bank_v[:, 0:D], xT[:, kd, :], win[:, kd, 2 * D:3 * D],
                                                start=kd == 0, stop=kd == KD - 1)
                    last.then_inc(c.v_ps.sem, 1)
                    pe.wait_ge(c.a_ready.sem, c.a_ready.at(i + 1))
                    pe.wait_ge(c.c_ready.sem, c.c_ready.at(i * NP))
                    for p in range(NP):
                        nc.tensor.matmul(bank_c[p][:, 0:W], c.upto[:, :], R[:, p, :], start=True, stop=True)\
                            .then_inc(c.c_ps.sem, 1)
                    pe.wait_ge(c.o_ready.sem, c.o_ready.at(i + 1))
                    for k in range(KD):
                        last = nc.tensor.transpose(bank_m[:, k * S:(k + 1) * S], o[:, k * P:(k + 1) * P],
                                                   c.ident[:, :])
                    last.then_inc(c.ot_ps.sem, 1)
                    pe.wait_ge(c.oT_ready.sem, c.oT_ready.at(i + 1))
                    pe.wait_ge(c.v_ready.sem, c.v_ready.at(i + 1))
                    for k in range(KD):
                        last = nc.tensor.matmul(bank_v[:, D:2 * D], oT[:, k, :], wo[:, k, :],
                                                start=k == 0, stop=k == KD - 1)
                    last.then_inc(c.y_ps.sem, 1)
        c.passed(chain_v=B * KV, xn_ready=B, xt_ps=B, xT_ready=B, k_ps=B, k_ready=B, v_ps=B, v_ready=B, a_ready=B,
                 c_ps=B * NP, c_ready=B * NP, o_ready=B, ot_ps=B, oT_ready=B, y_ps=B, x_added=B)

class Rotary:
    pass


def shift_in(c, xin, shifted):
    with c.nc.Block() as block:
        @block.sync
        def _(sp):
            sp.dma_start(shifted[1:P, :, :], xin[0:P - 1, :, P:D]).then_inc(c.shifted.sem, 16)
            sp.wait_ge(c.shifted.sem, c.shifted.at(16))
    c.passed(shifted=16)


def l3_ffn(c, w):
    with ExitStack() as ctx:
        xin, shifted = c.sb(ctx, "l3_xin", [P, B, D]), c.sb(ctx, "l3_shifted", [P, B, P])
        layernorm_stats(c, [c.x])
        with c.nc.Block() as block:
            @block.vector
            def _(dve):
                c.nc.vector.memset(shifted[:, :, :], 0.0)
                with dve.Fori(0, B) as i:
                    c.nc.vector.tensor_scalar(xin[:, i, :], c.x[:, i, :], c.mv[:, i, 0:1], c.rstd[:, bass.ds(i, 1)],
                                              ALU.subtract, ALU.mult)
        for layer in range(2):
            shift_in(c, xin, shifted)
            local_attention(c, w, layer, xin, shifted)
            shift_in(c, xin, shifted)
            gated_mlp(c, w, layer, xin, shifted)
        with c.nc.Block() as block:
            @block.vector
            def _(dve):
                c.nc.vector.tensor_tensor(c.x[:, :, :], c.x[:, :, :], xin[:, :, :], ALU.add)


def local_attention(c, w, layer, xin, shifted):
    nc, heads, dh = c.nc, 8, 64
    I = heads * dh
    name = f"l3l{layer}"
    with ExitStack() as outer:
        r = Rotary()
        r.QK = c.sb(outer, name + "_QK", [P, B, 2 * I])
        r.V = c.sb(outer, name + "_V", [P, B, heads, dh + 1])
        r.rnorm = c.sb(outer, name + "_rnorm", [P, B, 2 * heads])
        with ExitStack() as ctx:
            sb = lambda n, shape: c.sb(ctx, f"{name}_{n}", shape)
            wqkv = sb("wqkv", [P, KD, 3 * I])
            hs, hT, sq, ss = sb("hs", [P, D]), sb("hT", [P, KD, S]), sb("sq", [P, 2 * I]), sb("ss", [P, B, 2 * heads])
            load(c, [(wqkv[:, :, :], w["L3_ffn_wqkv"][layer])])
            bank_x, bank_q, bank_k, bank_v = c.bank[0:4]
            with nc.Block() as block:
                @block.gpsimd
                def _(pool):
                    nc.gpsimd.memset(r.V[:, :, :, :], 1.0).then_inc(c.a_ready.sem, 1)
                    with pool.Fori(0, B) as i:
                        pool.wait_ge(c.xt_ps.sem, c.xt_ps.at(i))
                        nc.gpsimd.tensor_copy(hs[:, 0:P], xin[:, i, 0:P])
                        nc.gpsimd.tensor_copy(hs[:, P:D], shifted[:, i, :]).then_inc(c.xn_ready.sem, 1)

                @block.tensor
                def _(pe):
                    with pe.Fori(0, B) as i:
                        pe.wait_ge(c.xn_ready.sem, c.xn_ready.at(i + 1))
                        for j in range(KD):
                            last = nc.tensor.transpose(bank_x[:, j * S:(j + 1) * S], hs[:, j * P:(j + 1) * P],
                                                       c.ident[:, :])
                        last.then_inc(c.xt_ps.sem, 1)
                        pe.wait_ge(c.xT_ready.sem, c.xT_ready.at(i + 1))
                        pe.wait_ge(c.k_ready.sem, c.k_ready.at(i))
                        for a, bank in enumerate((bank_q, bank_k)):
                            for kd in range(KD):
                                last = nc.tensor.matmul(bank[:, :], hT[:, kd, :], wqkv[:, kd, a * I:(a + 1) * I],
                                                        start=kd == 0, stop=kd == KD - 1)
                        last.then_inc(c.k_ps.sem, 1)
                        pe.wait_ge(c.v_ready.sem, c.v_ready.at(i))
                        for kd in range(KD):
                            last = nc.tensor.matmul(bank_v[:, :], hT[:, kd, :], wqkv[:, kd, 2 * I:3 * I],
                                                    start=kd == 0, stop=kd == KD - 1)
                        last.then_inc(c.v_ps.sem, 1)

                @block.scalar
                def _(act):
                    with act.Fori(0, B) as i:
                        act.wait_ge(c.xt_ps.sem, c.xt_ps.at(i + 1))
                        act.wait_ge(c.v_ps.sem, c.v_ps.at(i))
                        nc.scalar.copy(hT[:, :, :], bank_x[:, 0:D].rearrange("p (j t) -> p j t", j=KD))\
                            .then_inc(c.xT_ready.sem, 1)
                        act.wait_ge(c.k_ps.sem, c.k_ps.at(i + 1))
                        nc.scalar.copy(r.QK[:, i, 0:I], bank_q[:, :])
                        nc.scalar.copy(r.QK[:, i, I:2 * I], bank_k[:, :]).then_inc(c.k_ready.sem, 1)

                @block.vector
                def _(dve):
                    dve.wait_ge(c.a_ready.sem, c.a_ready.at(1))
                    with dve.Fori(0, B) as i:
                        chain = Chain(dve, c.chain_v, i * 2)
                        dve.wait_ge(c.v_ps.sem, c.v_ps.at(i + 1))
                        nc.vector.tensor_copy(r.V[:, i, :, 0:dh], heads_of(bank_v[:, :], heads))\
                            .then_inc(c.v_ready.sem, 1)
                        dve.wait_ge(c.k_ready.sem, c.k_ready.at(i + 1))
                        chain(nc.vector.tensor_tensor(sq[:, :], r.QK[:, i, :], r.QK[:, i, :], ALU.mult))
                        chain(nc.vector.tensor_reduce(ss[:, i, :], heads_of(sq[:, :], 2 * heads), AX.X, ALU.add))
            c.passed(xn_ready=B, xt_ps=B, xT_ready=B, k_ps=B, k_ready=B, v_ps=B, v_ready=B, chain_v=2 * B, a_ready=1)
            with nc.Block() as block:
                @block.scalar
                def _(act):
                    nc.scalar.activation(r.rnorm[:, :, :], ss[:, :, :], ACT.Sqrt).then_inc(c.std_ready.sem, 1)

                @block.vector
                def _(dve):
                    chain = Chain(dve, c.chain_v, 0)
                    dve.wait_ge(c.std_ready.sem, c.std_ready.at(1))
                    chain(nc.vector.tensor_scalar(ss[:, :, :], r.rnorm[:, :, :], 1e-12, None, ALU.max))
                    chain(nc.vector.reciprocal(r.rnorm[:, :, :], ss[:, :, :]))
            c.passed(std_ready=1, chain_v=2)
        with ExitStack() as ctx:
            wo = c.sb(ctx, name + "_wo", [P, I // P, D])
            r.scale, r.cos, r.sin = (c.sb(ctx, f"{name}_{n}", [P, 2, dh]) for n in ("scale", "cos", "sin"))
            load(c, [(wo[:, :, :], w["L3_ffn_wo"][layer]), (r.scale[:, :, :], w["L3_ffn_qk_scale"][layer]),
                     (r.cos[:, :, :], w["rotary_cos"]), (r.sin[:, :, :], w["rotary_sin"])])
            attention(c, name + "a", 2, 1, dh, (None, None, None, wo), q_scale=[8.0] * 2, rotary=r, into=xin,
                      mask_of=lambda g, t, i: (None, per_head(c.causal_add[:, :])))


def gated_mlp(c, w, layer, xin, shifted):
    nc, FC, TB, TW = c.nc, L3_HID // P, 4, 512
    TT = TW // P
    name = f"l3m{layer}"
    layernorm_stats(c, [xin[:, :, 0:P], shifted])
    with ExitStack() as ctx:
        sb = lambda n, shape: c.sb(ctx, f"{name}_{n}", shape)
        w1, w2 = sb("w1", [P, KD, 2 * L3_HID]), sb("w2", [P, FC, D])
        lg, lb, b1, b2 = sb("lg", [P, KD]), sb("lb", [P, KD]), sb("b1", [P, 2, FC]), sb("b2", [P, D])
        hs, hT = sb("hs", [P, D]), sb("hT", [P, KD, B * S])
        G = [sb(f"G{i}", [P, TW]) for i in range(2)]
        u, yb = sb("u", [P, FC, TW]), sb("yb", [P, D])
        load(c, [(w1[:, :, :], w["L3_ffn_w1"][layer]), (w2[:, :, :], w["L3_ffn_w2"][layer]),
                 (lg[:, :], w["L3_ffn_ln_g"][layer]), (lb[:, :], w["L3_ffn_ln_b"][layer]),
                 (b1[:, :, :], w["L3_ffn_b1"][layer]), (b2[:, :], w["L3_ffn_b2"][layer])])
        with nc.Block() as block:
            @block.vector
            def _(dve):
                with dve.Fori(0, B) as i:
                    dve.wait_ge(c.xt_ps.sem, c.xt_ps.at(i))
                    for cols, src in ((slice(0, P), xin[:, i, 0:P]), (slice(P, D), shifted[:, i, :])):
                        last = nc.vector.tensor_scalar(hs[:, cols], src, c.mv[:, i, 0:1], c.rstd[:, bass.ds(i, 1)],
                                                       ALU.subtract, ALU.mult)
                    last.then_inc(c.xn_ready.sem, 1)

            @block.tensor
            def _(pe):
                with pe.Fori(0, B) as i:
                    pe.wait_ge(c.xn_ready.sem, c.xn_ready.at(i + 1))
                    pe.wait_ge(c.xT_ready.sem, c.xT_ready.at(i))
                    for j in range(KD):
                        last = nc.tensor.transpose(c.bank[0][:, j * S:(j + 1) * S], hs[:, j * P:(j + 1) * P],
                                                   c.ident[:, :])
                    last.then_inc(c.xt_ps.sem, 1)

            @block.scalar
            def _(act):
                with act.Fori(0, B) as i:
                    act.wait_ge(c.xt_ps.sem, c.xt_ps.at(i + 1))
                    for j in range(KD):
                        last = nc.scalar.activation(hT[:, j, bass.ds(i * S, S)], c.bank[0][:, j * S:(j + 1) * S],
                                                    ACT.Identity, bias=lb[:, j:j + 1], scale=lg[:, j:j + 1])
                    last.then_inc(c.xT_ready.sem, 1)
        c.passed(xn_ready=B, xt_ps=B, xT_ready=B)

        bank_a, bank_g, bank_y = c.bank[0:2], c.bank[2:4], c.bank[4:8]
        with nc.Block() as block:
            @block.tensor
            def _(pe):
                with pe.Fori(0, TB) as tb:
                    for f in range(FC):
                        n = tb * FC + f
                        pe.wait_ge(c.a_ready.sem, c.a_ready.at(n - 1))
                        for kd in range(KD):
                            last = nc.tensor.matmul(bank_g[f % 2][:, :], w1[:, kd, L3_HID + f * P:L3_HID + (f + 1) * P],
                                                    hT[:, kd, bass.ds(tb * TW, TW)], start=kd == 0, stop=kd == KD - 1)
                        last.then_inc(c.h_ps.sem, 1)
                        for kd in range(KD):
                            last = nc.tensor.matmul(bank_a[f % 2][:, :], w1[:, kd, f * P:(f + 1) * P],
                                                    hT[:, kd, bass.ds(tb * TW, TW)], start=kd == 0, stop=kd == KD - 1)
                        last.then_inc(c.l_ps.sem, 1)
                    for tt in range(TT):
                        pe.wait_ge(c.x_added.sem, c.x_added.at(tb * TT + tt - 3))
                        for f in range(FC):
                            if tt == 0:
                                pe.wait_ge(c.a_ready.sem, c.a_ready.at(tb * FC + f + 1))
                            last = nc.tensor.matmul(bank_y[tt][:, 0:D], u[:, f, tt * P:(tt + 1) * P], w2[:, f, :],
                                                    start=f == 0, stop=f == FC - 1)
                        last.then_inc(c.y_ps.sem, 1)

            @block.scalar
            def _(act):
                with act.Fori(0, TB) as tb:
                    for f in range(FC):
                        n = tb * FC + f
                        act.wait_ge(c.h_ps.sem, c.h_ps.at(n + 1))
                        act.wait_ge(c.a_ready.sem, c.a_ready.at(n - 1))
                        nc.scalar.activation(G[f % 2][:, :], bank_g[f % 2][:, :], ACT.Gelu,
                                             bias=b1[:, 1, f:f + 1]).then_inc(c.h_ready.sem, 1)

            @block.vector
            def _(dve):
                with dve.Fori(0, TB) as tb:
                    for f in range(FC):
                        n = tb * FC + f
                        dve.wait_ge(c.h_ready.sem, c.h_ready.at(n + 1))
                        dve.wait_ge(c.l_ps.sem, c.l_ps.at(n + 1))
                        if f == 0:
                            dve.wait_ge(c.y_ps.sem, c.y_ps.at(tb * TT))
                        nc.vector.scalar_tensor_tensor(out=u[:, f, :], in0=bank_a[f % 2][:, :],
                                                       scalar=b1[:, 0, f:f + 1], in1=G[f % 2][:, :],
                                                       op0=ALU.add, op1=ALU.mult).then_inc(c.a_ready.sem, 1)
                    chain = Chain(dve, c.chain_v, tb * TT)
                    for tt in range(TT):
                        b = tb * TT + tt
                        dve.wait_ge(c.y_ps.sem, c.y_ps.at(b + 1))
                        dve.wait_ge(c.x_added.sem, c.x_added.at(b))
                        chain(nc.vector.tensor_tensor(yb[:, :], bank_y[tt][:, 0:D], b2[:, :], ALU.add))
                        nc.vector.tensor_tensor(xin[:, b, :], xin[:, b, :], yb[:, :], ALU.add)\
                            .then_inc(c.x_added.sem, 1)
        c.passed(h_ps=TB * FC, l_ps=TB * FC, h_ready=TB * FC, a_ready=TB * FC, y_ps=B, x_added=B, chain_v=B)


STEPS = [l0_attn, l0_xattn, l0_ffn, l1_attn, l1_xattn, l1_ffn, l2_attn, l2_xattn, l2_ffn, l3_attn, l3_xattn, l3_ffn]


def decoder(nc, w, out):
    with ExitStack() as ctx:
        c = Core(nc, ctx)
        c.hm16, c.hm64 = c.sb(ctx, "hm16", [P, 8]), c.sb(ctx, "hm64", [P, 2])
        c.one = c.sb(ctx, "one", [P, 1])
        c.ones, c.earlier, c.upto = (c.sb(ctx, n, [P, P]) for n in ("ones", "earlier", "upto"))
        c.w = w
        with nc.Block() as block:
            @block.sync
            def _(sp):
                for s in c.sig.values():
                    sp.sem_inc(s.sem, START)
        load(c, [(c.x[:, :, :], w["x"]), (c.ctxT[:, :, :], w["ctx_1024"]), (c.ident[:, :], w["ident"]),
                 (c.causal_add[:, :], w["causal_add"]), (c.hm16[:, :], w["hm16"]), (c.hm64[:, :], w["hm64"]),
                 (c.one[:, :], w["one"]), (c.ones[:, :], w["ones"]), (c.earlier[:, :], w["earlier"]),
                 (c.upto[:, :], w["upto"])])
        for n in SUBLAYERS:
            STEPS[n](c, w)
        with nc.Block() as block:
            @block.sync
            def _(sp):
                sp.dma_start(out, c.x[:, :, :]).then_inc(c.stored.sem, 16)
                sp.wait_ge(c.stored.sem, c.stored.at(16))


def layout(inputs):
    a = {k: np.asarray(v) for k, v in inputs.items()}
    cont = np.ascontiguousarray

    def rows(m):
        return cont(m.reshape(-1, P, m.shape[1]).transpose(1, 0, 2))

    def column(m):
        return cont(m.reshape(-1, P).T)

    def everywhere(m):
        return cont(np.broadcast_to(m, (P,) + m.shape))

    w = {"x": cont(a["x"].transpose(1, 0, 2)), "ctx_1024": rows(a["ctx_1024"].reshape(B * S, D).T)}
    w["mask_Bx1xSxS2_ik1"] = cont(a["mask_Bx1xSxS2_ik1"][:, 0].transpose(1, 0, 2))
    w["mask_BxSxS2_if1"] = cont(a["mask_BxSxS2_if1"].transpose(1, 0, 2))
    for n in ("L0_attn_W_qkv", "L0_attn_W_out", "L0_xattn_Wq", "L0_xattn_Wkv", "L0_xattn_Wout", "L0_ffn_Wg",
              "L1_attn_Wq", "L1_attn_Wk", "L1_attn_Wv", "L1_attn_Wout", "L1_ffn_Wg", "L2_ffn_wg1"):
        w[n] = rows(a[n])
    for n in ("L1_xattn_WQ_w", "L1_xattn_WK_w", "L1_xattn_WV_w", "L1_xattn_WO_w", "L2_attn_W_in", "L2_attn_W_out",
              "L2_xattn_Wq", "L2_xattn_Wk", "L2_xattn_Wv", "L2_xattn_Wo", "L3_attn_Wq", "L3_attn_Wk", "L3_attn_Wv",
              "L3_attn_Wo", "L3_xattn_Wq", "L3_xattn_Wk", "L3_xattn_Wv", "L3_xattn_Wo"):
        w[n] = rows(a[n].T)
    for n in ("L1_attn_norm_w", "L1_xattn_WQ_b", "L1_xattn_WK_b", "L3_attn_bq", "L3_attn_bk", "L3_xattn_bq",
              "L3_xattn_bk"):
        w[n] = column(a[n])
    for n in ("L0_xattn_bout", "L1_xattn_WV_b", "L1_xattn_WO_b", "L3_attn_bv", "L3_attn_bo", "L3_xattn_bv",
              "L3_xattn_bo"):
        w[n] = everywhere(a[n])
    for n in "qk":
        w[f"L1_attn_W{n}T"] = rows(a[f"L1_attn_W{n}"].T)
        f = a[f"L1_attn_W{n}f"]
        wide = np.zeros((D, D), f.dtype)
        for h in range(D // 16):
            wide[16 * h:16 * h + 16, 16 * h:16 * h + 16] = f
        w[f"L1_attn_W{n}f"] = rows(wide)
    for n in ("L0_ffn", "L1_ffn"):
        w[n + "_W1"] = cont(a[n + "_W1"].reshape(8, KD, P, 1024).transpose(0, 2, 1, 3))
        w[n + "_W2"] = cont(a[n + "_W2"].reshape(8, 8, P, D).transpose(0, 2, 1, 3))
        w[n + "_b1"] = cont(a[n + "_b1"].reshape(8, 8, P).transpose(2, 0, 1))
        w[n + "_b2"] = a[n + "_b2"]
    w["L0_ffn_bg"] = everywhere(a["L0_ffn_bg"])
    w["L2_ffn_bg1"] = cont(a["L2_ffn_bg1"][:, None])
    w["L2_ffn_wg2"] = a["L2_ffn_wg2"]
    w["L2_ffn_bg2"] = everywhere(a["L2_ffn_bg2"][:20])
    w["L2_ffn_We"] = cont(a["L2_ffn_We"].reshape(20, KD, P, D).transpose(2, 1, 0, 3))
    w["L2_ffn_be"] = a["L2_ffn_be"]
    n = "L3_ffn_"
    HID = int(D * 4 * 2 / 3)
    short = -HID % P
    w[n + "w1"] = np.stack([rows(np.pad(v.reshape(D, 2, HID), ((0, 0), (0, 0), (0, short))).reshape(D, -1))
                            for v in a[n + "w1"]])
    for m in ("wqkv", "wo"):
        w[n + m] = np.stack([rows(v) for v in a[n + m]])
    w[n + "w2"] = np.stack([rows(np.pad(v, ((0, short), (0, 0)))) for v in a[n + "w2"]])
    w[n + "ln_g"], w[n + "ln_b"] = (np.stack([column(v) for v in a[n + m]]) for m in ("ln_g", "ln_b"))
    w[n + "b1"] = cont(np.pad(a[n + "b1"].reshape(2, 2, HID), ((0, 0), (0, 0), (0, short)))
                       .reshape(2, 2, -1, P).transpose(0, 3, 1, 2))
    w[n + "b2"] = np.stack([everywhere(v) for v in a[n + "b2"]])
    w[n + "qk_scale"] = np.stack([everywhere(np.stack([q, k])) for q, k in zip(a[n + "q_scale"], a[n + "k_scale"])])
    f32 = np.float32
    q, k = np.arange(S)[:, None], np.arange(S)[None, :]
    w["ident"] = np.eye(P, dtype=f32)
    w["causal"] = (k <= q).astype(f32)
    w["causal_add"] = np.where(k <= q, 0.0, NEG).astype(f32)
    w["causal_minus2"] = np.where(k <= q, 0.0, -2.0).astype(f32)
    w["window_add"] = np.where((k <= q) & (k >= q - 64), 0.0, NEG).astype(f32)
    slopes = np.array([(2 ** (-2 ** (-(math.log2(16) - 3)))) ** (i + 1) for i in range(16)], f32)
    w["alibi"] = np.where(k[:, None] <= q[:, None], slopes[None, :, None] * (k - q)[:, None].astype(f32), f32(NEG)).astype(f32)
    p = np.arange(P)[:, None]
    w["hm16"] = (p // 16 == np.arange(8)[None]).astype(f32)
    w["hm64"] = (p // 64 == np.arange(2)[None]).astype(f32)
    w["ones"] = np.ones((P, P), f32)
    w["earlier"] = (q < k).astype(f32)
    w["upto"] = (q <= k).astype(f32)
    for n in (8, 20):
        w[f"rev{n}"] = everywhere(np.arange(n, 0, -1).astype(f32))
    dh, window = 64, 128
    even = np.arange(0, dh, 2, dtype=f32)
    turn = np.arange(S, dtype=f32)[:, None] * (f32(1.0) / f32(10000.0) ** (even / f32(dh)))[None]
    grow = ((even + f32(0.4 * dh)) / f32(1.4 * dh))[None] ** ((np.arange(S, dtype=f32) - S // 2)
                                                              / f32(window // 2))[:, None]
    cos, sin = np.cos(turn), np.sin(turn)
    w["rotary_cos"] = np.stack([np.concatenate([cos * g, cos * g], 1) for g in (grow, 1 / grow)], 1).astype(f32)
    w["rotary_sin"] = np.stack([np.concatenate([-sin * g, sin * g], 1) for g in (grow, 1 / grow)], 1).astype(f32)
    w["one"] = np.ones((P, 1), f32)
    return w


def kernel(**inputs):
    import concourse.bacc as bacc
    from concourse.bass_utils import run_bass_kernel_spmd

    nc = bacc.Bacc("TRN2", target_bir_lowering=False, num_devices=1)
    arrays = {f"in_{k}_dram": v for k, v in layout(inputs).items()}
    w = {k: nc.dram_tensor(f"in_{k}_dram", v.shape, mybir.dt.from_np(v.dtype), kind="ExternalInput").ap()
         for k, v in ((n[3:-5], v) for n, v in arrays.items())}
    out = nc.dram_tensor("out_0_dram", (S, B, D), F32, kind="ExternalOutput").ap()
    decoder(nc, w, out)
    got = run_bass_kernel_spmd(nc, [arrays], core_ids=[0]).results[0]["out_0_dram"]
    return np.ascontiguousarray(np.asarray(got).transpose(1, 0, 2))
```

```python
from contextlib import ExitStack
import math

import numpy as np

import concourse.bass as bass
from concourse import mybir

F32 = mybir.dt.float32
I32 = mybir.dt.int32
ALU = mybir.AluOpType
ACT = mybir.ActivationFunctionType
AX = mybir.AxisListType

B, S, D = 16, 128, 256
P = 128
KD = D // P
LN_EPS = 1e-5
NEG = -1e30

L3_HID = -(-int(D * 4 * 2 / 3) // P) * P
WIDTH = 256
MOST = B * S // WIDTH
ROWS = (2 * MOST + 8) * WIDTH
START = 8

SUBLAYERS = range(12)


class Signal:

    def __init__(self, sem, start=START):
        self.sem, self.base, self.start = sem, start, start

    def at(self, n):
        return self.base + n

    def passed(self, n):
        self.base += n


class Chain:

    def __init__(self, eng, counted, start):
        self.eng, self.counted, self.start, self.first, self.n = eng, counted, start, start, 0

    def __call__(self, ins):
        self.n += 1
        ins.then_inc(self.counted.sem, 1)
        self.eng.wait_ge(self.counted.sem, self.counted.at(self.start + self.n))


class Core:

    def __init__(self, nc, ctx):
        self.nc, self.ctx = nc, ctx
        self.sig = {}
        self.loaded = self.count("loaded")
        self.stored = self.count("stored")
        self.xn_ready = self.count("xn_ready")
        self.xt_ps = self.count("xt_ps")
        self.xT_ready = self.count("xT_ready")
        self.ctx_ready = self.count("ctx_ready")
        self.k_ps = self.count("k_ps")
        self.q_ready = self.count("q_ready")
        self.k_ready = self.count("k_ready")
        self.v_ps = self.count("v_ps")
        self.v_ready = self.count("v_ready")
        self.km_ready = self.count("km_ready")
        self.s_ps = self.count("s_ps")
        self.e_ready = self.count("e_ready")
        self.p_ready = self.count("p_ready")
        self.pt_ps = self.count("pt_ps")
        self.pT_ready = self.count("pT_ready")
        self.pv_done = self.count("pv_done")
        self.o_ready = self.count("o_ready")
        self.ot_ps = self.count("ot_ps")
        self.oT_ready = self.count("oT_ready")
        self.y_ps = self.count("y_ps")
        self.x_added = self.count("x_added")
        self.v_set = self.count("v_set")
        self.chain_v = self.count("chain_v")
        self.chain_p = self.count("chain_p")
        self.stats_ready = self.count("stats_ready")
        self.std_ready = self.count("std_ready")
        self.h_ps = self.count("h_ps")
        self.h_ready = self.count("h_ready")
        self.l_ps = self.count("l_ps")
        self.l_ready = self.count("l_ready")
        self.c_ps = self.count("c_ps")
        self.c_ready = self.count("c_ready")
        self.shifted = self.count("shifted")
        self.comb_ready = self.count("comb_ready")
        self.cT_ps = self.count("cT_ps")
        self.cT_ready = self.count("cT_ready")
        self.a_ready = self.count("a_ready")
        self.xs_ready = self.count("xs_ready")
        self.cleared = self.count("cleared")
        self.scattered = self.count("scattered", 0)
        self.gathered = [self.count(f"gathered{i}", 0) for i in range(2)]
        self.w_loaded = [self.count(f"w_loaded{i}") for i in range(2)]
        sb = self.sb
        self.x = sb(ctx, "x_res", [P, B, D])
        self.ctxT = sb(ctx, "ctxT", [P, KD, B * S])
        self.ident = sb(ctx, "ident", [P, P])
        self.causal_add = sb(ctx, "causal_add", [P, P])
        self.stats = sb(ctx, "stats", [P, B, 2, 6])
        self.mv = sb(ctx, "mv", [P, B, 2])
        self.std = sb(ctx, "std", [P, B])
        self.rstd = sb(ctx, "rstd", [P, B])
        self.bank = [ctx.enter_context(nc.psum_tensor(f"bank{i}", [P, 512], F32)) for i in range(8)]

    def count(self, name, start=START):
        self.sig[name] = Signal(self.ctx.enter_context(self.nc.semaphore("s_" + name)), start)
        return self.sig[name]

    def sb(self, ctx, name, shape, dt=F32):
        return ctx.enter_context(self.nc.sbuf_tensor(name, shape, dt))

    def passed(self, **counts):
        for name, n in counts.items():
            self.sig[name].passed(n)


def m_parity(g, quads, t):
    return (g * quads + t) % 2


def token_tile(t, b):
    return t[:, :, bass.ds(b * S, S)]


def heads_of(ap, h):
    return ap.rearrange("p (h d) -> p h d", h=h)


def load(c, pairs):
    with c.nc.Block() as block:
        @block.sync
        def _(sp):
            for dst, src in pairs:
                sp.dma_start(dst, src).then_inc(c.loaded.sem, 16)
            sp.wait_ge(c.loaded.sem, c.loaded.at(16 * len(pairs)))
    c.passed(loaded=16 * len(pairs))


def layernorm_stats(c, halves, eps=LN_EPS, rms_eps=None):
    nc, n = c.nc, len(halves)
    with nc.Block() as block:
        @block.vector
        def _(dve):
            with dve.Fori(0, B) as b:
                for k, half in enumerate(halves):
                    last = nc.vector.bn_stats(c.stats[:, b, k, :], half[:, b, :])
                last.then_inc(c.stats_ready.sem, 1)
            dve.wait_ge(c.stats_ready.sem, c.stats_ready.at(B))
            chain = Chain(dve, c.chain_v, 0)
            for b in range(B):
                last = nc.vector.bn_aggr(c.mv[:, b, :], c.stats[:, b, 0:n, :])
            chain(last)
            chain(nc.vector.tensor_scalar(c.std[:, :], c.mv[:, :, 1], eps, None, ALU.add))
            if rms_eps is not None:
                chain(nc.vector.scalar_tensor_tensor(out=c.std[:, :], in0=c.std[:, :], scalar=rms_eps,
                                                     in1=c.mv[:, :, 1], op0=ALU.mult, op1=ALU.add))
            nc.vector.tensor_copy(c.rstd[:, :], c.std[:, :]).then_inc(c.stats_ready.sem, 1)
            dve.wait_ge(c.std_ready.sem, c.std_ready.at(1))
            chain(nc.vector.reciprocal(c.rstd[:, :], c.std[:, :]))

        @block.scalar
        def _(act):
            act.wait_ge(c.stats_ready.sem, c.stats_ready.at(B + 1))
            nc.scalar.activation(c.std[:, :], c.rstd[:, :], ACT.Sqrt).then_inc(c.std_ready.sem, 1)
    c.passed(stats_ready=B + 1, std_ready=1, chain_v=3 + (rms_eps is not None))


class Pipeline:

    def __init__(self, groups, quads, lags):
        self.groups, self.quads, self.lags = groups, quads, lags
        self.T = groups * quads
        self.sequences = 1 if self.T >= 4 and groups > 1 else 2
        self.span = self.T * self.sequences
        self.bodies = B // self.sequences
        self.peeled = -(-max(lags.values()) // self.span)

    def item(self, i, k, stage):
        return Item(self, i, k - self.lags[stage])

    def issued(self, i, k, stage, unit, first):
        k -= self.lags[stage]
        n = i * (self.span // unit) + (-(-k // unit) if first else k // unit)
        return min(max(n, 0), B * self.T // unit) if isinstance(n, int) else n

    def run(self, eng, body, chain=None, steps=0):
        for i in range(self.peeled):
            body(i)
        before = chain.n if chain else 0
        with eng.Fori(self.peeled, self.bodies) as i:
            if chain:
                chain.start, chain.n = chain.first + before + (i - self.peeled) * steps, 0
            body(i)
            assert chain is None or chain.n == steps, (chain.n, steps)
        if chain:
            chain.start, chain.n = chain.first, before + (self.bodies - self.peeled) * steps
        for i in range(self.bodies, self.bodies + self.peeled):
            body(i)


class Item:

    def __init__(self, pipe, i, k):
        r = k % pipe.T
        self.g, self.t, self.at = r // pipe.quads, r % pipe.quads, k % pipe.span
        self.b = i * pipe.sequences + (k - r) // pipe.T
        self.n = self.b * pipe.groups + self.g
        self.m = self.b * pipe.T + r
        self.missing = isinstance(self.b, int) and not 0 <= self.b < B
        self.first = self.t == 0
        self.last = self.t == pipe.quads - 1
        self.group_at = self.at // pipe.quads


def attention(c, name, groups, quads, dh, weights, *, ctx_kv=False, norm_w=None, q_scale, q_bias=None,
              k_bias=None, v_bias=None, y_bias=None, lin_group=None, mask_of=None,
              xin=None, rotary=None, into=None):
    nc = c.nc
    H = 4 * quads
    T = groups * quads
    wq, wk, wv, wo = weights
    into = c.x if into is None else into
    bank_m, bank_v, bank_o, bank_y = c.bank[0], c.bank[1], c.bank[6], c.bank[7]
    bank_s, bank_t = c.bank[2:4], c.bank[4:6]
    if quads == 1:
        lags = dict(xn=0, x=1, qkv=2, s=3, e=3, t=4, pv=5, ot=6, y=7)
        NV = 4
    else:
        lags = dict(xn=0, x=1, qkv=2, s=4, e=5, t=6, pv=7, ot=8, y=9)
        NV = 2
    pipe = Pipeline(groups, quads, lags)
    NG = pipe.span // quads
    NV = min(NV, NG)
    NK = min(4, pipe.span)
    own = rotary is None
    with ExitStack() as ctx:
        sb = lambda n, shape: c.sb(ctx, f"{name}_{n}", shape)
        xn, xT = sb("xn", [P, D]), sb("xT", [P, KD, S])
        q = [sb(f"q{i}", [P, KD, S]) for i in range(2)]
        k = [sb(f"k{i}", [P, KD, S]) for i in range(2)]
        kv_src = sb("ctx", [P, KD, S]) if ctx_kv else xT
        km = [sb(f"km{i}", [P, 4, S]) for i in range(NK)]
        v = [sb(f"v{i}", [P, H, dh + 1]) for i in range(NV)] if own else []
        E = [sb(f"E{i}", [P, 4, S]) for i in range(2)]
        Pr = [sb(f"P{i}", [P, 4, S]) for i in range(2)]
        PT = [sb(f"PT{i}", [P, 4, S]) for i in range(2)]
        mx = [sb(f"mx{i}", [P, 4]) for i in range(2)]
        rden = sb("rden", [P, H])
        o, oT = sb("o", [P, D]), sb("oT", [P, KD, S])
        yb = sb("yb", [P, D])
        hm = c.hm16 if dh == 16 else c.hm64
        vector_steps = (y_bias is not None) + (xin is not None) + 4 * (not own)
        for g in range(groups):
            masks = sum(a is not None for a in mask_of(g, 0, 0))
            vector_steps += quads * (masks - 1) + 2 if g == lin_group else quads * (masks + 1) + 1
        rotated = [[sb(f"rot{a}{n}", [P, H * groups, dh]) for n in range(2)] for a in range(2)] if rotary else None
        turning = [sb(f"turning{a}", [P, H * groups, dh]) for a in range(2)] if rotary else None

        def rotate(eng, chain, a, it):
            n = H * groups
            t, r, i = turning[a], rotated[a][it.at // T % 2], it.b
            per_token = lambda m: m.unsqueeze(1).to_broadcast([P, n, m.shape[1]])
            src = heads_of(rotary.QK[:, i, a * n * dh:(a + 1) * n * dh], n)
            eng.wait_ge(c.v_ps.sem, c.v_ps.at((i - 1) * groups))
            chain(eng.tensor_tensor(t[:, :, :], src, rotary.rnorm[:, i, a * n:(a + 1) * n].unsqueeze(2)
                                    .to_broadcast([P, n, dh]), ALU.mult))
            chain(eng.tensor_tensor(t[:, :, :], t[:, :, :], per_token(rotary.scale[:, a, :]), ALU.mult))
            half = dh // 2
            eng.tensor_tensor(r[:, :, 0:half], t[:, :, half:], per_token(rotary.sin[:, a, 0:half]), ALU.mult)
            chain(eng.tensor_tensor(r[:, :, half:], t[:, :, 0:half], per_token(rotary.sin[:, a, half:]), ALU.mult))
            chain(eng.tensor_tensor(t[:, :, :], t[:, :, :], per_token(rotary.cos[:, a, :]), ALU.mult))
            eng.tensor_tensor(r[:, :, :], r[:, :, :], t[:, :, :], ALU.add).then_inc(c.xn_ready.sem, 1)

        with nc.Block() as block:
            @block.vector
            def _(dve):
                for buffer in v:
                    last = nc.vector.memset(buffer[:, :, :], 1.0)
                if own:
                    last.then_inc(c.v_set.sem, 1)
                    dve.wait_ge(c.v_set.sem, c.v_set.at(1))
                chain = Chain(dve, c.chain_v, 0)

                def normalised(it):
                    dve.wait_ge(c.xt_ps.sem, c.xt_ps.at(it.b))
                    nc.vector.tensor_scalar(xn[:, :], c.x[:, it.b, :], c.mv[:, it.b, 0:1],
                                            c.rstd[:, bass.ds(it.b, 1)],
                                            ALU.subtract, ALU.mult).then_inc(c.xn_ready.sem, 1)

                def projected(it):
                    dve.wait_ge(c.v_ps.sem, c.v_ps.at(it.n + 1))
                    dve.wait_ge(c.s_ps.sem, c.s_ps.at((it.n - 1) * quads))
                    for j in range(KD):
                        src = bank_v[:, D + j * S:D + (j + 1) * S]
                        dst = q[it.group_at % 2][:, j, :]
                        if q_bias is not None:
                            last = nc.vector.tensor_scalar(dst, src, q_bias[:, j:j + 1], q_scale[it.g],
                                                           ALU.add, ALU.mult)
                        else:
                            last = nc.vector.tensor_scalar(dst, src, q_scale[it.g], None, ALU.mult)
                    last.then_inc(c.q_ready.sem, 1)
                    if own:
                        dve.wait_ge(c.pv_done.sem, c.pv_done.at((it.n - NV + 1) * quads))
                        vd = v[it.group_at % NV][:, :, 0:dh]
                        vs = heads_of(bank_v[:, 0:D], H)
                        if v_bias is not None:
                            nc.vector.tensor_tensor(vd, vs, heads_of(v_bias[:, :], H), ALU.add)\
                                .then_inc(c.v_ready.sem, 1)
                        else:
                            nc.vector.tensor_copy(vd, vs).then_inc(c.v_ready.sem, 1)

                def exponents(it):
                    par = it.at % 2
                    lin = it.g == lin_group
                    e = E[par]
                    src = bank_s[par][:, :].rearrange("p (h k) -> p h k", h=4)
                    dve.wait_ge(c.s_ps.sem, c.s_ps.at(it.m + 1))
                    dve.wait_ge(c.p_ready.sem, c.p_ready.at(it.m - 1))
                    mul, plus = mask_of(it.g, it.t, it.b)
                    if mul is not None:
                        chain(nc.vector.tensor_tensor(e[:, :, :], src, mul, ALU.mult))
                        src = e[:, :, :]
                    if plus is not None:
                        ins = nc.vector.tensor_tensor(e[:, :, :], src, plus, ALU.add)
                        if lin:
                            ins.then_inc(c.e_ready.sem, 1)
                            return
                        chain(ins)
                        src = e[:, :, :]
                    most = mx[par]
                    chain(nc.vector.tensor_reduce(most[:, :], src, AX.X, ALU.max))
                    nc.vector.tensor_tensor(e[:, :, :], src, most[:, :].unsqueeze(2).to_broadcast([P, 4, S]),
                                            ALU.subtract).then_inc(c.e_ready.sem, 1)

                def output(it):
                    dve.wait_ge(c.pv_done.sem, c.pv_done.at((it.n + 1) * quads))
                    po = bank_o[:, 0:H * (dh + 1)].rearrange("p (h d) -> p h d", h=H)
                    if it.g == lin_group:
                        chain(nc.vector.tensor_scalar(rden[:, :], po[:, :, dh], 1e-6, None, ALU.add))
                        chain(nc.vector.reciprocal(rden[:, :], rden[:, :]))
                    else:
                        chain(nc.vector.reciprocal(rden[:, :], po[:, :, dh]))
                    dve.wait_ge(c.ot_ps.sem, c.ot_ps.at(it.n))
                    nc.vector.tensor_tensor(heads_of(o[:, :], H), po[:, :, 0:dh],
                                            rden[:, :].unsqueeze(2).to_broadcast([P, H, dh]), ALU.mult)\
                        .then_inc(c.o_ready.sem, 1)

                def residual(it):
                    dve.wait_ge(c.y_ps.sem, c.y_ps.at((it.b + 1) * groups))
                    y = bank_y[:, 0:D]
                    if y_bias is not None:
                        chain(nc.vector.tensor_tensor(yb[:, :], y, y_bias[:, :], ALU.add))
                        y = yb[:, :]
                    if xin is not None:
                        chain(nc.vector.tensor_tensor(yb[:, :], y, xin[:, it.b, :], ALU.add))
                        y = yb[:, :]
                    nc.vector.tensor_tensor(into[:, it.b, :], into[:, it.b, :], y, ALU.add)\
                        .then_inc(c.x_added.sem, 1)

                def body(i):
                    for step in range(pipe.span):
                        it = pipe.item(i, step, "y")
                        if not it.missing and it.last and it.g == groups - 1:
                            residual(it)
                        it = pipe.item(i, step, "pv")
                        if not it.missing and it.last:
                            output(it)
                        it = pipe.item(i, step, "s")
                        if not it.missing:
                            exponents(it)
                        it = pipe.item(i, step, "qkv")
                        if not it.missing and it.first:
                            projected(it)
                        it = pipe.item(i, step, "xn")
                        if not it.missing and it.first and it.g == 0:
                            if rotary:
                                rotate(nc.vector, chain, 1, it)
                            else:
                                normalised(it)

                pipe.run(dve, body, chain, pipe.sequences * vector_steps)

            @block.gpsimd
            def _(pool):
                chain = Chain(pool, c.chain_p, 0)

                def context(it):
                    pool.wait_ge(c.v_ps.sem, c.v_ps.at(it.b * groups))
                    nc.gpsimd.tensor_copy(kv_src[:, :, :], token_tile(c.ctxT, it.b)).then_inc(c.ctx_ready.sem, 1)

                def masked(it):
                    if it.first:
                        pool.wait_ge(c.k_ready.sem, c.k_ready.at(it.n + 1))
                    pool.wait_ge(c.s_ps.sem, c.s_ps.at(it.m - NK + 1))
                    src, dst = k[it.group_at % 2], km[it.at % NK]
                    if dh == 16:
                        j, h0 = it.t // 2, 4 * (it.t % 2)
                        last = nc.gpsimd.tensor_tensor(
                            dst[:, :, :], src[:, j, :].unsqueeze(1).to_broadcast([P, 4, S]),
                            hm[:, h0:h0 + 4].unsqueeze(2).to_broadcast([P, 4, S]), ALU.mult)
                    else:
                        for j in range(KD):
                            last = nc.gpsimd.tensor_tensor(
                                dst[:, 2 * j:2 * j + 2, :], src[:, j, :].unsqueeze(1).to_broadcast([P, 2, S]),
                                hm[:, 0:2].unsqueeze(2).to_broadcast([P, 2, S]), ALU.mult)
                    last.then_inc(c.km_ready.sem, 1)

                def body(i):
                    for step in range(pipe.span):
                        it = pipe.item(i, step, "qkv")
                        if not it.missing:
                            masked(it)
                        it = pipe.item(i, step, "x")
                        if ctx_kv and not it.missing and it.first and it.g == 0:
                            context(it)
                        it = pipe.item(i, step, "xn")
                        if rotary and not it.missing and it.first and it.g == 0:
                            rotate(nc.gpsimd, chain, 0, it)

                pipe.run(pool, body, chain, 0 if own else 4 * pipe.sequences)

            @block.scalar
            def _(act):
                def normalised(it):
                    act.wait_ge(c.xt_ps.sem, c.xt_ps.at(it.b + 1))
                    act.wait_ge(c.v_ps.sem, c.v_ps.at(it.b * groups))
                    for j in range(KD):
                        src = bank_m[:, j * S:(j + 1) * S]
                        if norm_w is not None:
                            last = nc.scalar.activation(xT[:, j, :], src, ACT.Identity, scale=norm_w[:, j:j + 1])
                        elif j == 0:
                            last = nc.scalar.copy(xT[:, :, :], bank_m[:, 0:D].rearrange("p (j t) -> p j t", j=KD))
                    last.then_inc(c.xT_ready.sem, 1)

                def projected(it):
                    act.wait_ge(c.k_ps.sem, c.k_ps.at(it.n + 1))
                    act.wait_ge(c.km_ready.sem, c.km_ready.at((it.n - 1) * quads))
                    dst = k[it.group_at % 2]
                    for j in range(KD):
                        src = bank_m[:, j * S:(j + 1) * S]
                        if k_bias is not None:
                            last = nc.scalar.activation(dst[:, j, :], src, ACT.Identity, bias=k_bias[:, j:j + 1])
                        elif j == 0:
                            last = nc.scalar.copy(dst[:, :, :], bank_m[:, 0:D].rearrange("p (j t) -> p j t", j=KD))
                    last.then_inc(c.k_ready.sem, 1)

                def exponentials(it):
                    par = it.at % 2
                    act.wait_ge(c.e_ready.sem, c.e_ready.at(it.m + 1))
                    act.wait_ge(c.pt_ps.sem, c.pt_ps.at(it.m - 1))
                    if it.g == lin_group:
                        nc.scalar.activation(Pr[par][:, :, :], E[par][:, :, :], ACT.Square, bias=c.one[:, :],
                                             scale=0.5).then_inc(c.p_ready.sem, 1)
                    else:
                        nc.scalar.activation(Pr[par][:, :, :], E[par][:, :, :], ACT.Exp).then_inc(c.p_ready.sem, 1)

                def transposed(it):
                    par = it.at % 2
                    act.wait_ge(c.pt_ps.sem, c.pt_ps.at(it.m + 1))
                    act.wait_ge(c.pv_done.sem, c.pv_done.at(it.m - 1))
                    nc.scalar.copy(PT[par][:, :, :], bank_t[par][:, :].rearrange("p (h q) -> p h q", h=4))\
                        .then_inc(c.pT_ready.sem, 1)

                def output(it):
                    act.wait_ge(c.ot_ps.sem, c.ot_ps.at(it.n + 1))
                    act.wait_ge(c.y_ps.sem, c.y_ps.at(it.n))
                    nc.scalar.copy(oT[:, :, :], bank_m[:, 0:D].rearrange("p (j q) -> p j q", j=KD))\
                        .then_inc(c.oT_ready.sem, 1)

                def body(i):
                    for step in range(pipe.span):
                        it = pipe.item(i, step, "ot")
                        if not it.missing and it.last:
                            output(it)
                        if lags["e"] > lags["s"]:
                            it = pipe.item(i, step, "e")
                            if not it.missing:
                                exponentials(it)
                        it = pipe.item(i, step, "t")
                        if not it.missing:
                            transposed(it)
                        it = pipe.item(i, step, "qkv")
                        if not it.missing and it.first:
                            projected(it)
                        it = pipe.item(i, step, "x")
                        if own and not it.missing and it.first and it.g == 0:
                            normalised(it)
                        if lags["e"] == lags["s"]:
                            it = pipe.item(i, step, "e")
                            if not it.missing:
                                exponentials(it)

                pipe.run(act, body)

            @block.tensor
            def _(pe):
                def normalised(it):
                    pe.wait_ge(c.xn_ready.sem, c.xn_ready.at(it.b + 1))
                    for j in range(KD):
                        last = nc.tensor.transpose(bank_m[:, j * S:(j + 1) * S], xn[:, j * P:(j + 1) * P],
                                                   c.ident[:, :])
                    last.then_inc(c.xt_ps.sem, 1)

                def bank_m_free(oT, k, xT):
                    pe.wait_ge(c.oT_ready.sem, c.oT_ready.at(oT))
                    pe.wait_ge(c.k_ready.sem, c.k_ready.at(k))
                    if own:
                        pe.wait_ge(c.xT_ready.sem, c.xT_ready.at(xT))

                def projected(it):
                    if rotary and it.g == 0:
                        pe.wait_ge(c.xn_ready.sem, c.xn_ready.at(2 * (it.b + 1)))
                    if ctx_kv:
                        pe.wait_ge(c.ctx_ready.sem, c.ctx_ready.at(it.b + 1))
                    if rotary:
                        q_rot, k_rot = (rotated[a][it.at // T % 2][:, :, :].rearrange("p h d -> p (h d)") for a in range(2))
                        for j in range(KD):
                            col = it.g * D + j * P
                            last = nc.tensor.transpose(bank_m[:, j * S:(j + 1) * S], k_rot[:, col:col + P],
                                                       c.ident[:, :])
                        last.then_inc(c.k_ps.sem, 1)
                        pe.wait_ge(c.q_ready.sem, c.q_ready.at(it.n))
                        for j in range(KD):
                            col = it.g * D + j * P
                            last = nc.tensor.transpose(bank_v[:, D + j * S:D + (j + 1) * S],
                                                       q_rot[:, col:col + P], c.ident[:, :])
                        last.then_inc(c.v_ps.sem, 1)
                        return
                    for j in range(KD):
                        for kd in range(KD):
                            last = nc.tensor.matmul(bank_m[:, j * S:(j + 1) * S],
                                                    wk[:, kd, it.g * D + j * P:it.g * D + (j + 1) * P],
                                                    kv_src[:, kd, :], start=kd == 0, stop=kd == KD - 1)
                    last.then_inc(c.k_ps.sem, 1)
                    pe.wait_ge(c.v_ready.sem, c.v_ready.at(it.n))
                    for j in range(KD):
                        for kd in range(KD):
                            nc.tensor.matmul(bank_v[:, D + j * S:D + (j + 1) * S],
                                             wq[:, kd, it.g * D + j * P:it.g * D + (j + 1) * P],
                                             xT[:, kd, :], start=kd == 0, stop=kd == KD - 1)
                    for kd in range(KD):
                        last = nc.tensor.matmul(bank_v[:, 0:D], kv_src[:, kd, :],
                                                wv[:, kd, it.g * D:(it.g + 1) * D],
                                                start=kd == 0, stop=kd == KD - 1)
                    last.then_inc(c.v_ps.sem, 1)

                def scores(it):
                    if it.first:
                        pe.wait_ge(c.q_ready.sem, c.q_ready.at(it.n + 1))
                    pe.wait_ge(c.km_ready.sem, c.km_ready.at(it.m + 1))
                    pe.wait_ge(c.e_ready.sem, c.e_ready.at(it.m - 1))
                    s = bank_s[it.at % 2]
                    qs, ks = q[it.group_at % 2], km[it.at % NK]
                    if dh == 16:
                        last = nc.tensor.matmul(s[:, :], qs[:, it.t // 2, :], ks[:, :, :].rearrange("p h k -> p (h k)"),
                                                start=True, stop=True)
                    else:
                        for j in range(KD):
                            last = nc.tensor.matmul(s[:, j * D:(j + 1) * D], qs[:, j, :],
                                                    ks[:, 2 * j:2 * j + 2, :].rearrange("p h k -> p (h k)"),
                                                    start=True, stop=True)
                    last.then_inc(c.s_ps.sem, 1)

                def transposes(it):
                    par = it.at % 2
                    pe.wait_ge(c.p_ready.sem, c.p_ready.at(it.m + 1))
                    pe.wait_ge(c.pT_ready.sem, c.pT_ready.at(it.m - 1))
                    for h in range(4):
                        last = nc.tensor.transpose(bank_t[par][:, h * S:(h + 1) * S], Pr[par][:, h, :],
                                                   c.ident[:, :])
                    last.then_inc(c.pt_ps.sem, 1)

                def values(it):
                    par = it.at % 2
                    if it.first and own:
                        pe.wait_ge(c.v_ready.sem, c.v_ready.at(it.n + 1))
                    if it.first:
                        pe.wait_ge(c.o_ready.sem, c.o_ready.at(it.n))
                    pe.wait_ge(c.pT_ready.sem, c.pT_ready.at(it.m + 1))
                    for h in range(4):
                        hh = 4 * it.t + h
                        vh = v[it.group_at % NV][:, hh, :] if own else rotary.V[:, it.b, it.g * H + hh, :]
                        last = nc.tensor.matmul(bank_o[:, hh * (dh + 1):(hh + 1) * (dh + 1)], PT[par][:, h, :], vh,
                                                start=True, stop=True)
                    last.then_inc(c.pv_done.sem, 1)

                def output(it):
                    pe.wait_ge(c.o_ready.sem, c.o_ready.at(it.n + 1))
                    for j in range(KD):
                        last = nc.tensor.transpose(bank_m[:, j * S:(j + 1) * S], o[:, j * P:(j + 1) * P],
                                                   c.ident[:, :])
                    last.then_inc(c.ot_ps.sem, 1)

                def projection(it):
                    pe.wait_ge(c.oT_ready.sem, c.oT_ready.at(it.n + 1))
                    if it.g == 0:
                        pe.wait_ge(c.x_added.sem, c.x_added.at(it.b))
                    for j in range(KD):
                        last = nc.tensor.matmul(bank_y[:, 0:D], oT[:, j, :], wo[:, it.g * KD + j, :],
                                                start=(it.g == 0 and j == 0),
                                                stop=(it.g == groups - 1 and j == KD - 1))
                    last.then_inc(c.y_ps.sem, 1)

                def body(i):
                    for step in range(pipe.span):
                        ot, qkv, x = (pipe.item(i, step, n) for n in ("ot", "qkv", "x"))
                        outs = lambda k: pipe.issued(i, k, "ot", quads, False)
                        ks = lambda k: pipe.issued(i, k, "qkv", quads, True)
                        xs = lambda k: pipe.issued(i, k, "x", T, True)
                        it = pipe.item(i, step, "y")
                        if not it.missing and it.last:
                            projection(it)
                        if not ot.missing and ot.last:
                            bank_m_free(outs(step), ks(step), xs(step))
                            output(ot)
                        it = pipe.item(i, step, "pv")
                        if not it.missing:
                            values(it)
                        it = pipe.item(i, step, "t")
                        if not it.missing:
                            transposes(it)
                        it = pipe.item(i, step, "s")
                        if not it.missing:
                            scores(it)
                        if not qkv.missing and qkv.first:
                            bank_m_free(outs(step + 1), ks(step), xs(step))
                            projected(qkv)
                        if own and not x.missing and x.first and x.g == 0:
                            bank_m_free(outs(step + 1), ks(step + 1), xs(step))
                            normalised(x)

                pipe.run(pe, body)

    c.passed(v_set=own, chain_v=B * vector_steps, chain_p=0 if own else 4 * B, xn_ready=B if own else 2 * B,
             xt_ps=B * own, xT_ready=B * own, ctx_ready=B * ctx_kv,
             k_ps=B * groups, q_ready=B * groups, k_ready=B * groups, v_ps=B * groups, v_ready=B * groups * own,
             km_ready=B * T, s_ps=B * T, e_ready=B * T, p_ready=B * T, pt_ps=B * T, pT_ready=B * T, pv_done=B * T,
             o_ready=B * groups, ot_ps=B * groups, oT_ready=B * groups, y_ps=B * groups, x_added=B)


def per_head(ap):
    return ap.unsqueeze(1).to_broadcast([P, 4, S])


def no_mask(g, t, i):
    return None, None


def l0_attn(c, w):
    with ExitStack() as ctx:
        wqkv = c.sb(ctx, "l0a_wqkv", [P, KD, 3072])
        wo = c.sb(ctx, "l0a_wo", [P, 8, D])
        load(c, [(wqkv[:, :, :], w["L0_attn_W_qkv"]), (wo[:, :, :], w["L0_attn_W_out"])])
        layernorm_stats(c, [c.x])
        attention(c, "l0a", 4, 1, 64, (wqkv[:, :, 0:1024], wqkv[:, :, 1024:2048], wqkv[:, :, 2048:3072], wo),
                  q_scale=[0.125] * 4, mask_of=lambda g, t, i: (None, per_head(c.causal_add[:, :])))


def l0_xattn(c, w):
    with ExitStack() as ctx:
        wq = c.sb(ctx, "l0x_wq", [P, KD, 1024])
        wkv = c.sb(ctx, "l0x_wkv", [P, KD, 2048])
        wo = c.sb(ctx, "l0x_wo", [P, 8, D])
        bo = c.sb(ctx, "l0x_bo", [P, D])
        load(c, [(wq[:, :, :], w["L0_xattn_Wq"]), (wkv[:, :, :], w["L0_xattn_Wkv"]),
                 (wo[:, :, :], w["L0_xattn_Wout"]), (bo[:, :], w["L0_xattn_bout"])])
        layernorm_stats(c, [c.x])
        attention(c, "l0x", 4, 1, 64, (wq, wkv[:, :, 0:1024], wkv[:, :, 1024:2048], wo), ctx_kv=True,
                  q_scale=[0.125] * 4, y_bias=bo, mask_of=no_mask)


def xattn_masked(c, w, name, mask, fill, names):
    q, qb, k, kb, v, vb, o, ob = names
    with ExitStack() as ctx:
        ws = [c.sb(ctx, f"{name}_w{i}", [P, KD, D]) for i in range(4)]
        qkb = [c.sb(ctx, f"{name}_b{i}", [P, KD]) for i in range(2)]
        vob = [c.sb(ctx, f"{name}_bb{i}", [P, D]) for i in range(2)]
        mi = c.sb(ctx, f"{name}_mi", [P, B, S], I32)
        keep = c.sb(ctx, f"{name}_keep", [P, B, S])
        put = c.sb(ctx, f"{name}_put", [P, B, S])
        load(c, [(ws[0][:, :, :], w[q]), (ws[1][:, :, :], w[k]), (ws[2][:, :, :], w[v]), (ws[3][:, :, :], w[o]),
                 (qkb[0][:, :], w[qb]), (qkb[1][:, :], w[kb]), (vob[0][:, :], w[vb]), (vob[1][:, :], w[ob]),
                 (mi[:, :, :], w[mask])])
        layernorm_stats(c, [c.x])
        with c.nc.Block() as block:
            @block.vector
            def _(dve):
                chain = Chain(dve, c.chain_v, 0)
                chain(c.nc.vector.tensor_scalar(keep[:, :, :], mi[:, :, :], 0.0, None, ALU.not_equal))
                chain(c.nc.vector.tensor_scalar(put[:, :, :], keep[:, :, :], -fill, fill, ALU.mult, ALU.add))
        c.passed(chain_v=2)
        attention(c, name, 1, 4, 16, ws, ctx_kv=True, q_scale=[0.25], q_bias=qkb[0], k_bias=qkb[1], v_bias=vob[0],
                  y_bias=vob[1], mask_of=lambda g, t, i: (per_head(keep[:, i, :]), per_head(put[:, i, :])))


def l1_xattn(c, w):
    n = "L1_xattn_W"
    xattn_masked(c, w, "l1x", "mask_Bx1xSxS2_ik1", 1e-9,
                 [n + "Q_w", n + "Q_b", n + "K_w", n + "K_b", n + "V_w", n + "V_b", n + "O_w", n + "O_b"])


def l3_xattn(c, w):
    n = "L3_xattn_"
    xattn_masked(c, w, "l3x", "mask_BxSxS2_if1", -1e9,
                 [n + "Wq", n + "bq", n + "Wk", n + "bk", n + "Wv", n + "bv", n + "Wo", n + "bo"])


def l2_xattn(c, w):
    with ExitStack() as ctx:
        ws = [c.sb(ctx, f"l2x_w{i}", [P, KD, D]) for i in range(4)]
        load(c, [(ws[i][:, :, :], w["L2_xattn_W" + n]) for i, n in enumerate("qkvo")])
        layernorm_stats(c, [c.x])
        attention(c, "l2x", 1, 4, 16, ws, ctx_kv=True, q_scale=[0.25], mask_of=no_mask)


def l3_attn(c, w):
    with ExitStack() as ctx:
        ws = [c.sb(ctx, f"l3a_w{i}", [P, KD, D]) for i in range(4)]
        qkb = [c.sb(ctx, f"l3a_b{i}", [P, KD]) for i in range(2)]
        vob = [c.sb(ctx, f"l3a_bb{i}", [P, D]) for i in range(2)]
        alibi = c.sb(ctx, "l3a_alibi", [P, 16, S])
        n = "L3_attn_"
        load(c, [(ws[i][:, :, :], w[n + "W" + m]) for i, m in enumerate("qkvo")]
             + [(qkb[0][:, :], w[n + "bq"]), (qkb[1][:, :], w[n + "bk"]), (vob[0][:, :], w[n + "bv"]),
                (vob[1][:, :], w[n + "bo"]), (alibi[:, :, :], w["alibi"])])
        layernorm_stats(c, [c.x])
        attention(c, "l3a", 1, 4, 16, ws, q_scale=[0.25], q_bias=qkb[0], k_bias=qkb[1], v_bias=vob[0],
                  y_bias=vob[1], mask_of=lambda g, t, i: (None, alibi[:, 4 * t:4 * t + 4, :]))


def l1_attn(c, w):
    nc = c.nc
    with ExitStack() as ctx:
        wq, wk, wv = (c.sb(ctx, f"l1a_w{n}", [P, KD, 2 * D]) for n in "qkv")
        wo = c.sb(ctx, "l1a_wo", [P, 4, D])
        wT = c.sb(ctx, "l1a_wT", [P, 2, KD, D])
        feat = c.sb(ctx, "l1a_feat", [P, 2, KD, D])
        norm_w = c.sb(ctx, "l1a_norm", [P, KD])
        xin = c.sb(ctx, "l1a_xin", [P, B, D])
        causal, c2, window = (c.sb(ctx, f"l1a_m{i}", [P, S]) for i in range(3))
        a = "L1_attn_"
        load(c, [(wq[:, :, D:], w[a + "Wq"]), (wk[:, :, D:], w[a + "Wk"]), (wv[:, :, 0:D], w[a + "Wv"]),
                 (wv[:, :, D:], w[a + "Wv"]), (wo[:, :, :], w[a + "Wout"]), (wT[:, 0, :, :], w[a + "WqT"]),
                 (wT[:, 1, :, :], w[a + "WkT"]), (feat[:, 0, :, :], w[a + "Wqf"]), (feat[:, 1, :, :], w[a + "Wkf"]),
                 (norm_w[:, :], w[a + "norm_w"]), (causal[:, :], w["causal"]), (c2[:, :], w["causal_minus2"]),
                 (window[:, :], w["window_add"])])
        layernorm_stats(c, [c.x])
        with nc.Block() as block:
            @block.tensor
            def _(pe):
                for a in range(2):
                    for j in range(KD):
                        for m in range(KD):
                            last = nc.tensor.matmul(c.bank[a][:, j * D:(j + 1) * D], wT[:, a, m, j * P:(j + 1) * P],
                                                    feat[:, a, m, :], start=m == 0, stop=m == KD - 1)
                    last.then_inc(c.h_ps.sem, 1)

            @block.scalar
            def _(act):
                for a, dst in enumerate((wq, wk)):
                    act.wait_ge(c.h_ps.sem, c.h_ps.at(a + 1))
                    nc.scalar.copy(dst[:, :, 0:D], c.bank[a][:, :].rearrange("p (j n) -> p j n", j=KD))

            @block.vector
            def _(dve):
                with dve.Fori(0, B) as i:
                    nc.vector.tensor_scalar(xin[:, i, :], c.x[:, i, :], c.mv[:, i, 0:1], c.rstd[:, bass.ds(i, 1)],
                                            ALU.subtract, ALU.mult)
        c.passed(h_ps=2)
        layernorm_stats(c, [c.x], rms_eps=1e-6)
        attention(c, "l1a", 2, 4, 16, (wq, wk, wv, wo), norm_w=norm_w, q_scale=[1.0, 0.25], lin_group=0, xin=xin,
                  mask_of=lambda g, t, i: ((per_head(causal[:, :]), per_head(c2[:, :])) if g == 0
                                           else (None, per_head(window[:, :]))))


def first_largest(nc, chain, vals, rev, mx, tmp, mask):
    bc = mx.unsqueeze(2).to_broadcast(list(vals.shape))
    chain(nc.vector.tensor_reduce(mx, vals, AX.X, ALU.max))
    chain(nc.vector.tensor_tensor(tmp, vals, bc, ALU.is_equal))
    chain(nc.vector.tensor_tensor(tmp, tmp, rev, ALU.mult))
    chain(nc.vector.tensor_reduce(mx, tmp, AX.X, ALU.max))
    chain(nc.vector.tensor_tensor(mask, tmp, bc, ALU.is_equal))


def route(c, name, E, wg, *, xnT=None, comb=None, dispatch=None, g_bias=None, hidden=None, renorm_eps=None,
          capacity=None):
    nc = c.nc
    layernorm_stats(c, [c.x])
    with ExitStack() as ctx:
        sb = lambda n, shape: c.sb(ctx, f"{name}_r_{n}", shape)
        xn, xT = sb("xn", [P, D]), sb("xT", [P, KD, S])
        lg, pr, tmp, m1, m2 = (sb(n, [P, B, E]) for n in ("lg", "pr", "tmp", "m1", "m2"))
        before, place = sb("before", [P, 3, B + 1, E]), sb("place", [P, B, E])
        if dispatch:
            both, ge = sb("both", [P, B, E]), sb("ge", [P, E, dispatch.most])
            each = [sb(f"each{i}", [P, E]) for i in range(3)]
            limits, slot = sb("limits", [P, dispatch.most]), sb("slot", [P, B])
        r = [sb(f"r{i}", [P, B]) for i in range(3)]
        rev = sb("rev", [P, E])
        bg = sb("bg", [P, E])
        hT = sb("hT", [64, S]) if hidden else None
        load(c, [(rev[:, :], c.w[f"rev{E}"])] + ([(limits[:, :], c.w["block_limits"])] if dispatch else []) + ([(bg[:, :], g_bias)] if g_bias is not None else []))
        bank_x, bank_l, bank_h = c.bank[0], c.bank[1], c.bank[2]
        with nc.Block() as block:
            @block.vector
            def _(dve):
                with dve.Fori(0, B) as i:
                    dve.wait_ge(c.xt_ps.sem, c.xt_ps.at(i))
                    nc.vector.tensor_scalar(xn[:, :], c.x[:, i, :], c.mv[:, i, 0:1], c.rstd[:, bass.ds(i, 1)],
                                            ALU.subtract, ALU.mult).then_inc(c.xn_ready.sem, 1)
                    if dispatch:
                        nc.vector.tensor_scalar(dispatch.xn[:, i, :], c.x[:, i, :], c.mv[:, i, 0:1],
                                                c.rstd[:, bass.ds(i, 1)], ALU.subtract, ALU.mult)
                    dve.wait_ge(c.l_ps.sem, c.l_ps.at(i + 1))
                    nc.vector.tensor_copy(lg[:, i, :], bank_l[:, 0:E]).then_inc(c.l_ready.sem, 1)

            @block.tensor
            def _(pe):
                with pe.Fori(0, B) as i:
                    pe.wait_ge(c.xn_ready.sem, c.xn_ready.at(i + 1))
                    for j in range(KD):
                        last = nc.tensor.transpose(bank_x[:, j * S:(j + 1) * S], xn[:, j * P:(j + 1) * P],
                                                   c.ident[:, :])
                    last.then_inc(c.xt_ps.sem, 1)
                    pe.wait_ge(c.xT_ready.sem, c.xT_ready.at(i + 1))
                    if hidden:
                        pe.wait_ge(c.h_ready.sem, c.h_ready.at(i))
                        for j in range(KD):
                            last = nc.tensor.matmul(bank_h[0:64, 0:S], hidden[0][:, j, :], xT[:, j, :],
                                                    start=j == 0, stop=j == KD - 1)
                        last.then_inc(c.h_ps.sem, 1)
                        pe.wait_ge(c.h_ready.sem, c.h_ready.at(i + 1))
                    pe.wait_ge(c.l_ready.sem, c.l_ready.at(i))
                    if hidden:
                        last = nc.tensor.matmul(bank_l[:, 0:E], hT[:, :], wg[:, 0:E], start=True, stop=True)
                    else:
                        for j in range(KD):
                            last = nc.tensor.matmul(bank_l[:, 0:E], xT[:, j, :], wg[:, j, :],
                                                    start=j == 0, stop=j == KD - 1)
                    last.then_inc(c.l_ps.sem, 1)

            @block.scalar
            def _(act):
                with act.Fori(0, B) as i:
                    act.wait_ge(c.xt_ps.sem, c.xt_ps.at(i + 1))
                    act.wait_ge(c.l_ps.sem, c.l_ps.at(i))
                    src = bank_x[:, 0:D].rearrange("p (j t) -> p j t", j=KD)
                    if xnT is not None:
                        nc.scalar.copy(token_tile(xnT, i), src)
                    nc.scalar.copy(xT[:, :, :], src).then_inc(c.xT_ready.sem, 1)
                    if hidden:
                        act.wait_ge(c.h_ps.sem, c.h_ps.at(i + 1))
                        nc.scalar.activation(hT[:, :], bank_h[0:64, 0:S], ACT.Gelu, bias=hidden[1][:, 0:1])\
                            .then_inc(c.h_ready.sem, 1)
        c.passed(xn_ready=B, xt_ps=B, xT_ready=B, l_ps=B, l_ready=B, h_ps=B * bool(hidden), h_ready=B * bool(hidden))

        steps = [0]
        full = lambda a: a.unsqueeze(2).to_broadcast([P, B, E])
        with nc.Block() as block:
            @block.vector
            def _(dve):
                chain = Chain(dve, c.chain_v, 0)
                v = nc.vector
                L, Q, W, M1, M2 = (a[:, :, :] for a in (lg, pr, tmp, m1, m2))
                R = [a[:, :] for a in r]
                rv = rev[:, :].unsqueeze(1).to_broadcast([P, B, E])
                if g_bias is not None:
                    chain(v.tensor_tensor(L, L, bg[:, :].unsqueeze(1).to_broadcast([P, B, E]), ALU.add))
                chain(v.tensor_reduce(R[0], L, AX.X, ALU.max))
                v.tensor_tensor(Q, L, full(R[0]), ALU.subtract).then_inc(c.e_ready.sem, 1)
                dve.wait_ge(c.p_ready.sem, c.p_ready.at(1))
                chain(v.tensor_reduce(R[0], Q, AX.X, ALU.add))
                chain(v.reciprocal(R[1], R[0]))
                chain(v.tensor_tensor(Q, Q, full(R[1]), ALU.mult))
                vals = L if capacity else Q
                first_largest(nc, chain, vals, rv, R[0], W, M1)
                chain(v.scalar_tensor_tensor(out=L, in0=M1, scalar=NEG if capacity else -4.0, in1=vals,
                                             op0=ALU.mult, op1=ALU.add))
                first_largest(nc, chain, L, rv, R[0], W, M2)
                if renorm_eps is not None:
                    chain(v.tensor_tensor(W, M1, M2, ALU.add))
                    chain(v.tensor_tensor(W, W, Q, ALU.mult))
                    chain(v.tensor_reduce(R[0], W, AX.X, ALU.add))
                    chain(v.tensor_scalar(R[0], R[0], renorm_eps, None, ALU.add))
                    chain(v.reciprocal(R[1], R[0]))
                    chain(v.tensor_tensor(Q, Q, full(R[1]), ALU.mult))
                sets = [None, M1, M2]
                used = ([0] if dispatch else []) + ([1, 2] if capacity else [])
                if dispatch:
                    sets[0] = both[:, :, :]
                    chain(v.tensor_tensor(sets[0], M1, M2, ALU.add))
                if used:
                    chain(v.memset(before[:, :, 0, :], 0.0))
                    v.tensor_copy(W, M1).then_inc(c.a_ready.sem, 1)
                    dve.wait_ge(c.c_ps.sem, c.c_ps.at(1))
                    dve.wait_ge(c.a_ready.sem, c.a_ready.at(1))
                    for a in used:
                        tot = c.bank[5 + a][:, 0:B * E].rearrange("p (b e) -> p b e", b=B)
                        if a == 2:
                            chain(v.tensor_copy(before[:, 2, 0, :], before[:, 1, B, :]))
                        for b in range(B):
                            chain(v.tensor_tensor(before[:, a, b + 1, :], before[:, a, b, :], tot[:, b, :], ALU.add))
                if dispatch:
                    count, blocks, start = before[:, 0, B, :], each[0][:, :], each[1][:, :]
                    chain(v.tensor_tensor(ge[:, :, :], count.unsqueeze(2).to_broadcast([P, E, dispatch.most]),
                                          limits[:, :].unsqueeze(1).to_broadcast([P, E, dispatch.most]), ALU.is_gt))
                    chain(v.tensor_reduce(blocks, ge[:, :, :], AX.X, ALU.add))
                    chain(v.memset(each[2][:, :], 1.0))
                    chain(v.tensor_tensor_scan(start, each[2][:, :], blocks, 0.0, ALU.mult, ALU.add))
                    chain(v.tensor_tensor(start, start, blocks, ALU.subtract))
                    chain(v.tensor_copy(dispatch.blocks[:, 0, :], blocks))
                    chain(v.tensor_copy(dispatch.blocks[:, 1, :], start))
                    chain(v.tensor_scalar(start, start, float(dispatch.width), None, ALU.mult))
                    within = c.bank[2][:, 0:B * E].rearrange("p (b e) -> p b e", b=B)
                    chain(v.tensor_tensor(place[:, :, :], within, before[:, 0, 0:B, :], ALU.add))
                    chain(v.tensor_tensor(place[:, :, :], place[:, :, :],
                                          start.unsqueeze(1).to_broadcast([P, B, E]), ALU.add))
                    for a, M in enumerate((M1, M2)):
                        chain(v.tensor_tensor(W, place[:, :, :], M, ALU.mult))
                        chain(v.tensor_reduce(slot[:, :], W, AX.X, ALU.add))
                        chain(v.tensor_copy(dispatch.slot[:, a, :], slot[:, :]))
                if capacity:
                    for a, M in ((1, M1), (2, M2)):
                        within = c.bank[2 + a][:, 0:B * E].rearrange("p (b e) -> p b e", b=B)
                        chain(v.tensor_tensor(place[:, :, :], within, before[:, a, 0:B, :], ALU.add))
                        chain(v.tensor_scalar(place[:, :, :], place[:, :, :], float(capacity), None, ALU.is_lt))
                        chain(v.tensor_tensor(M, M, place[:, :, :], ALU.mult))
                if dispatch:
                    for a, M in enumerate((M1, M2)):
                        chain(v.tensor_tensor(W, Q, M, ALU.mult))
                        chain(v.tensor_reduce(dispatch.weight[:, a, :], W, AX.X, ALU.add))
                else:
                    chain(v.tensor_tensor(W, M1, M2, ALU.add))
                    chain(v.tensor_tensor(comb[:, :, :], Q, W, ALU.mult))
                steps[0] = chain.n

            @block.scalar
            def _(act):
                act.wait_ge(c.e_ready.sem, c.e_ready.at(1))
                nc.scalar.activation(pr[:, :, :], pr[:, :, :], ACT.Exp).then_inc(c.p_ready.sem, 1)

            counted = bool(capacity or dispatch)
            if counted:
                @block.tensor
                def _(pe):
                    pe.wait_ge(c.a_ready.sem, c.a_ready.at(1))
                    for a, m in ([(0, both)] if dispatch else []) + ([(1, m1), (2, m2)] if capacity else []):
                        flat = m[:, :, :].rearrange("p b e -> p (b e)")
                        nc.tensor.matmul(c.bank[2 + a][:, 0:B * E], c.earlier[:, :], flat, start=True, stop=True)
                        last = nc.tensor.matmul(c.bank[5 + a][:, 0:B * E], c.ones[:, :], flat, start=True, stop=True)
                    last.then_inc(c.c_ps.sem, 1)
        c.passed(e_ready=1, p_ready=1, chain_v=steps[0], a_ready=counted, c_ps=counted)


def add_output_bias(c, name, E, comb, bias):
    nc = c.nc
    with ExitStack() as ctx:
        cs, cT = c.sb(ctx, f"{name}_cs", [P, E]), c.sb(ctx, f"{name}_cT", [E, S])
        b2 = c.sb(ctx, f"{name}_b2", [E, D])
        load(c, [(b2[:, :], bias)])
        with nc.Block() as block:
            @block.gpsimd
            def _(pool):
                with pool.Fori(0, B) as i:
                    pool.wait_ge(c.cT_ps.sem, c.cT_ps.at(i))
                    nc.gpsimd.tensor_copy(cs[:, :], comb[:, i, :]).then_inc(c.comb_ready.sem, 1)

            @block.tensor
            def _(pe):
                with pe.Fori(0, B) as i:
                    pe.wait_ge(c.comb_ready.sem, c.comb_ready.at(i + 1))
                    nc.tensor.transpose(c.bank[0][0:E, 0:S], cs[:, :], c.ident[:, :]).then_inc(c.cT_ps.sem, 1)
                    pe.wait_ge(c.cT_ready.sem, c.cT_ready.at(i + 1))
                    pe.wait_ge(c.x_added.sem, c.x_added.at(i))
                    nc.tensor.matmul(c.bank[1][:, 0:D], cT[:, :], b2[:, :], start=True, stop=True)\
                        .then_inc(c.y_ps.sem, 1)

            @block.scalar
            def _(act):
                with act.Fori(0, B) as i:
                    act.wait_ge(c.cT_ps.sem, c.cT_ps.at(i + 1))
                    act.wait_ge(c.y_ps.sem, c.y_ps.at(i))
                    nc.scalar.copy(cT[:, :], c.bank[0][0:E, 0:S]).then_inc(c.cT_ready.sem, 1)

            @block.vector
            def _(dve):
                with dve.Fori(0, B) as i:
                    dve.wait_ge(c.y_ps.sem, c.y_ps.at(i + 1))
                    nc.vector.tensor_tensor(c.x[:, i, :], c.x[:, i, :], c.bank[1][:, 0:D], ALU.add)\
                        .then_inc(c.x_added.sem, 1)
    c.passed(comb_ready=B, cT_ps=B, cT_ready=B, y_ps=B, x_added=B)


class Dispatch:

    def __init__(self, c, ctx, name):
        sb = lambda n, shape, dt=F32: c.sb(ctx, f"{name}_{n}", shape, dt)
        self.width, self.most = WIDTH, MOST
        self.xn = sb("xnat", [P, B, D])
        self.slot, self.weight = sb("slots", [P, 2, B], I32), sb("weights", [P, 2, B])
        self.blocks = sb("blocks", [P, 2, 8], I32)


def expert_mlps(c, name, w, gelu, capacity, renorm_eps, g_bias):
    nc, E, F = c.nc, 8, 1024
    FC = F // P
    TT = WIDTH // P
    with ExitStack() as ctx:
        sb = lambda n, shape: c.sb(ctx, f"{name}_{n}", shape)
        wg, b1, b2 = sb("wg", [P, KD, E]), sb("b1", [P, E, FC]), sb("b2", [P, E, D])
        d = Dispatch(c, ctx, name)
        w1 = [sb(f"w1_{i}", [P, KD, F]) for i in range(2)]
        w2 = [sb(f"w2_{i}", [P, FC, D]) for i in range(2)]
        xs, xT = sb("xs", [P, TT, D]), sb("xT", [P, KD, WIDTH])
        hT, ys = sb("hT", [P, FC, WIDTH]), sb("ys", [P, TT, D])
        got = [[sb(f"got{a}{i}", [P, D]) for i in range(2)] for a in range(2)]
        own = {n: Signal(ctx.enter_context(nc.semaphore(f"s_{name}_{n}")))
               for n in ("in", "xt", "xT", "hps", "h", "yps", "y", "out")}
        x_in, xt_ps, xT_ready, h_ps = own["in"], own["xt"], own["xT"], own["hps"]
        h_ready, y_ps, y_ready, y_out = own["h"], own["yps"], own["y"], own["out"]
        load(c, [(wg[:, :, :], w[name + "_Wg"]), (b1[:, :, :], w[name + "_b1"]), (b2[:, :, :], w[name + "_b2"])])
        route(c, name, E, wg, dispatch=d, g_bias=g_bias, renorm_eps=renorm_eps, capacity=capacity)
        bank_x, banks_h, banks_y = c.bank[0], c.bank[1:5], c.bank[5:7]

        def blocks_of(eng, e):
            return (eng.value_load(d.blocks[0:1, 0, e:e + 1], min_val=1, max_val=MOST),
                    eng.value_load(d.blocks[0:1, 1, e:e + 1], min_val=0, max_val=ROWS // WIDTH - 1))

        with nc.Block() as block:
            @block.sync
            def _(sp):
                for s in own.values():
                    sp.sem_inc(s.sem, START)
                for e in range(2):
                    sp.dma_start(w1[e][:, :, :], w[name + "_W1"][e]).then_inc(c.w_loaded[e].sem, 16)
                    sp.dma_start(w2[e][:, :, :], w[name + "_W2"][e]).then_inc(c.w_loaded[e].sem, 16)

            @block.gpsimd
            def _(pool):
                pool.wait_ge(c.cleared.sem, c.cleared.at(0))
                for b in range(B):
                    for a in range(2):
                        nc.gpsimd.indirect_dma_start(
                            out=c.rows_in[:, :], out_offset=bass.IndirectOffsetOnAxis(
                                ap=d.slot[:, a, b:b + 1], axis=0),
                            in_=d.xn[:, b, :], in_offset=None).then_inc(c.scattered.sem, 16)
                pool.wait_ge(c.scattered.sem, c.scattered.at(2 * B * 16))
        c.passed(scattered=2 * B * 16)

        with nc.Block() as block:
            @block.sync
            def _(sp):
                for e in range(E):
                    if e >= 2:
                        before = sp.value_load(d.blocks[0:1, 1, e - 1:e], min_val=0, max_val=ROWS // WIDTH - 1)
                        sp.wait_ge(y_ps.sem, y_ps.at(before * TT))
                        sp.dma_start(w1[e % 2][:, :, :], w[name + "_W1"][e]).then_inc(c.w_loaded[e % 2].sem, 16)
                        sp.dma_start(w2[e % 2][:, :, :], w[name + "_W2"][e]).then_inc(c.w_loaded[e % 2].sem, 16)
                    n, start = blocks_of(sp, e)
                    with sp.Fori(0, n) as j:
                        sp.wait_ge(xt_ps.sem, xt_ps.at(start + j))
                        sp.dma_start(xs[:, :, :], c.rows_in[bass.ds((start + j) * WIDTH, WIDTH), :]
                                     .rearrange("(t p) d -> p t d", p=P)).then_inc(x_in.sem, 16)

            @block.tensor
            def _(pe):
                for e in range(E):
                    n, start = blocks_of(pe, e)
                    with pe.Fori(0, n) as j:
                        k = start + j
                        pe.wait_ge(c.w_loaded[e % 2].sem, c.w_loaded[e % 2].at(32 * (e // 2) + 32))
                        pe.wait_ge(x_in.sem, x_in.at((k + 1) * 16))
                        pe.wait_ge(xT_ready.sem, xT_ready.at(k))
                        for kd in range(KD):
                            for t in range(TT):
                                last = nc.tensor.transpose(
                                    bank_x[:, kd * WIDTH + t * P:kd * WIDTH + (t + 1) * P],
                                    xs[:, t, kd * P:(kd + 1) * P], c.ident[:, :])
                        last.then_inc(xt_ps.sem, 1)
                        pe.wait_ge(xT_ready.sem, xT_ready.at(k + 1))
                        for f in range(FC):
                            pe.wait_ge(h_ready.sem, h_ready.at(k * FC + f - 3))
                            for kd in range(KD):
                                last = nc.tensor.matmul(banks_h[f % 4][:, 0:WIDTH], w1[e % 2][:, kd, f * P:(f + 1) * P],
                                                        xT[:, kd, :], start=kd == 0, stop=kd == KD - 1)
                            last.then_inc(h_ps.sem, 1)
                        for t in range(TT):
                            pe.wait_ge(y_ready.sem, y_ready.at(k * TT + t - 1))
                            for f in range(FC):
                                if t == 0:
                                    pe.wait_ge(h_ready.sem, h_ready.at(k * FC + f + 1))
                                last = nc.tensor.matmul(banks_y[t][:, 0:D], hT[:, f, t * P:(t + 1) * P],
                                                        w2[e % 2][:, f, :], start=f == 0, stop=f == FC - 1)
                            last.then_inc(y_ps.sem, 1)

            @block.scalar
            def _(act):
                for e in range(E):
                    n, start = blocks_of(act, e)
                    with act.Fori(0, n) as j:
                        k = start + j
                        act.wait_ge(xt_ps.sem, xt_ps.at(k + 1))
                        nc.scalar.copy(xT[:, :, :], bank_x[:, :].rearrange("p (k t) -> p k t", k=KD))\
                            .then_inc(xT_ready.sem, 1)
                        for f in range(FC):
                            act.wait_ge(h_ps.sem, h_ps.at(k * FC + f + 1))
                            if f == 0:
                                act.wait_ge(y_ps.sem, y_ps.at(k * TT))
                            nc.scalar.activation(hT[:, f, :], banks_h[f % 4][:, 0:WIDTH], gelu,
                                                 bias=b1[:, e, f:f + 1]).then_inc(h_ready.sem, 1)
                        act.wait_ge(y_ready.sem, y_ready.at((k + 1) * TT))
                        act.dma_start(c.rows_out[bass.ds(k * WIDTH, WIDTH), :].rearrange("(t p) d -> p t d", p=P),
                                      ys[:, :, :]).then_inc(y_out.sem, 16)

            @block.vector
            def _(dve):
                for e in range(E):
                    n, start = blocks_of(dve, e)
                    with dve.Fori(0, n) as j:
                        k = start + j
                        dve.wait_ge(y_out.sem, y_out.at(k * 16))
                        for t in range(TT):
                            dve.wait_ge(y_ps.sem, y_ps.at(k * TT + t + 1))
                            nc.vector.tensor_tensor(ys[:, t, :], banks_y[t][:, 0:D], b2[:, e, :], ALU.add)\
                                .then_inc(y_ready.sem, 1)
                for b in range(B):
                    dve.wait_ge(c.gathered[b % 2].sem, c.gathered[b % 2].at(32 * (b // 2 + 1)))
                    for a in range(2):
                        dve.wait_ge(c.x_added.sem, c.x_added.at(2 * b + a))
                        nc.vector.scalar_tensor_tensor(out=c.x[:, b, :], in0=got[a][b % 2][:, :],
                                                       scalar=d.weight[:, a, b:b + 1], in1=c.x[:, b, :],
                                                       op0=ALU.mult, op1=ALU.add).then_inc(c.x_added.sem, 1)

            @block.gpsimd
            def _(pool):
                n, start = blocks_of(pool, E - 1)
                pool.wait_ge(y_out.sem, y_out.at((start + n) * 16))
                pool.sem_inc(c.chain_p.sem, 1)
                pool.wait_ge(c.chain_p.sem, c.chain_p.at(1))
                for b in range(B):
                    pool.wait_ge(c.x_added.sem, c.x_added.at(2 * b - 2))
                    for a in range(2):
                        nc.gpsimd.indirect_dma_start(
                            out=got[a][b % 2][:, :], out_offset=None, in_=c.rows_out[:, :],
                            in_offset=bass.IndirectOffsetOnAxis(ap=d.slot[:, a, b:b + 1], axis=0))\
                            .then_inc(c.gathered[b % 2].sem, 16)

        c.passed(x_added=2 * B, chain_p=1)
        for s in c.gathered:
            s.passed(16 * B)
        for s in c.w_loaded:
            s.passed(16 * E)


def l0_ffn(c, w):
    expert_mlps(c, "L0_ffn", w, ACT.Gelu_apprx_tanh, None, 1e-8, w["L0_ffn_bg"])


def l1_ffn(c, w):
    expert_mlps(c, "L1_ffn", w, ACT.Gelu, 2 * 2 * B * S // 8, 1e-9, None)


def l2_ffn(c, w):
    nc, E = c.nc, 20
    with ExitStack() as ctx:
        sb = lambda n, shape: c.sb(ctx, f"l2f_{n}", shape)
        xnT, comb = sb("xnT", [P, KD, B * S]), sb("comb", [P, B, E])
        wg1, bg1, wg2 = sb("wg1", [P, KD, 64]), sb("bg1", [64, 1]), sb("wg2", [64, 2 * E])
        we = sb("we", [P, KD, E, D])
        xs = sb("xs", [P, KD, S])
        load(c, [(wg1[:, :, :], w["L2_ffn_wg1"]), (bg1[:, :], w["L2_ffn_bg1"]), (wg2[:, :], w["L2_ffn_wg2"]),
                 (we[:, :, :, :], w["L2_ffn_We"])])
        route(c, "l2f", E, wg2, xnT=xnT, comb=comb, g_bias=w["L2_ffn_bg2"], hidden=(wg1, bg1))
        add_output_bias(c, "l2f", E, comb, w["L2_ffn_be"])
        PAIRS = E // 2
        with nc.Block() as block:
            @block.gpsimd
            def _(pool):
                with pool.Fori(0, B) as i:
                    pool.wait_ge(c.y_ps.sem, c.y_ps.at(i * PAIRS))
                    nc.gpsimd.tensor_copy(xs[:, :, :], token_tile(xnT, i)).then_inc(c.xs_ready.sem, 1)

            @block.tensor
            def _(pe):
                with pe.Fori(0, B) as i:
                    pe.wait_ge(c.xs_ready.sem, c.xs_ready.at(i + 1))
                    for e in range(PAIRS):
                        pe.wait_ge(c.x_added.sem, c.x_added.at(2 * (i * PAIRS + e - 4)))
                        for kd in range(KD):
                            last = nc.tensor.matmul(c.bank[e % 5][:, :], xs[:, kd, :],
                                                    we[:, kd, 2 * e:2 * e + 2, :].rearrange("p a n -> p (a n)"),
                                                    start=kd == 0, stop=kd == KD - 1)
                        last.then_inc(c.y_ps.sem, 1)

            @block.vector
            def _(dve):
                with dve.Fori(0, B) as i:
                    for e in range(E):
                        dve.wait_ge(c.y_ps.sem, c.y_ps.at(i * PAIRS + e // 2 + 1))
                        dve.wait_ge(c.x_added.sem, c.x_added.at(i * E + e))
                        nc.vector.scalar_tensor_tensor(out=c.x[:, i, :],
                                                       in0=c.bank[e // 2 % 5][:, (e % 2) * D:(e % 2 + 1) * D],
                                                       scalar=comb[:, i, e:e + 1], in1=c.x[:, i, :],
                                                       op0=ALU.mult, op1=ALU.add).then_inc(c.x_added.sem, 1)
        c.passed(xs_ready=B, y_ps=B * PAIRS, x_added=B * E)


def l2_attn(c, w):
    nc, NP, H, W = c.nc, 5, 16, D + 16
    j = np.arange(6, dtype=np.float32)
    tail = np.flip(np.cumsum(np.flip((j + 1.0) ** (-1.5))))
    beta = tail[1:].astype(np.float32)
    beta = beta / beta.sum()
    lo, hi = -1.0 + 1e-6, 1.0 - 1e-6
    with ExitStack() as ctx:
        sb = lambda n, shape: c.sb(ctx, f"l2a_{n}", shape)
        win, wo = sb("win", [P, KD, 3 * D]), sb("wo", [P, KD, D])
        xn, xT, v = sb("xn", [P, D]), sb("xT", [P, KD, S]), sb("v", [P, D])
        TQ, TK, R, CS = (sb(n, [P, NP, W]) for n in ("TQ", "TK", "R", "CS"))
        tmp = [sb(f"tmp{i}", [P, D]) for i in range(2)]
        nd, rden = sb("nd", [P, W]), sb("rden", [P, H])
        o, oT = sb("o", [P, D]), sb("oT", [P, KD, S])
        load(c, [(win[:, :, :], w["L2_attn_W_in"]), (wo[:, :, :], w["L2_attn_W_out"])])
        layernorm_stats(c, [c.x])
        bank_m, bank_qk, bank_v, bank_c = c.bank[0], c.bank[1], c.bank[2], c.bank[3:8]
        KV = 14

        with nc.Block() as block:
            @block.vector
            def _(dve):
                with dve.Fori(0, B) as i:
                    chain = Chain(dve, c.chain_v, i * KV)
                    v_ = nc.vector
                    dve.wait_ge(c.xt_ps.sem, c.xt_ps.at(i))
                    v_.tensor_scalar(xn[:, :], c.x[:, i, :], c.mv[:, i, 0:1], c.rstd[:, bass.ds(i, 1)],
                                     ALU.subtract, ALU.mult).then_inc(c.xn_ready.sem, 1)
                    dve.wait_ge(c.k_ps.sem, c.k_ps.at(i + 1))
                    for a, T in enumerate((TQ, TK)):
                        last = v_.tensor_scalar(T[:, 0, 0:D], bank_qk[:, a * D:(a + 1) * D], 0.25, hi,
                                                ALU.mult, ALU.min)
                    last.then_inc(c.k_ready.sem, 1)
                    dve.wait_ge(c.k_ready.sem, c.k_ready.at(i + 1))
                    for T in (TQ, TK):
                        last = v_.tensor_scalar(T[:, 0, 0:D], T[:, 0, 0:D], lo, None, ALU.max)
                    chain(last)
                    for p in range(1, NP):
                        for a, T in enumerate((TQ, TK)):
                            last = v_.scalar_tensor_tensor(out=tmp[a][:, :], in0=T[:, 0, 0:D], scalar=2.0,
                                                           in1=T[:, p - 1, 0:D], op0=ALU.mult, op1=ALU.mult)
                        chain(last)
                        for a, T in enumerate((TQ, TK)):
                            if p == 1:
                                last = v_.tensor_scalar(T[:, 1, 0:D], tmp[a][:, :], -1.0, None, ALU.add)
                            else:
                                last = v_.tensor_tensor(T[:, p, 0:D], tmp[a][:, :], T[:, p - 2, 0:D], ALU.subtract)
                        chain(last)
                    dve.wait_ge(c.v_ready.sem, c.v_ready.at(i + 1))
                    dve.wait_ge(c.c_ps.sem, c.c_ps.at(i * NP))
                    v_.tensor_tensor(R[:, :, 0:D], TK[:, :, 0:D], v[:, :].unsqueeze(1).to_broadcast([P, NP, D]),
                                     ALU.mult)
                    v_.tensor_reduce(R[:, :, D:W], TK[:, :, 0:D].rearrange("p n (h d) -> p n h d", h=H), AX.X,
                                     ALU.add).then_inc(c.a_ready.sem, 1)
                    chain(v_.tensor_reduce(TQ[:, :, D:W], TQ[:, :, 0:D].rearrange("p n (h d) -> p n h d", h=H),
                                           AX.X, ALU.add))
                    dve.wait_ge(c.c_ready.sem, c.c_ready.at((i + 1) * NP))
                    chain(v_.tensor_tensor(TQ[:, :, :], TQ[:, :, :], CS[:, :, :], ALU.mult))
                    chain(v_.tensor_reduce(nd[:, :], TQ[:, :, :].rearrange("p n f -> p f n"), AX.X, ALU.add))
                    chain(v_.tensor_scalar(nd[:, D:W], nd[:, D:W], 1e-7, None, ALU.add))
                    chain(v_.reciprocal(rden[:, :], nd[:, D:W]))
                    dve.wait_ge(c.ot_ps.sem, c.ot_ps.at(i))
                    v_.tensor_tensor(heads_of(o[:, :], H), heads_of(nd[:, 0:D], H),
                                     rden[:, :].unsqueeze(2).to_broadcast([P, H, 16]), ALU.mult)\
                        .then_inc(c.o_ready.sem, 1)
                    dve.wait_ge(c.y_ps.sem, c.y_ps.at(i + 1))
                    v_.tensor_tensor(c.x[:, i, :], c.x[:, i, :], bank_v[:, D:2 * D], ALU.add)\
                        .then_inc(c.x_added.sem, 1)
                    assert chain.n == KV, chain.n

            @block.scalar
            def _(act):
                with act.Fori(0, B) as i:
                    act.wait_ge(c.xt_ps.sem, c.xt_ps.at(i + 1))
                    act.wait_ge(c.v_ps.sem, c.v_ps.at(i))
                    nc.scalar.copy(xT[:, :, :], bank_m[:, 0:D].rearrange("p (j t) -> p j t", j=KD))\
                        .then_inc(c.xT_ready.sem, 1)
                    act.wait_ge(c.v_ps.sem, c.v_ps.at(i + 1))
                    act.wait_ge(c.a_ready.sem, c.a_ready.at(i))
                    nc.scalar.copy(v[:, :], bank_v[:, 0:D]).then_inc(c.v_ready.sem, 1)
                    for p in range(NP):
                        act.wait_ge(c.c_ps.sem, c.c_ps.at(i * NP + p + 1))
                        if p == 0:
                            act.wait_ge(c.o_ready.sem, c.o_ready.at(i))
                        nc.scalar.mul(CS[:, p, :], bank_c[p][:, 0:W], float(beta[p])).then_inc(c.c_ready.sem, 1)
                    act.wait_ge(c.ot_ps.sem, c.ot_ps.at(i + 1))
                    act.wait_ge(c.y_ps.sem, c.y_ps.at(i))
                    nc.scalar.copy(oT[:, :, :], bank_m[:, 0:D].rearrange("p (j q) -> p j q", j=KD))\
                        .then_inc(c.oT_ready.sem, 1)

            @block.tensor
            def _(pe):
                with pe.Fori(0, B) as i:
                    pe.wait_ge(c.xn_ready.sem, c.xn_ready.at(i + 1))
                    pe.wait_ge(c.oT_ready.sem, c.oT_ready.at(i))
                    for k in range(KD):
                        last = nc.tensor.transpose(bank_m[:, k * S:(k + 1) * S], xn[:, k * P:(k + 1) * P],
                                                   c.ident[:, :])
                    last.then_inc(c.xt_ps.sem, 1)
                    pe.wait_ge(c.xT_ready.sem, c.xT_ready.at(i + 1))
                    pe.wait_ge(c.k_ready.sem, c.k_ready.at(i))
                    for kd in range(KD):
                        last = nc.tensor.matmul(bank_qk[:, :], xT[:, kd, :], win[:, kd, 0:2 * D],
                                                start=kd == 0, stop=kd == KD - 1)
                    last.then_inc(c.k_ps.sem, 1)
                    pe.wait_ge(c.x_added.sem, c.x_added.at(i))
                    for kd in range(KD):
                        last = nc.tensor.matmul(bank_v[:, 0:D], xT[:, kd, :], win[:, kd, 2 * D:3 * D],
                                                start=kd == 0, stop=kd == KD - 1)
                    last.then_inc(c.v_ps.sem, 1)
                    pe.wait_ge(c.a_ready.sem, c.a_ready.at(i + 1))
                    pe.wait_ge(c.c_ready.sem, c.c_ready.at(i * NP))
                    for p in range(NP):
                        nc.tensor.matmul(bank_c[p][:, 0:W], c.upto[:, :], R[:, p, :], start=True, stop=True)\
                            .then_inc(c.c_ps.sem, 1)
                    pe.wait_ge(c.o_ready.sem, c.o_ready.at(i + 1))
                    for k in range(KD):
                        last = nc.tensor.transpose(bank_m[:, k * S:(k + 1) * S], o[:, k * P:(k + 1) * P],
                                                   c.ident[:, :])
                    last.then_inc(c.ot_ps.sem, 1)
                    pe.wait_ge(c.oT_ready.sem, c.oT_ready.at(i + 1))
                    pe.wait_ge(c.v_ready.sem, c.v_ready.at(i + 1))
                    for k in range(KD):
                        last = nc.tensor.matmul(bank_v[:, D:2 * D], oT[:, k, :], wo[:, k, :],
                                                start=k == 0, stop=k == KD - 1)
                    last.then_inc(c.y_ps.sem, 1)
        c.passed(chain_v=B * KV, xn_ready=B, xt_ps=B, xT_ready=B, k_ps=B, k_ready=B, v_ps=B, v_ready=B, a_ready=B,
                 c_ps=B * NP, c_ready=B * NP, o_ready=B, ot_ps=B, oT_ready=B, y_ps=B, x_added=B)

class Rotary:
    pass


def shift_in(c, xin, shifted):
    with c.nc.Block() as block:
        @block.sync
        def _(sp):
            sp.dma_start(shifted[1:P, :, :], xin[0:P - 1, :, P:D]).then_inc(c.shifted.sem, 16)
            sp.wait_ge(c.shifted.sem, c.shifted.at(16))
    c.passed(shifted=16)


def l3_ffn(c, w):
    with ExitStack() as ctx:
        xin, shifted = c.sb(ctx, "l3_xin", [P, B, D]), c.sb(ctx, "l3_shifted", [P, B, P])
        layernorm_stats(c, [c.x])
        with c.nc.Block() as block:
            @block.vector
            def _(dve):
                c.nc.vector.memset(shifted[:, :, :], 0.0)
                with dve.Fori(0, B) as i:
                    c.nc.vector.tensor_scalar(xin[:, i, :], c.x[:, i, :], c.mv[:, i, 0:1], c.rstd[:, bass.ds(i, 1)],
                                              ALU.subtract, ALU.mult)
        for layer in range(2):
            shift_in(c, xin, shifted)
            local_attention(c, w, layer, xin, shifted)
            shift_in(c, xin, shifted)
            gated_mlp(c, w, layer, xin, shifted)
        with c.nc.Block() as block:
            @block.vector
            def _(dve):
                c.nc.vector.tensor_tensor(c.x[:, :, :], c.x[:, :, :], xin[:, :, :], ALU.add)


def local_attention(c, w, layer, xin, shifted):
    nc, heads, dh = c.nc, 8, 64
    I = heads * dh
    name = f"l3l{layer}"
    with ExitStack() as outer:
        r = Rotary()
        r.QK = c.sb(outer, name + "_QK", [P, B, 2 * I])
        r.V = c.sb(outer, name + "_V", [P, B, heads, dh + 1])
        r.rnorm = c.sb(outer, name + "_rnorm", [P, B, 2 * heads])
        with ExitStack() as ctx:
            sb = lambda n, shape: c.sb(ctx, f"{name}_{n}", shape)
            wqkv = sb("wqkv", [P, KD, 3 * I])
            hs, hT, sq, ss = sb("hs", [P, D]), sb("hT", [P, KD, S]), sb("sq", [P, 2 * I]), sb("ss", [P, B, 2 * heads])
            load(c, [(wqkv[:, :, :], w["L3_ffn_wqkv"][layer])])
            bank_x, bank_q, bank_k, bank_v = c.bank[0:4]
            with nc.Block() as block:
                @block.gpsimd
                def _(pool):
                    nc.gpsimd.memset(r.V[:, :, :, :], 1.0).then_inc(c.a_ready.sem, 1)
                    with pool.Fori(0, B) as i:
                        pool.wait_ge(c.xt_ps.sem, c.xt_ps.at(i))
                        nc.gpsimd.tensor_copy(hs[:, 0:P], xin[:, i, 0:P])
                        nc.gpsimd.tensor_copy(hs[:, P:D], shifted[:, i, :]).then_inc(c.xn_ready.sem, 1)

                @block.tensor
                def _(pe):
                    with pe.Fori(0, B) as i:
                        pe.wait_ge(c.xn_ready.sem, c.xn_ready.at(i + 1))
                        for j in range(KD):
                            last = nc.tensor.transpose(bank_x[:, j * S:(j + 1) * S], hs[:, j * P:(j + 1) * P],
                                                       c.ident[:, :])
                        last.then_inc(c.xt_ps.sem, 1)
                        pe.wait_ge(c.xT_ready.sem, c.xT_ready.at(i + 1))
                        pe.wait_ge(c.k_ready.sem, c.k_ready.at(i))
                        for a, bank in enumerate((bank_q, bank_k)):
                            for kd in range(KD):
                                last = nc.tensor.matmul(bank[:, :], hT[:, kd, :], wqkv[:, kd, a * I:(a + 1) * I],
                                                        start=kd == 0, stop=kd == KD - 1)
                        last.then_inc(c.k_ps.sem, 1)
                        pe.wait_ge(c.v_ready.sem, c.v_ready.at(i))
                        for kd in range(KD):
                            last = nc.tensor.matmul(bank_v[:, :], hT[:, kd, :], wqkv[:, kd, 2 * I:3 * I],
                                                    start=kd == 0, stop=kd == KD - 1)
                        last.then_inc(c.v_ps.sem, 1)

                @block.scalar
                def _(act):
                    with act.Fori(0, B) as i:
                        act.wait_ge(c.xt_ps.sem, c.xt_ps.at(i + 1))
                        act.wait_ge(c.v_ps.sem, c.v_ps.at(i))
                        nc.scalar.copy(hT[:, :, :], bank_x[:, 0:D].rearrange("p (j t) -> p j t", j=KD))\
                            .then_inc(c.xT_ready.sem, 1)
                        act.wait_ge(c.k_ps.sem, c.k_ps.at(i + 1))
                        nc.scalar.copy(r.QK[:, i, 0:I], bank_q[:, :])
                        nc.scalar.copy(r.QK[:, i, I:2 * I], bank_k[:, :]).then_inc(c.k_ready.sem, 1)

                @block.vector
                def _(dve):
                    dve.wait_ge(c.a_ready.sem, c.a_ready.at(1))
                    with dve.Fori(0, B) as i:
                        chain = Chain(dve, c.chain_v, i * 2)
                        dve.wait_ge(c.v_ps.sem, c.v_ps.at(i + 1))
                        nc.vector.tensor_copy(r.V[:, i, :, 0:dh], heads_of(bank_v[:, :], heads))\
                            .then_inc(c.v_ready.sem, 1)
                        dve.wait_ge(c.k_ready.sem, c.k_ready.at(i + 1))
                        chain(nc.vector.tensor_tensor(sq[:, :], r.QK[:, i, :], r.QK[:, i, :], ALU.mult))
                        chain(nc.vector.tensor_reduce(ss[:, i, :], heads_of(sq[:, :], 2 * heads), AX.X, ALU.add))
            c.passed(xn_ready=B, xt_ps=B, xT_ready=B, k_ps=B, k_ready=B, v_ps=B, v_ready=B, chain_v=2 * B, a_ready=1)
            with nc.Block() as block:
                @block.scalar
                def _(act):
                    nc.scalar.activation(r.rnorm[:, :, :], ss[:, :, :], ACT.Sqrt).then_inc(c.std_ready.sem, 1)

                @block.vector
                def _(dve):
                    chain = Chain(dve, c.chain_v, 0)
                    dve.wait_ge(c.std_ready.sem, c.std_ready.at(1))
                    chain(nc.vector.tensor_scalar(ss[:, :, :], r.rnorm[:, :, :], 1e-12, None, ALU.max))
                    chain(nc.vector.reciprocal(r.rnorm[:, :, :], ss[:, :, :]))
            c.passed(std_ready=1, chain_v=2)
        with ExitStack() as ctx:
            wo = c.sb(ctx, name + "_wo", [P, I // P, D])
            r.scale, r.cos, r.sin = (c.sb(ctx, f"{name}_{n}", [P, 2, dh]) for n in ("scale", "cos", "sin"))
            load(c, [(wo[:, :, :], w["L3_ffn_wo"][layer]), (r.scale[:, :, :], w["L3_ffn_qk_scale"][layer]),
                     (r.cos[:, :, :], w["rotary_cos"]), (r.sin[:, :, :], w["rotary_sin"])])
            attention(c, name + "a", 2, 1, dh, (None, None, None, wo), q_scale=[8.0] * 2, rotary=r, into=xin,
                      mask_of=lambda g, t, i: (None, per_head(c.causal_add[:, :])))


def gated_mlp(c, w, layer, xin, shifted):
    nc, FC, TB, TW = c.nc, L3_HID // P, 4, 512
    TT = TW // P
    name = f"l3m{layer}"
    layernorm_stats(c, [xin[:, :, 0:P], shifted])
    with ExitStack() as ctx:
        sb = lambda n, shape: c.sb(ctx, f"{name}_{n}", shape)
        w1, w2 = sb("w1", [P, KD, 2 * L3_HID]), sb("w2", [P, FC, D])
        lg, lb, b1, b2 = sb("lg", [P, KD]), sb("lb", [P, KD]), sb("b1", [P, 2, FC]), sb("b2", [P, D])
        hs, hT = sb("hs", [P, D]), sb("hT", [P, KD, B * S])
        G = [sb(f"G{i}", [P, TW]) for i in range(2)]
        u, yb = sb("u", [P, FC, TW]), sb("yb", [P, D])
        load(c, [(w1[:, :, :], w["L3_ffn_w1"][layer]), (w2[:, :, :], w["L3_ffn_w2"][layer]),
                 (lg[:, :], w["L3_ffn_ln_g"][layer]), (lb[:, :], w["L3_ffn_ln_b"][layer]),
                 (b1[:, :, :], w["L3_ffn_b1"][layer]), (b2[:, :], w["L3_ffn_b2"][layer])])
        with nc.Block() as block:
            @block.vector
            def _(dve):
                with dve.Fori(0, B) as i:
                    dve.wait_ge(c.xt_ps.sem, c.xt_ps.at(i))
                    for cols, src in ((slice(0, P), xin[:, i, 0:P]), (slice(P, D), shifted[:, i, :])):
                        last = nc.vector.tensor_scalar(hs[:, cols], src, c.mv[:, i, 0:1], c.rstd[:, bass.ds(i, 1)],
                                                       ALU.subtract, ALU.mult)
                    last.then_inc(c.xn_ready.sem, 1)

            @block.tensor
            def _(pe):
                with pe.Fori(0, B) as i:
                    pe.wait_ge(c.xn_ready.sem, c.xn_ready.at(i + 1))
                    pe.wait_ge(c.xT_ready.sem, c.xT_ready.at(i))
                    for j in range(KD):
                        last = nc.tensor.transpose(c.bank[0][:, j * S:(j + 1) * S], hs[:, j * P:(j + 1) * P],
                                                   c.ident[:, :])
                    last.then_inc(c.xt_ps.sem, 1)

            @block.scalar
            def _(act):
                with act.Fori(0, B) as i:
                    act.wait_ge(c.xt_ps.sem, c.xt_ps.at(i + 1))
                    for j in range(KD):
                        last = nc.scalar.activation(hT[:, j, bass.ds(i * S, S)], c.bank[0][:, j * S:(j + 1) * S],
                                                    ACT.Identity, bias=lb[:, j:j + 1], scale=lg[:, j:j + 1])
                    last.then_inc(c.xT_ready.sem, 1)
        c.passed(xn_ready=B, xt_ps=B, xT_ready=B)

        bank_a, bank_g, bank_y = c.bank[0:2], c.bank[2:4], c.bank[4:8]
        with nc.Block() as block:
            @block.tensor
            def _(pe):
                with pe.Fori(0, TB) as tb:
                    for f in range(FC):
                        n = tb * FC + f
                        pe.wait_ge(c.a_ready.sem, c.a_ready.at(n - 1))
                        for kd in range(KD):
                            last = nc.tensor.matmul(bank_g[f % 2][:, :], w1[:, kd, L3_HID + f * P:L3_HID + (f + 1) * P],
                                                    hT[:, kd, bass.ds(tb * TW, TW)], start=kd == 0, stop=kd == KD - 1)
                        last.then_inc(c.h_ps.sem, 1)
                        for kd in range(KD):
                            last = nc.tensor.matmul(bank_a[f % 2][:, :], w1[:, kd, f * P:(f + 1) * P],
                                                    hT[:, kd, bass.ds(tb * TW, TW)], start=kd == 0, stop=kd == KD - 1)
                        last.then_inc(c.l_ps.sem, 1)
                    for tt in range(TT):
                        pe.wait_ge(c.x_added.sem, c.x_added.at(tb * TT + tt - 3))
                        for f in range(FC):
                            if tt == 0:
                                pe.wait_ge(c.a_ready.sem, c.a_ready.at(tb * FC + f + 1))
                            last = nc.tensor.matmul(bank_y[tt][:, 0:D], u[:, f, tt * P:(tt + 1) * P], w2[:, f, :],
                                                    start=f == 0, stop=f == FC - 1)
                        last.then_inc(c.y_ps.sem, 1)

            @block.scalar
            def _(act):
                with act.Fori(0, TB) as tb:
                    for f in range(FC):
                        n = tb * FC + f
                        act.wait_ge(c.h_ps.sem, c.h_ps.at(n + 1))
                        act.wait_ge(c.a_ready.sem, c.a_ready.at(n - 1))
                        nc.scalar.activation(G[f % 2][:, :], bank_g[f % 2][:, :], ACT.Gelu,
                                             bias=b1[:, 1, f:f + 1]).then_inc(c.h_ready.sem, 1)

            @block.vector
            def _(dve):
                with dve.Fori(0, TB) as tb:
                    for f in range(FC):
                        n = tb * FC + f
                        dve.wait_ge(c.h_ready.sem, c.h_ready.at(n + 1))
                        dve.wait_ge(c.l_ps.sem, c.l_ps.at(n + 1))
                        if f == 0:
                            dve.wait_ge(c.y_ps.sem, c.y_ps.at(tb * TT))
                        nc.vector.scalar_tensor_tensor(out=u[:, f, :], in0=bank_a[f % 2][:, :],
                                                       scalar=b1[:, 0, f:f + 1], in1=G[f % 2][:, :],
                                                       op0=ALU.add, op1=ALU.mult).then_inc(c.a_ready.sem, 1)
                    chain = Chain(dve, c.chain_v, tb * TT)
                    for tt in range(TT):
                        b = tb * TT + tt
                        dve.wait_ge(c.y_ps.sem, c.y_ps.at(b + 1))
                        dve.wait_ge(c.x_added.sem, c.x_added.at(b))
                        chain(nc.vector.tensor_tensor(yb[:, :], bank_y[tt][:, 0:D], b2[:, :], ALU.add))
                        nc.vector.tensor_tensor(xin[:, b, :], xin[:, b, :], yb[:, :], ALU.add)\
                            .then_inc(c.x_added.sem, 1)
        c.passed(h_ps=TB * FC, l_ps=TB * FC, h_ready=TB * FC, a_ready=TB * FC, y_ps=B, x_added=B, chain_v=B)


STEPS = [l0_attn, l0_xattn, l0_ffn, l1_attn, l1_xattn, l1_ffn, l2_attn, l2_xattn, l2_ffn, l3_attn, l3_xattn, l3_ffn]


def decoder(nc, w, out):
    with ExitStack() as ctx:
        c = Core(nc, ctx)
        c.hm16, c.hm64 = c.sb(ctx, "hm16", [P, 8]), c.sb(ctx, "hm64", [P, 2])
        c.one = c.sb(ctx, "one", [P, 1])
        c.ones, c.earlier, c.upto = (c.sb(ctx, n, [P, P]) for n in ("ones", "earlier", "upto"))
        c.w = w
        with nc.Block() as block:
            @block.sync
            def _(sp):
                for s in c.sig.values():
                    if s.start:
                        sp.sem_inc(s.sem, s.start)
        load(c, [(c.x[:, :, :], w["x"]), (c.ctxT[:, :, :], w["ctx_1024"]), (c.ident[:, :], w["ident"]),
                 (c.causal_add[:, :], w["causal_add"]), (c.hm16[:, :], w["hm16"]), (c.hm64[:, :], w["hm64"]),
                 (c.one[:, :], w["one"]), (c.ones[:, :], w["ones"]), (c.earlier[:, :], w["earlier"]),
                 (c.upto[:, :], w["upto"])])
        c.rows_in, c.rows_out = (nc.dram_tensor(n, (ROWS + (MOST - 1) * WIDTH, D), F32).ap()
                                 for n in ("rows_in", "rows_out"))
        blocks = ROWS // WIDTH + MOST - 1
        zeros = c.sb(ctx, "zeros", [P, WIDTH // P * D])
        with nc.Block() as block:
            @block.gpsimd
            def _(pool):
                nc.gpsimd.memset(zeros[:, :], 0.0).then_inc(c.chain_p.sem, 1)
                pool.wait_ge(c.chain_p.sem, c.chain_p.at(1))

            @block.sync
            def _(sp):
                sp.wait_ge(c.chain_p.sem, c.chain_p.at(1))
                for rows in (c.rows_in, c.rows_out):
                    part = rows.rearrange("(r p t) d -> r p (t d)", p=P, r=blocks)
                    for r in range(blocks):
                        sp.dma_start(part[r], zeros[:, :]).then_inc(c.cleared.sem, 16)
        c.passed(chain_p=1, cleared=16 * 2 * blocks)
        for n in SUBLAYERS:
            STEPS[n](c, w)
        with nc.Block() as block:
            @block.sync
            def _(sp):
                sp.dma_start(out, c.x[:, :, :]).then_inc(c.stored.sem, 16)
                sp.wait_ge(c.stored.sem, c.stored.at(16))


def layout(inputs):
    a = {k: np.asarray(v) for k, v in inputs.items()}
    cont = np.ascontiguousarray

    def rows(m):
        return cont(m.reshape(-1, P, m.shape[1]).transpose(1, 0, 2))

    def column(m):
        return cont(m.reshape(-1, P).T)

    def everywhere(m):
        return cont(np.broadcast_to(m, (P,) + m.shape))

    w = {"x": cont(a["x"].transpose(1, 0, 2)), "ctx_1024": rows(a["ctx_1024"].reshape(B * S, D).T)}
    w["mask_Bx1xSxS2_ik1"] = cont(a["mask_Bx1xSxS2_ik1"][:, 0].transpose(1, 0, 2))
    w["mask_BxSxS2_if1"] = cont(a["mask_BxSxS2_if1"].transpose(1, 0, 2))
    for n in ("L0_attn_W_qkv", "L0_attn_W_out", "L0_xattn_Wq", "L0_xattn_Wkv", "L0_xattn_Wout", "L0_ffn_Wg",
              "L1_attn_Wq", "L1_attn_Wk", "L1_attn_Wv", "L1_attn_Wout", "L1_ffn_Wg", "L2_ffn_wg1"):
        w[n] = rows(a[n])
    for n in ("L1_xattn_WQ_w", "L1_xattn_WK_w", "L1_xattn_WV_w", "L1_xattn_WO_w", "L2_attn_W_in", "L2_attn_W_out",
              "L2_xattn_Wq", "L2_xattn_Wk", "L2_xattn_Wv", "L2_xattn_Wo", "L3_attn_Wq", "L3_attn_Wk", "L3_attn_Wv",
              "L3_attn_Wo", "L3_xattn_Wq", "L3_xattn_Wk", "L3_xattn_Wv", "L3_xattn_Wo"):
        w[n] = rows(a[n].T)
    for n in ("L1_attn_norm_w", "L1_xattn_WQ_b", "L1_xattn_WK_b", "L3_attn_bq", "L3_attn_bk", "L3_xattn_bq",
              "L3_xattn_bk"):
        w[n] = column(a[n])
    for n in ("L0_xattn_bout", "L1_xattn_WV_b", "L1_xattn_WO_b", "L3_attn_bv", "L3_attn_bo", "L3_xattn_bv",
              "L3_xattn_bo"):
        w[n] = everywhere(a[n])
    for n in "qk":
        w[f"L1_attn_W{n}T"] = rows(a[f"L1_attn_W{n}"].T)
        f = a[f"L1_attn_W{n}f"]
        wide = np.zeros((D, D), f.dtype)
        for h in range(D // 16):
            wide[16 * h:16 * h + 16, 16 * h:16 * h + 16] = f
        w[f"L1_attn_W{n}f"] = rows(wide)
    for n in ("L0_ffn", "L1_ffn"):
        w[n + "_W1"] = cont(a[n + "_W1"].reshape(8, KD, P, 1024).transpose(0, 2, 1, 3))
        w[n + "_W2"] = cont(a[n + "_W2"].reshape(8, 8, P, D).transpose(0, 2, 1, 3))
        w[n + "_b1"] = cont(a[n + "_b1"].reshape(8, 8, P).transpose(2, 0, 1))
        w[n + "_b2"] = everywhere(a[n + "_b2"])
    w["L0_ffn_bg"] = everywhere(a["L0_ffn_bg"])
    w["L2_ffn_bg1"] = cont(a["L2_ffn_bg1"][:, None])
    w["L2_ffn_wg2"] = a["L2_ffn_wg2"]
    w["L2_ffn_bg2"] = everywhere(a["L2_ffn_bg2"][:20])
    w["L2_ffn_We"] = cont(a["L2_ffn_We"].reshape(20, KD, P, D).transpose(2, 1, 0, 3))
    w["L2_ffn_be"] = a["L2_ffn_be"]
    n = "L3_ffn_"
    HID = int(D * 4 * 2 / 3)
    short = -HID % P
    w[n + "w1"] = np.stack([rows(np.pad(v.reshape(D, 2, HID), ((0, 0), (0, 0), (0, short))).reshape(D, -1))
                            for v in a[n + "w1"]])
    for m in ("wqkv", "wo"):
        w[n + m] = np.stack([rows(v) for v in a[n + m]])
    w[n + "w2"] = np.stack([rows(np.pad(v, ((0, short), (0, 0)))) for v in a[n + "w2"]])
    w[n + "ln_g"], w[n + "ln_b"] = (np.stack([column(v) for v in a[n + m]]) for m in ("ln_g", "ln_b"))
    w[n + "b1"] = cont(np.pad(a[n + "b1"].reshape(2, 2, HID), ((0, 0), (0, 0), (0, short)))
                       .reshape(2, 2, -1, P).transpose(0, 3, 1, 2))
    w[n + "b2"] = np.stack([everywhere(v) for v in a[n + "b2"]])
    w[n + "qk_scale"] = np.stack([everywhere(np.stack([q, k])) for q, k in zip(a[n + "q_scale"], a[n + "k_scale"])])
    f32 = np.float32
    q, k = np.arange(S)[:, None], np.arange(S)[None, :]
    w["ident"] = np.eye(P, dtype=f32)
    w["causal"] = (k <= q).astype(f32)
    w["causal_add"] = np.where(k <= q, 0.0, NEG).astype(f32)
    w["causal_minus2"] = np.where(k <= q, 0.0, -2.0).astype(f32)
    w["window_add"] = np.where((k <= q) & (k >= q - 64), 0.0, NEG).astype(f32)
    slopes = np.array([(2 ** (-2 ** (-(math.log2(16) - 3)))) ** (i + 1) for i in range(16)], f32)
    w["alibi"] = np.where(k[:, None] <= q[:, None], slopes[None, :, None] * (k - q)[:, None].astype(f32), f32(NEG)).astype(f32)
    p = np.arange(P)[:, None]
    w["hm16"] = (p // 16 == np.arange(8)[None]).astype(f32)
    w["hm64"] = (p // 64 == np.arange(2)[None]).astype(f32)
    w["ones"] = np.ones((P, P), f32)
    w["earlier"] = (q < k).astype(f32)
    w["upto"] = (q <= k).astype(f32)
    for n in (8, 20):
        w[f"rev{n}"] = everywhere(np.arange(n, 0, -1).astype(f32))
    dh, window = 64, 128
    even = np.arange(0, dh, 2, dtype=f32)
    turn = np.arange(S, dtype=f32)[:, None] * (f32(1.0) / f32(10000.0) ** (even / f32(dh)))[None]
    grow = ((even + f32(0.4 * dh)) / f32(1.4 * dh))[None] ** ((np.arange(S, dtype=f32) - S // 2)
                                                              / f32(window // 2))[:, None]
    cos, sin = np.cos(turn), np.sin(turn)
    w["rotary_cos"] = np.stack([np.concatenate([cos * g, cos * g], 1) for g in (grow, 1 / grow)], 1).astype(f32)
    w["rotary_sin"] = np.stack([np.concatenate([-sin * g, sin * g], 1) for g in (grow, 1 / grow)], 1).astype(f32)
    w["block_limits"] = everywhere(np.array([-1.0] + [WIDTH * i for i in range(1, MOST)], f32))
    w["one"] = np.ones((P, 1), f32)
    return w


def kernel(**inputs):
    import concourse.bacc as bacc
    from concourse.bass_utils import run_bass_kernel_spmd

    nc = bacc.Bacc("TRN2", target_bir_lowering=False, num_devices=1)
    arrays = {f"in_{k}_dram": v for k, v in layout(inputs).items()}
    w = {k: nc.dram_tensor(f"in_{k}_dram", v.shape, mybir.dt.from_np(v.dtype), kind="ExternalInput").ap()
         for k, v in ((n[3:-5], v) for n, v in arrays.items())}
    out = nc.dram_tensor("out_0_dram", (S, B, D), F32, kind="ExternalOutput").ap()
    decoder(nc, w, out)
    got = run_bass_kernel_spmd(nc, [arrays], core_ids=[0]).results[0]["out_0_dram"]
    return np.ascontiguousarray(np.asarray(got).transpose(1, 0, 2))
```

```python
from contextlib import ExitStack
import math

import numpy as np

import concourse.bass as bass
from concourse import mybir

F32 = mybir.dt.float32
I32 = mybir.dt.int32
ALU = mybir.AluOpType
ACT = mybir.ActivationFunctionType
AX = mybir.AxisListType

B, S, D = 16, 128, 256
P = 128
KD = D // P
LN_EPS = 1e-5
NEG = -1e30

L3_HID = -(-int(D * 4 * 2 / 3) // P) * P
WIDTH = 128
MOST = B * S // WIDTH
ROWS = (2 * MOST + 8) * WIDTH
BLOCKS = ROWS // WIDTH + 1
LIST_PARTS = 4
START = 8

ARENA = 10752

DEEP = 4
CHEBYSHEV = 5

SUBLAYERS = range(12)


class Signal:

    def __init__(self, sem, start=START):
        self.sem, self.base, self.start = sem, start, start

    def at(self, n):
        return self.base + n

    def passed(self, n):
        self.base += n


class Chain:

    def __init__(self, eng, counted, start):
        self.eng, self.counted, self.start, self.first, self.n = eng, counted, start, start, 0

    def __call__(self, ins):
        self.n += 1
        ins.then_inc(self.counted.sem, 1)
        self.eng.wait_ge(self.counted.sem, self.counted.at(self.start + self.n))


class Core:

    def __init__(self, nc, ctx):
        self.nc, self.ctx = nc, ctx
        self.sig = {}
        self.loaded = self.count("loaded")
        self.part_loaded = [self.count(f"part_loaded{g}") for g in range(5)]
        self.fetched = self.count("fetched")
        self.stored = self.count("stored")
        self.xn_ready = self.count("xn_ready")
        self.xt_ps = self.count("xt_ps")
        self.xT_ready = self.count("xT_ready")
        self.ctx_ready = self.count("ctx_ready")
        self.k_ps = self.count("k_ps")
        self.q_ready = self.count("q_ready")
        self.k_ready = self.count("k_ready")
        self.v_ps = self.count("v_ps")
        self.v_ready = self.count("v_ready")
        self.km_ready = self.count("km_ready")
        self.s_ps = self.count("s_ps")
        self.e_ready = self.count("e_ready")
        self.p_ready = self.count("p_ready")
        self.pt_ps = self.count("pt_ps")
        self.pT_ready = self.count("pT_ready")
        self.pv_done = self.count("pv_done")
        self.o_ready = self.count("o_ready")
        self.ot_ps = self.count("ot_ps")
        self.oT_ready = self.count("oT_ready")
        self.y_ps = self.count("y_ps")
        self.x_added = self.count("x_added")
        self.v_set = self.count("v_set")
        self.chain_v = self.count("chain_v")
        self.chain_o = self.count("chain_o")
        self.chain_a = self.count("chain_a")
        self.chain_p = self.count("chain_p")
        self.stats_ready = self.count("stats_ready")
        self.halves_ready = self.count("halves_ready")
        self.std_ready = self.count("std_ready")
        self.h_ps = self.count("h_ps")
        self.h_ready = self.count("h_ready")
        self.l_ps = self.count("l_ps")
        self.l_ready = self.count("l_ready")
        self.c_ps = self.count("c_ps")
        self.c_ready = self.count("c_ready")
        self.shifted = self.count("shifted")
        self.cT_ps = self.count("cT_ps")
        self.cT_ready = self.count("cT_ready")
        self.b_ps = self.count("b_ps")
        self.b_added = self.count("b_added")
        self.a_ready = self.count("a_ready")
        self.qk_ps = self.count("qk_ps")
        self.qk_ready = self.count("qk_ready")
        self.squared = self.count("squared")
        self.summed = self.count("summed")
        self.norm_ready = self.count("norm_ready")
        self.q_turned = self.count("q_turned")
        self.k_turned = self.count("k_turned")
        self.vs_ps = self.count("vs_ps")
        self.xs_ready = self.count("xs_ready")
        self.cleared = self.count("cleared")
        self.ended = self.count("ended")
        self.placed = self.count("placed")
        self.listed = self.count("listed")
        self.kept = self.count("kept")
        self.fetched_rows = self.count("fetched_rows", 0)
        self.gathered = [self.count(f"gathered{i}", 0) for i in range(DEEP)]
        self.w_loaded = [self.count(f"w_loaded{i}") for i in range(2)]
        sb = self.sb
        self.x = sb(ctx, "x_res", [P, B, D])
        self.ctxT = sb(ctx, "ctxT", [P, KD, B * S])
        self.ident = sb(ctx, "ident", [P, P])
        self.causal_add = sb(ctx, "causal_add", [P, P])
        self.stats = sb(ctx, "stats", [P, B, 2, 6])
        self.mv = sb(ctx, "mv", [P, B, 2])
        self.std = sb(ctx, "std", [P, B])
        self.rstd = sb(ctx, "rstd", [P, B])
        self.bank = [ctx.enter_context(nc.psum_tensor(f"bank{i}", [P, 512], F32)) for i in range(8)]

    def count(self, name, start=START):
        self.sig[name] = Signal(self.ctx.enter_context(self.nc.semaphore("s_" + name)), start)
        return self.sig[name]

    def sb(self, ctx, name, shape, dt=F32):
        return ctx.enter_context(self.nc.sbuf_tensor(name, shape, dt))

    def passed(self, **counts):
        for name, n in counts.items():
            self.sig[name].passed(n)


def token_tile(t, b):
    return t[:, :, bass.ds(b * S, S)]


def heads_of(ap, h):
    return ap.rearrange("p (h d) -> p h d", h=h)


class Weights:

    def __init__(self, arena):
        self.arena, self.used, self.views, self.pairs, self.parts = arena, 0, {}, [], []

    def __getitem__(self, name):
        return self.views[name]

    def add(self, name, src, *shape):
        size = math.prod(shape[1:])
        flat = self.arena[0:shape[0], self.used:self.used + size]
        letters = "abc"[:len(shape) - 1]
        self.views[name] = flat if len(shape) == 2 else flat.rearrange(
            f"p ({' '.join(letters)}) -> p {' '.join(letters)}", **dict(zip(letters, shape[1:])))
        self.used += size
        self.pairs.append((self.views[name], src))
        return self.views[name]


def prefetch(c, sp, pairs):
    for dst, src in pairs:
        sp.dma_start(dst, src).then_inc(c.fetched.sem, 16)


def prefetched(c, sp, pairs):
    if pairs:
        sp.wait_ge(c.fetched.sem, c.fetched.at(16 * len(pairs)))


def skewed(eng, stages, count=B, span=2):
    most = -(-max(lag for lag, _ in stages) // span) * span

    def step(s, r):
        for lag, f in stages:
            if not isinstance(s, int) or 0 <= s - lag < count:
                f(s - lag, (r - lag) % span)

    for s in range(most):
        step(s, s)
    with eng.Fori(most // span, count // span) as n:
        for r in range(span):
            step(n * span + r, r)
    for s in range(count, count + most):
        step(s, s)


def layernorm(c, parts=1, eps=LN_EPS, rms_eps=None, beside=None, second_half=None):
    nc = c.nc
    with nc.Block() as block:
        @block.vector
        def _(dve):
            if second_half is not None:
                for b in range(B):
                    last = nc.vector.bn_stats(c.stats[:, b, 1, :], second_half[:, b, :])
                last.then_inc(c.halves_ready.sem, 1)
                dve.wait_ge(c.halves_ready.sem, c.halves_ready.at(1))
            for b in range(B):
                last = nc.vector.bn_aggr(c.mv[:, b, :], c.stats[:, b, 0:parts, :])
            chain = Chain(dve, c.chain_v, 0)
            chain(last)
            if rms_eps is not None:
                chain(nc.vector.tensor_scalar(c.rstd[:, :], c.mv[:, :, 1], eps, rms_eps, ALU.add, ALU.mult))
                nc.vector.tensor_tensor(c.rstd[:, :], c.rstd[:, :], c.mv[:, :, 1], ALU.add).then_inc(c.stats_ready.sem, 1)
            else:
                nc.vector.tensor_scalar(c.rstd[:, :], c.mv[:, :, 1], eps, None, ALU.add).then_inc(c.stats_ready.sem, 1)
            if beside:
                beside(dve)
            dve.wait_ge(c.std_ready.sem, c.std_ready.at(1))
            nc.vector.reciprocal(c.rstd[:, :], c.std[:, :])

        @block.scalar
        def _(act):
            act.wait_ge(c.stats_ready.sem, c.stats_ready.at(1))
            nc.scalar.activation(c.std[:, :], c.rstd[:, :], ACT.Sqrt).then_inc(c.std_ready.sem, 1)
    c.passed(stats_ready=1, std_ready=1, chain_v=1 if rms_eps is None else 2, halves_ready=second_half is not None)


class Pipeline:

    def __init__(self, groups, quads, lags):
        self.groups, self.quads, self.lags = groups, quads, lags
        self.T = groups * quads
        self.sequences = 1 if self.T >= 4 and groups > 1 else 2
        self.span = self.T * self.sequences
        self.bodies = B // self.sequences
        self.peeled = -(-max(lags.values()) // self.span)

    def item(self, i, k, stage):
        return Item(self, i, k - self.lags[stage])

    def issued(self, i, k, stage, unit, first):
        k -= self.lags[stage]
        n = i * (self.span // unit) + (-(-k // unit) if first else k // unit)
        return min(max(n, 0), B * self.T // unit) if isinstance(n, int) else n

    def run(self, eng, body, chain=None, steps=0):
        for i in range(self.peeled):
            body(i)
        before = chain.n if chain else 0
        with eng.Fori(self.peeled, self.bodies) as i:
            if chain:
                chain.start, chain.n = chain.first + before + (i - self.peeled) * steps, 0
            body(i)
            assert chain is None or chain.n == steps, (chain.n, steps)
        if chain:
            chain.start, chain.n = chain.first, before + (self.bodies - self.peeled) * steps
        for i in range(self.bodies, self.bodies + self.peeled):
            body(i)


class Item:

    def __init__(self, pipe, i, k):
        r = k % pipe.T
        self.g, self.t, self.at = r // pipe.quads, r % pipe.quads, k % pipe.span
        self.b = i * pipe.sequences + (k - r) // pipe.T
        self.n = self.b * pipe.groups + self.g
        self.m = self.b * pipe.T + r
        self.missing = isinstance(self.b, int) and not 0 <= self.b < B
        self.first = self.t == 0
        self.last = self.t == pipe.quads - 1
        self.group_at = self.at // pipe.quads


def attention(c, name, groups, quads, dh, weights, *, ctx_kv=False, norm_w=None, q_scale, q_bias=None,
              k_bias=None, v_bias=None, y_bias=None, lin_group=None, mask_of=None,
              xin=None, rotary=None, into=None, following=(), arriving=()):
    nc = c.nc
    H = 4 * quads
    T = groups * quads
    wq, wk, wv, wo = weights
    into = c.x if into is None else into
    bank_m, bank_v, bank_o, bank_y = c.bank[0], c.bank[1], c.bank[6], c.bank[7]
    bank_s, bank_t = c.bank[2:4], c.bank[4:6]
    if rotary:
        lags = dict(xn=0, x=1, qk=2, turn=3, qkv=5, s=6, e=6, t=7, pv=8, ot=9, y=10)
        NV = 2
        bank_t, bank_qk = [c.bank[4]] * 2, [c.bank[1], c.bank[5]]
    elif quads == 1:
        lags = dict(xn=0, x=1, qkv=2, s=3, e=3, t=4, pv=5, ot=6, y=7)
        NV = 4
    else:
        lags = dict(xn=0, x=1, qkv=2, s=4, e=5, t=6, pv=8, ot=9, y=10)
        NV = 2
    pipe = Pipeline(groups, quads, lags)
    NG = pipe.span // quads
    NV = min(NV, NG)
    NK = min(4, pipe.span)
    own = rotary is None
    NP = 4 if lin_group is not None else 2
    TS = T - quads * (lin_group is not None)
    unmasked = mask_of(0, 0, 0) == (None, None)
    with ExitStack() as ctx:
        sb = lambda n, shape: c.sb(ctx, f"{name}_{n}", shape)
        xn, xT = sb("xn", [P, D]), sb("xT", [P, KD, S]) if own else None
        if rotary:
            hT, raw = ([sb(f"{n}{i}", shape) for i in range(2)] for n, shape in
                       (("hT", [P, KD, S]), ("raw", [P, 2, H * groups, dh])))
            squares = rotary["squares"]
            lengths, norms = (sb(n, [P, 2, 2, H * groups]) for n in ("lengths", "norms"))
            cos, sin = sb("cos", [P, 2, dh]), sb("sin", [P, 2, dh])
        q = [sb(f"q{i}", [P, KD, S]) for i in range(2)]
        k = [sb(f"k{i}", [P, KD, S]) for i in range(2)]
        kv_src = sb("ctx", [P, KD, S]) if ctx_kv else xT
        km = [sb(f"km{i}", [P, 4, S]) for i in range(NK)]
        v = [sb(f"v{i}", [P, H if own else H * groups, dh + 1]) for i in range(NV)]
        E = [sb(f"E{i}", [P, 4, S]) for i in range(2)]
        Pr = [sb(f"P{i}", [P, 4, S]) for i in range(NP)]
        PT = [sb(f"PT{i}", [P, 4, S]) for i in range(2)]
        mx = [sb(f"mx{i}", [P, 4]) for i in range(2)]
        rden = sb("rden", [P, H])
        o, oT = sb("o", [P, D]), sb("oT", [P, KD, S])
        yb = sb("yb", [P, D])
        hm = c.hm16 if dh == 16 else c.hm64
        vector_steps = (y_bias is not None) + (xin is not None) + 4 * (not own)
        half = dh // 2
        for g in range(groups):
            masks = sum(a is not None for a in mask_of(g, 0, 0))
            vector_steps += quads * (masks - 1) + 2 if g == lin_group else quads * masks + 1
        rotated = [[sb(f"rot{a}{n}", [P, H * groups, dh]) for n in range(2)] for a in range(2)] if rotary else None
        turning = [sb(f"turning{a}", [P, H * groups, dh]) for a in range(2)] if rotary else None

        def rotate(eng, chain, a, it):
            n = H * groups
            t, r, p = turning[a], rotated[a][it.at // T % 2], it.at // T % 2
            per_token = lambda m: m.unsqueeze(1).to_broadcast([P, n, m.shape[1]])
            eng.wait_ge(c.norm_ready.sem, c.norm_ready.at(it.b + 1))
            eng.wait_ge(c.k_ps.sem, c.k_ps.at((it.b - 1) * groups))
            chain(eng.tensor_tensor(t[:, :, :], raw[p][:, a, :, :], norms[:, p, a, :].unsqueeze(2)
                                    .to_broadcast([P, n, dh]), ALU.mult))
            eng.tensor_tensor(r[:, :, 0:half], t[:, :, half:], per_token(sin[:, a, 0:half]), ALU.mult)
            chain(eng.tensor_tensor(r[:, :, half:], t[:, :, 0:half], per_token(sin[:, a, half:]), ALU.mult))
            chain(eng.tensor_tensor(t[:, :, :], t[:, :, :], per_token(cos[:, a, :]), ALU.mult))
            turned = (c.q_turned, c.k_turned)[a]
            eng.tensor_tensor(r[:, :, :], r[:, :, :], t[:, :, :], ALU.add).then_inc(turned.sem, 1)

        def softmax_quads(it, before=0):
            r = it.g * quads + it.t - before
            b, r = (it.b, r) if r >= 0 else (it.b - 1, r + T)
            return b * TS + sum(i // quads != lin_group for i in range(r))

        def is_linear(it, before=0):
            return (it.g * quads + it.t - before) % T // quads == lin_group

        with nc.Block() as block:
            @block.vector
            def _(dve):
                for buffer in v:
                    last = nc.vector.memset(buffer[:, :, :], 1.0)
                if rotary:
                    for a in range(2):
                        nc.vector.tensor_tensor(cos[:, a, :], rotary["cos"][:, a, :], rotary["scale"][:, a, :], ALU.mult)
                        nc.vector.tensor_tensor(sin[:, a, 0:half], rotary["sin"][:, a, 0:half],
                                                rotary["scale"][:, a, half:], ALU.mult)
                        last = nc.vector.tensor_tensor(sin[:, a, half:], rotary["sin"][:, a, half:],
                                                       rotary["scale"][:, a, 0:half], ALU.mult)
                last.then_inc(c.v_set.sem, 1)
                dve.wait_ge(c.v_set.sem, c.v_set.at(1))
                chain = Chain(dve, c.chain_v, 0)

                def normalised(it):
                    dve.wait_ge(c.xt_ps.sem, c.xt_ps.at(it.b))
                    nc.vector.tensor_scalar(xn[:, :], c.x[:, it.b, :], c.mv[:, it.b, 0:1],
                                            c.rstd[:, bass.ds(it.b, 1)],
                                            ALU.subtract, ALU.mult).then_inc(c.xn_ready.sem, 1)

                def lengths_of(it):
                    ss = lengths[:, it.at // T % 2, :, :]
                    dve.wait_ge(c.squared.sem, c.squared.at(it.b + 1))
                    chain(nc.vector.tensor_reduce(ss, squares[:, :, :, :], AX.X, ALU.add))
                    nc.vector.tensor_scalar(ss, ss, 1e-24, None, ALU.max).then_inc(c.summed.sem, 1)

                def projected(it):
                    dve.wait_ge(c.v_ps.sem, c.v_ps.at(it.n + 1))
                    dve.wait_ge(c.s_ps.sem, c.s_ps.at((it.n - 1) * quads))
                    for j in range(KD):
                        src = bank_v[:, D + j * S:D + (j + 1) * S]
                        dst = q[it.group_at % 2][:, j, :]
                        if q_bias is not None:
                            last = nc.vector.tensor_scalar(dst, src, q_bias[:, j:j + 1], q_scale[it.g],
                                                           ALU.add, ALU.mult)
                        else:
                            last = nc.vector.tensor_scalar(dst, src, q_scale[it.g], None, ALU.mult)
                    last.then_inc(c.q_ready.sem, 1)
                    if own:
                        dve.wait_ge(c.pv_done.sem, c.pv_done.at((it.n - NV + 1) * quads))
                        vd = v[it.group_at % NV][:, :, 0:dh]
                        vs = heads_of(bank_v[:, 0:D], H)
                        if v_bias is not None:
                            nc.vector.tensor_tensor(vd, vs, heads_of(v_bias[:, :], H), ALU.add)\
                                .then_inc(c.v_ready.sem, 1)
                        else:
                            nc.vector.tensor_copy(vd, vs).then_inc(c.v_ready.sem, 1)

                def exponents(it):
                    par = it.at % 2
                    lin = it.g == lin_group
                    e = E[par]
                    src = bank_s[par][:, :].rearrange("p (h k) -> p h k", h=4)
                    dve.wait_ge(c.s_ps.sem, c.s_ps.at(it.m + 1))
                    dve.wait_ge(c.p_ready.sem, c.p_ready.at(it.m - 1))
                    mul, plus = mask_of(it.g, it.t, it.b)
                    if mul is not None:
                        chain(nc.vector.tensor_tensor(e[:, :, :], src, mul, ALU.mult))
                        src = e[:, :, :]
                    if plus is not None:
                        ins = nc.vector.tensor_tensor(e[:, :, :], src, plus, ALU.add)
                        if lin:
                            ins.then_inc(c.e_ready.sem, 1)
                            return
                        chain(ins)
                        src = e[:, :, :]
                    nc.vector.tensor_reduce(mx[par][:, :], src, AX.X, ALU.max, negate=True).then_inc(c.e_ready.sem, 1)

                def output(it):
                    dve.wait_ge(c.pv_done.sem, c.pv_done.at((it.n + 1) * quads))
                    po = bank_o[:, 0:H * (dh + 1)].rearrange("p (h d) -> p h d", h=H)
                    if it.g == lin_group:
                        chain(nc.vector.tensor_scalar(rden[:, :], po[:, :, dh], 1e-6, None, ALU.add))
                        chain(nc.vector.reciprocal(rden[:, :], rden[:, :]))
                    else:
                        chain(nc.vector.reciprocal(rden[:, :], po[:, :, dh]))
                    dve.wait_ge(c.ot_ps.sem, c.ot_ps.at(it.n))
                    nc.vector.tensor_tensor(heads_of(o[:, :], H), po[:, :, 0:dh],
                                            rden[:, :].unsqueeze(2).to_broadcast([P, H, dh]), ALU.mult)\
                        .then_inc(c.o_ready.sem, 1)

                def residual(it):
                    dve.wait_ge(c.y_ps.sem, c.y_ps.at((it.b + 1) * groups))
                    y = bank_y[:, 0:D]
                    if y_bias is not None:
                        chain(nc.vector.tensor_tensor(yb[:, :], y, y_bias[:, :], ALU.add))
                        y = yb[:, :]
                    if xin is not None:
                        chain(nc.vector.tensor_tensor(yb[:, :], y, xin[:, it.b, :], ALU.add))
                        y = yb[:, :]
                    nc.vector.tensor_tensor(into[:, it.b, :], into[:, it.b, :], y, ALU.add)\
                        .then_inc(c.x_added.sem, 1)

                def statistics(it):
                    dve.wait_ge(c.x_added.sem, c.x_added.at(it.b + 1))
                    nc.vector.bn_stats(c.stats[:, it.b, 0, :], into[:, it.b, 0:P] if rotary else into[:, it.b, :])

                def body(i):
                    for step in range(pipe.span):
                        done = pipe.item(i, step, "y")
                        ends = not done.missing and done.last and done.g == groups - 1
                        if rotary:
                            it = pipe.item(i, step, "turn")
                            if not it.missing and it.g == 0:
                                lengths_of(it)
                        if ends:
                            residual(done)
                        it = pipe.item(i, step, "pv")
                        if not it.missing and it.last:
                            output(it)
                        it = pipe.item(i, step, "s")
                        if not it.missing:
                            exponents(it)
                        if ends:
                            statistics(done)
                        it = pipe.item(i, step, "qkv")
                        if own and not it.missing and it.first:
                            projected(it)
                        it = pipe.item(i, step, "turn" if rotary else "xn")
                        if not it.missing and it.first and it.g == 0:
                            if rotary:
                                rotate(nc.vector, chain, 1, it)
                            else:
                                normalised(it)

                pipe.run(dve, body, chain, pipe.sequences * vector_steps)

            @block.gpsimd
            def _(pool):
                chain = Chain(pool, c.chain_p, 0)

                def staged(it):
                    pool.wait_ge(c.xt_ps.sem, c.xt_ps.at(it.b))
                    nc.gpsimd.tensor_copy(xn[:, 0:P], into[:, it.b, 0:P])
                    nc.gpsimd.tensor_copy(xn[:, P:D], rotary["shifted"][:, it.b, :]).then_inc(c.xn_ready.sem, 1)

                def context(it):
                    pool.wait_ge(c.v_ps.sem, c.v_ps.at(it.b * groups))
                    nc.gpsimd.tensor_copy(kv_src[:, :, :], token_tile(c.ctxT, it.b)).then_inc(c.ctx_ready.sem, 1)

                def masked(it):
                    if it.first:
                        pool.wait_ge(c.k_ready.sem, c.k_ready.at(it.n + 1))
                    pool.wait_ge(c.s_ps.sem, c.s_ps.at(it.m - NK + 1))
                    src, dst = k[it.group_at % 2], km[it.at % NK]
                    if dh == 16:
                        j, h0 = it.t // 2, 4 * (it.t % 2)
                        last = nc.gpsimd.tensor_tensor(
                            dst[:, :, :], src[:, j, :].unsqueeze(1).to_broadcast([P, 4, S]),
                            hm[:, h0:h0 + 4].unsqueeze(2).to_broadcast([P, 4, S]), ALU.mult)
                    else:
                        for j in range(KD):
                            last = nc.gpsimd.tensor_tensor(
                                dst[:, 2 * j:2 * j + 2, :], src[:, j, :].unsqueeze(1).to_broadcast([P, 2, S]),
                                hm[:, 0:2].unsqueeze(2).to_broadcast([P, 2, S]), ALU.mult)
                    last.then_inc(c.km_ready.sem, 1)

                def body(i):
                    for step in range(pipe.span):
                        it = pipe.item(i, step, "qkv")
                        if not it.missing:
                            masked(it)
                        it = pipe.item(i, step, "x")
                        if ctx_kv and not it.missing and it.first and it.g == 0:
                            context(it)
                        if rotary:
                            it = pipe.item(i, step, "xn")
                            if not it.missing and it.g == 0:
                                staged(it)
                            it = pipe.item(i, step, "turn")
                            if not it.missing and it.g == 0:
                                rotate(nc.gpsimd, chain, 0, it)

                if rotary:
                    pool.wait_ge(c.v_set.sem, c.v_set.at(1))
                pipe.run(pool, body, chain, 0 if own else 3 * pipe.sequences)

            @block.scalar
            def _(act):
                def staged(it):
                    act.wait_ge(c.xt_ps.sem, c.xt_ps.at(it.b + 1))
                    act.wait_ge(c.vs_ps.sem, c.vs_ps.at(it.b - 1))
                    nc.scalar.copy(hT[it.at // T % 2][:, :, :], bank_m[:, 0:D].rearrange("p (j t) -> p j t", j=KD))\
                        .then_inc(c.xT_ready.sem, 1)

                def queries_and_keys(it):
                    p = it.at // T % 2
                    act.wait_ge(c.q_turned.sem, c.q_turned.at(it.b - 1))
                    act.wait_ge(c.k_turned.sem, c.k_turned.at(it.b - 1))
                    for a in range(2):
                        act.wait_ge(c.qk_ps.sem, c.qk_ps.at(2 * it.b + a + 1))
                        nc.scalar.copy(raw[p][:, a, :, :], heads_of(bank_qk[a][:, :], H * groups))\
                            .then_inc(c.qk_ready.sem, 1)
                    act.wait_ge(c.qk_ready.sem, c.qk_ready.at(2 * it.b + 2))
                    act.wait_ge(c.summed.sem, c.summed.at(it.b))
                    nc.scalar.activation(squares[:, :, :, :], raw[p][:, :, :, :], ACT.Square).then_inc(c.squared.sem, 1)

                def inverse_lengths(it):
                    p = it.at // T % 2
                    act.wait_ge(c.summed.sem, c.summed.at(it.b + 1))
                    act.wait_ge(c.q_turned.sem, c.q_turned.at(it.b - 1))
                    act.wait_ge(c.k_turned.sem, c.k_turned.at(it.b - 1))
                    nc.scalar.activation(norms[:, p, :, :], lengths[:, p, :, :], ACT.Ln).then_inc(c.chain_a.sem, 1)
                    act.wait_ge(c.chain_a.sem, c.chain_a.at(it.b + 1))
                    nc.scalar.activation(norms[:, p, :, :], norms[:, p, :, :], ACT.Exp, scale=-0.5)\
                        .then_inc(c.norm_ready.sem, 1)

                def rotated_transposed(it):
                    act.wait_ge(c.k_ps.sem, c.k_ps.at(it.n + 1))
                    act.wait_ge(c.s_ps.sem, c.s_ps.at((it.n - 1) * quads))
                    act.wait_ge(c.km_ready.sem, c.km_ready.at((it.n - 1) * quads))
                    halves = bank_m[:, :].rearrange("p (a j t) -> p a j t", a=2, j=KD)
                    nc.scalar.copy(k[it.group_at % 2][:, :, :], halves[:, 0, :, :]).then_inc(c.k_ready.sem, 1)
                    nc.scalar.mul(q[it.group_at % 2][:, :, :], halves[:, 1, :, :], q_scale[it.g]).then_inc(c.q_ready.sem, 1)

                def value(it):
                    act.wait_ge(c.vs_ps.sem, c.vs_ps.at(it.b + 1))
                    act.wait_ge(c.pv_done.sem, c.pv_done.at((it.b - 1) * T))
                    nc.scalar.copy(v[it.at // T % NV][:, :, 0:dh], heads_of(bank_qk[1][:, :], H * groups))\
                        .then_inc(c.v_ready.sem, 1)

                def normalised(it):
                    act.wait_ge(c.xt_ps.sem, c.xt_ps.at(it.b + 1))
                    act.wait_ge(c.v_ps.sem, c.v_ps.at(it.b * groups))
                    for j in range(KD):
                        src = bank_m[:, j * S:(j + 1) * S]
                        if norm_w is not None:
                            last = nc.scalar.activation(xT[:, j, :], src, ACT.Identity, scale=norm_w[:, j:j + 1])
                        elif j == 0:
                            last = nc.scalar.copy(xT[:, :, :], bank_m[:, 0:D].rearrange("p (j t) -> p j t", j=KD))
                    last.then_inc(c.xT_ready.sem, 1)

                def projected(it):
                    act.wait_ge(c.k_ps.sem, c.k_ps.at(it.n + 1))
                    act.wait_ge(c.km_ready.sem, c.km_ready.at((it.n - 1) * quads))
                    dst = k[it.group_at % 2]
                    for j in range(KD):
                        src = bank_m[:, j * S:(j + 1) * S]
                        if k_bias is not None:
                            last = nc.scalar.activation(dst[:, j, :], src, ACT.Identity, bias=k_bias[:, j:j + 1])
                        elif j == 0:
                            last = nc.scalar.copy(dst[:, :, :], bank_m[:, 0:D].rearrange("p (j t) -> p j t", j=KD))
                    last.then_inc(c.k_ready.sem, 1)

                def exponentials(it):
                    par = it.at % 2
                    act.wait_ge(c.e_ready.sem, c.e_ready.at(it.m + 1))
                    if is_linear(it, NP):
                        act.wait_ge(c.pv_done.sem, c.pv_done.at(it.m - NP + 1))
                    else:
                        act.wait_ge(c.pt_ps.sem, c.pt_ps.at(softmax_quads(it, NP) + 1))
                    if it.g == lin_group:
                        nc.scalar.activation(Pr[it.at % NP][:, :, :], E[par][:, :, :], ACT.Square, bias=c.one[:, :],
                                             scale=0.5).then_inc(c.p_ready.sem, 1)
                    else:
                        masked = any(a is not None for a in mask_of(it.g, it.t, it.b))
                        src = E[par] if masked else bank_s[par][:, :].rearrange("p (h k) -> p h k", h=4)
                        for h in range(4):
                            last = nc.scalar.activation(Pr[it.at % NP][:, h, :], src[:, h, :], ACT.Exp, bias=mx[par][:, h:h + 1])
                        last.then_inc(c.p_ready.sem, 1)

                def transposed(it):
                    par = it.at % 2
                    if is_linear(it):
                        return
                    act.wait_ge(c.pt_ps.sem, c.pt_ps.at(softmax_quads(it) + 1))
                    act.wait_ge(c.pv_done.sem, c.pv_done.at(it.m - 1))
                    nc.scalar.copy(PT[par][:, :, :], bank_t[par][:, :].rearrange("p (h q) -> p h q", h=4))\
                        .then_inc(c.pT_ready.sem, 1)

                def output(it):
                    act.wait_ge(c.ot_ps.sem, c.ot_ps.at(it.n + 1))
                    act.wait_ge(c.y_ps.sem, c.y_ps.at(it.n))
                    nc.scalar.copy(oT[:, :, :], bank_m[:, 0:D].rearrange("p (j q) -> p j q", j=KD))\
                        .then_inc(c.oT_ready.sem, 1)

                def body(i):
                    for step in range(pipe.span):
                        it = pipe.item(i, step, "ot")
                        if not it.missing and it.last:
                            output(it)
                        if lags["e"] > lags["s"]:
                            it = pipe.item(i, step, "e")
                            if not it.missing:
                                exponentials(it)
                        if rotary:
                            it = pipe.item(i, step, "turn")
                            if not it.missing and it.g == 0:
                                inverse_lengths(it)
                        it = pipe.item(i, step, "t")
                        if not it.missing:
                            transposed(it)
                        it = pipe.item(i, step, "qkv")
                        if not it.missing and it.first:
                            if rotary:
                                rotated_transposed(it)
                                if it.g == 0:
                                    value(it)
                            else:
                                projected(it)
                        it = pipe.item(i, step, "x")
                        if not it.missing and it.first and it.g == 0:
                            if rotary:
                                staged(it)
                            else:
                                normalised(it)
                        if lags["e"] == lags["s"]:
                            it = pipe.item(i, step, "e")
                            if not it.missing:
                                exponentials(it)
                        if rotary:
                            it = pipe.item(i, step, "qk")
                            if not it.missing and it.g == 0:
                                queries_and_keys(it)

                pipe.run(act, body)

            @block.tensor
            def _(pe):
                def normalised(it):
                    pe.wait_ge(c.xn_ready.sem, c.xn_ready.at(it.b + 1))
                    for j in range(KD):
                        last = nc.tensor.transpose(bank_m[:, j * S:(j + 1) * S], xn[:, j * P:(j + 1) * P],
                                                   c.ident[:, :])
                    last.then_inc(c.xt_ps.sem, 1)

                def bank_m_free(oT, k, xT):
                    pe.wait_ge(c.oT_ready.sem, c.oT_ready.at(oT))
                    pe.wait_ge(c.k_ready.sem, c.k_ready.at(k))
                    if rotary:
                        pe.wait_ge(c.q_ready.sem, c.q_ready.at(k))
                    pe.wait_ge(c.xT_ready.sem, c.xT_ready.at(xT))

                def projected(it):
                    if ctx_kv:
                        pe.wait_ge(c.ctx_ready.sem, c.ctx_ready.at(it.b + 1))
                    if rotary:
                        if it.g == 0:
                            pe.wait_ge(c.q_turned.sem, c.q_turned.at(it.b + 1))
                            pe.wait_ge(c.k_turned.sem, c.k_turned.at(it.b + 1))
                        for a in range(2):
                            turned = rotated[a][it.at // T % 2][:, :, :].rearrange("p h d -> p (h d)")
                            for j in range(KD):
                                col = it.g * D + j * P
                                place = (1 - a) * D + j * S
                                last = nc.tensor.transpose(bank_m[:, place:place + S], turned[:, col:col + P],
                                                           c.ident[:, :])
                        last.then_inc(c.k_ps.sem, 1)
                        return
                    for j in range(KD):
                        if arriving and j == 0 and isinstance(it.b, int) and it.b == 0:
                            loaded = c.part_loaded[it.g]
                            pe.wait_ge(loaded.sem, loaded.at(16 * len(arriving[it.g])))
                        for kd in range(KD):
                            last = nc.tensor.matmul(bank_m[:, j * S:(j + 1) * S],
                                                    wk[:, kd, it.g * D + j * P:it.g * D + (j + 1) * P],
                                                    kv_src[:, kd, :], start=kd == 0, stop=kd == KD - 1)
                    last.then_inc(c.k_ps.sem, 1)
                    pe.wait_ge(c.v_ready.sem, c.v_ready.at(it.n))
                    for j in range(KD):
                        for kd in range(KD):
                            nc.tensor.matmul(bank_v[:, D + j * S:D + (j + 1) * S],
                                             wq[:, kd, it.g * D + j * P:it.g * D + (j + 1) * P],
                                             xT[:, kd, :], start=kd == 0, stop=kd == KD - 1)
                    for kd in range(KD):
                        last = nc.tensor.matmul(bank_v[:, 0:D], kv_src[:, kd, :],
                                                wv[:, kd, it.g * D:(it.g + 1) * D],
                                                start=kd == 0, stop=kd == KD - 1)
                    last.then_inc(c.v_ps.sem, 1)

                def queries_and_keys(it, values_before):
                    pe.wait_ge(c.xT_ready.sem, c.xT_ready.at(it.b + 1))
                    pe.wait_ge(c.qk_ready.sem, c.qk_ready.at(2 * it.b))
                    pe.wait_ge(c.v_ready.sem, c.v_ready.at(values_before))
                    n = H * groups * dh
                    for a in range(2):
                        for kd in range(KD):
                            last = nc.tensor.matmul(bank_qk[a][:, :], hT[it.at // T % 2][:, kd, :],
                                                    rotary["wqkv"][:, kd, a * n:(a + 1) * n],
                                                    start=kd == 0, stop=kd == KD - 1)
                        last.then_inc(c.qk_ps.sem, 1)

                def value(it, keys_before):
                    pe.wait_ge(c.qk_ready.sem, c.qk_ready.at(2 * keys_before))
                    pe.wait_ge(c.v_ready.sem, c.v_ready.at(it.b))
                    n = H * groups * dh
                    for kd in range(KD):
                        last = nc.tensor.matmul(bank_qk[1][:, :], hT[it.at // T % 2][:, kd, :],
                                                rotary["wqkv"][:, kd, 2 * n:3 * n], start=kd == 0, stop=kd == KD - 1)
                    last.then_inc(c.vs_ps.sem, 1)

                def scores(it):
                    if it.first:
                        pe.wait_ge(c.q_ready.sem, c.q_ready.at(it.n + 1))
                    pe.wait_ge(c.km_ready.sem, c.km_ready.at(it.m + 1))
                    bank_read = c.p_ready if unmasked else c.e_ready
                    pe.wait_ge(bank_read.sem, bank_read.at(it.m - 1))
                    s = bank_s[it.at % 2]
                    qs, ks = q[it.group_at % 2], km[it.at % NK]
                    if it.g == lin_group:
                        for h in range(4):
                            last = nc.tensor.matmul(s[:, h * S:(h + 1) * S], ks[:, h, :], qs[:, it.t // 2, :],
                                                    start=True, stop=True)
                    elif dh == 16:
                        last = nc.tensor.matmul(s[:, :], qs[:, it.t // 2, :], ks[:, :, :].rearrange("p h k -> p (h k)"),
                                                start=True, stop=True)
                    else:
                        for j in range(KD):
                            last = nc.tensor.matmul(s[:, j * D:(j + 1) * D], qs[:, j, :],
                                                    ks[:, 2 * j:2 * j + 2, :].rearrange("p h k -> p (h k)"),
                                                    start=True, stop=True)
                    last.then_inc(c.s_ps.sem, 1)

                def transposes(it):
                    par = it.at % 2
                    if is_linear(it):
                        return
                    pe.wait_ge(c.p_ready.sem, c.p_ready.at(it.m + 1))
                    pe.wait_ge(c.pT_ready.sem, c.pT_ready.at(softmax_quads(it) - 1))
                    for h in range(4):
                        last = nc.tensor.transpose(bank_t[par][:, h * S:(h + 1) * S], Pr[it.at % NP][:, h, :],
                                                   c.ident[:, :])
                    last.then_inc(c.pt_ps.sem, 1)

                def values(it):
                    par = it.at % 2
                    if it.first:
                        pe.wait_ge(c.v_ready.sem, c.v_ready.at(it.n + 1 if own else it.b + 1))
                    if it.first:
                        pe.wait_ge(c.o_ready.sem, c.o_ready.at(it.n))
                    if is_linear(it):
                        weights_T = Pr[it.at % NP]
                        pe.wait_ge(c.p_ready.sem, c.p_ready.at(it.m + 1))
                    else:
                        weights_T = PT[par]
                        pe.wait_ge(c.pT_ready.sem, c.pT_ready.at(softmax_quads(it) + 1))
                    for h in range(4):
                        hh = 4 * it.t + h
                        vh = v[it.group_at % NV][:, hh, :] if own else v[it.at // T % NV][:, it.g * H + hh, :]
                        last = nc.tensor.matmul(bank_o[:, hh * (dh + 1):(hh + 1) * (dh + 1)], weights_T[:, h, :], vh,
                                                start=True, stop=True)
                    last.then_inc(c.pv_done.sem, 1)

                def output(it):
                    pe.wait_ge(c.o_ready.sem, c.o_ready.at(it.n + 1))
                    for j in range(KD):
                        last = nc.tensor.transpose(bank_m[:, j * S:(j + 1) * S], o[:, j * P:(j + 1) * P],
                                                   c.ident[:, :])
                    last.then_inc(c.ot_ps.sem, 1)

                def projection(it):
                    pe.wait_ge(c.oT_ready.sem, c.oT_ready.at(it.n + 1))
                    if it.g == 0:
                        pe.wait_ge(c.x_added.sem, c.x_added.at(it.b))
                        if arriving and isinstance(it.b, int) and it.b == 0:
                            loaded = c.part_loaded[groups]
                            pe.wait_ge(loaded.sem, loaded.at(16 * len(arriving[groups])))
                    for j in range(KD):
                        last = nc.tensor.matmul(bank_y[:, 0:D], oT[:, j, :], wo[:, it.g * KD + j, :],
                                                start=(it.g == 0 and j == 0),
                                                stop=(it.g == groups - 1 and j == KD - 1))
                    last.then_inc(c.y_ps.sem, 1)

                def body(i):
                    for step in range(pipe.span):
                        ot, qkv, x = (pipe.item(i, step, n) for n in ("ot", "qkv", "x"))
                        outs = lambda k: pipe.issued(i, k, "ot", quads, False)
                        ks = lambda k: pipe.issued(i, k, "qkv", quads, True)
                        xs = lambda k: pipe.issued(i, k, "x", T, True)
                        it = pipe.item(i, step, "y")
                        if not it.missing and it.last:
                            projection(it)
                        if not ot.missing and ot.last:
                            bank_m_free(outs(step), ks(step), xs(step))
                            output(ot)
                        it = pipe.item(i, step, "pv")
                        if not it.missing:
                            values(it)
                        it = pipe.item(i, step, "t")
                        if not it.missing:
                            transposes(it)
                        it = pipe.item(i, step, "s")
                        if not it.missing:
                            scores(it)
                        if not qkv.missing and qkv.first:
                            bank_m_free(outs(step + 1), ks(step), xs(step))
                            projected(qkv)
                        if rotary and not qkv.missing and qkv.g == 0:
                            value(qkv, pipe.issued(i, step, "qk", T, True))
                        if not x.missing and x.first and x.g == 0:
                            bank_m_free(outs(step + 1), ks(step + 1), xs(step))
                            normalised(x)
                        if rotary:
                            it = pipe.item(i, step, "qk")
                            if not it.missing and it.g == 0:
                                queries_and_keys(it, pipe.issued(i, step + 1, "qkv", T, True))

                pipe.run(pe, body)

            @block.sync
            def _(sp):
                prefetch(c, sp, following)
                if rotary:
                    with sp.Fori(0, B) as b:
                        sp.wait_ge(c.x_added.sem, c.x_added.at(b + 1))
                        shift_sequence(c, sp, into, rotary["shifted"], b)
                    sp.wait_ge(c.shifted.sem, c.shifted.at(16 * B))
                prefetched(c, sp, following)

    if rotary:
        c.passed(shifted=16 * B, chain_p=3 * B, chain_a=B, qk_ps=2 * B, qk_ready=2 * B, squared=B, summed=B, norm_ready=B,
                 q_turned=B, k_turned=B, vs_ps=B, v_ready=B)
    else:
        c.passed(v_ps=B * groups, v_ready=B * groups)
    c.passed(fetched=16 * len(following), v_set=1, chain_v=B * vector_steps, xn_ready=B,
             xt_ps=B, xT_ready=B, ctx_ready=B * ctx_kv, k_ps=B * groups, q_ready=B * groups, k_ready=B * groups,
             km_ready=B * T, s_ps=B * T, e_ready=B * T, p_ready=B * T, pt_ps=B * TS, pT_ready=B * TS, pv_done=B * T,
             o_ready=B * groups, ot_ps=B * groups, oT_ready=B * groups, y_ps=B * groups, x_added=B)


def per_head(ap):
    return ap.unsqueeze(1).to_broadcast([P, 4, S])


def no_mask(g, t, i):
    return None, None


def l0_attn_weights(c, w, W):
    W.add("wqkv", w["L0_attn_W_qkv"], P, KD, 3072)
    W.add("wo", w["L0_attn_W_out"], P, 8, D)
    W.parts = [[(W["wqkv"][:, :, cols], w["L0_attn_W_qkv"][:, :, cols])
                for cols in (slice(a * 1024 + g * D, a * 1024 + (g + 1) * D) for a in range(3))] for g in range(4)]
    W.parts.append([W.pairs[-1]])
    W.pairs = []


def l0_attn(c, W, following):
    layernorm(c)
    wqkv = W["wqkv"]
    attention(c, "l0a", 4, 1, 64, (wqkv[:, :, 0:1024], wqkv[:, :, 1024:2048], wqkv[:, :, 2048:3072], W["wo"]),
              q_scale=[0.125] * 4, mask_of=lambda g, t, i: (None, per_head(c.causal_add[:, :])), following=following,
              arriving=W.parts)


def l0_xattn_weights(c, w, W):
    W.pairs.append((c.ctxT[:, :, :], w["ctx_1024"]))
    W.add("wq", w["L0_xattn_Wq"], P, KD, 1024)
    W.add("wkv", w["L0_xattn_Wkv"], P, KD, 2048)
    W.add("wo", w["L0_xattn_Wout"], P, 8, D)
    W.add("bo", w["L0_xattn_bout"], P, D)


def l0_xattn(c, W, following):
    layernorm(c)
    wkv = W["wkv"]
    attention(c, "l0x", 4, 1, 64, (W["wq"], wkv[:, :, 0:1024], wkv[:, :, 1024:2048], W["wo"]), ctx_kv=True,
              q_scale=[0.125] * 4, y_bias=W["bo"], mask_of=no_mask, following=following)


def sixteen_heads_weights(w, W, matrices, q_bias=None, k_bias=None, v_bias=None, o_bias=None):
    for n, m in zip("qkvo", matrices):
        W.add("w" + n, w[m], P, KD, D)
    for n, m in (("qb", q_bias), ("kb", k_bias)):
        if m:
            W.add(n, w[m], P, KD)
    for n, m in (("vb", v_bias), ("ob", o_bias)):
        if m:
            W.add(n, w[m], P, D)


def matrices_of(W):
    return W["wq"], W["wk"], W["wv"], W["wo"]


def xattn_masked(c, W, name, fill, following):
    with ExitStack() as ctx:
        keep = c.sb(ctx, f"{name}_keep", [P, B, S])
        put = c.sb(ctx, f"{name}_put", [P, B, S])

        def masks(dve):
            c.nc.vector.tensor_scalar(keep[:, :, :], c.mask_int[:, :, :], 0.0, None, ALU.not_equal)
            c.nc.vector.tensor_scalar(put[:, :, :], c.mask_int[:, :, :], 0.0, fill, ALU.is_equal, ALU.mult)

        layernorm(c, beside=masks)
        attention(c, name, 1, 4, 16, matrices_of(W), ctx_kv=True, q_scale=[0.25], q_bias=W["qb"], k_bias=W["kb"],
                  v_bias=W["vb"], y_bias=W["ob"], mask_of=lambda g, t, i: (per_head(keep[:, i, :]), per_head(put[:, i, :])),
                  following=following)


def l1_xattn_weights(c, w, W):
    n = "L1_xattn_W"
    W.pairs.append((c.mask_int[:, :, :], w["mask_Bx1xSxS2_ik1"]))
    sixteen_heads_weights(w, W, [f"{n}{m}_w" for m in "QKVO"], *(f"{n}{m}_b" for m in "QKVO"))


def l1_xattn(c, W, following):
    xattn_masked(c, W, "l1x", 1e-9, following)


def l3_xattn_weights(c, w, W):
    n = "L3_xattn_"
    W.pairs.append((c.mask_int[:, :, :], w["mask_BxSxS2_if1"]))
    sixteen_heads_weights(w, W, [n + "W" + m for m in "qkvo"], *(n + "b" + m for m in "qkvo"))


def l3_xattn(c, W, following):
    xattn_masked(c, W, "l3x", -1e9, following)


def l2_xattn_weights(c, w, W):
    sixteen_heads_weights(w, W, ["L2_xattn_W" + n for n in "qkvo"])


def l2_xattn(c, W, following):
    layernorm(c)
    attention(c, "l2x", 1, 4, 16, matrices_of(W), ctx_kv=True, q_scale=[0.25], mask_of=no_mask, following=following)


def l3_attn_weights(c, w, W):
    n = "L3_attn_"
    sixteen_heads_weights(w, W, [n + "W" + m for m in "qkvo"], *(n + "b" + m for m in "qkvo"))
    W.add("alibi", w["alibi"], P, 16, S)


def l3_attn(c, W, following):
    layernorm(c)
    attention(c, "l3a", 1, 4, 16, matrices_of(W), q_scale=[0.25], q_bias=W["qb"], k_bias=W["kb"], v_bias=W["vb"],
              y_bias=W["ob"], mask_of=lambda g, t, i: (None, W["alibi"][:, 4 * t:4 * t + 4, :]), following=following)


def l1_attn_weights(c, w, W):
    a = "L1_attn_"
    for n in "qkv":
        dst = W.add("w" + n, w[a + "W" + n], P, KD, 2 * D)
        W.pairs[-1] = (dst[:, :, D:], w[a + "W" + n])
    W.pairs.append((dst[:, :, 0:D], w[a + "Wv"]))
    W.add("wo", w[a + "Wout"], P, 4, D)
    for n in "qk":
        W.add(f"w{n}T", w[f"{a}W{n}T"], P, KD, D)
        W.add(f"w{n}f", w[f"{a}W{n}f"], P, KD, D)
    W.add("norm_w", w[a + "norm_w"], P, KD)
    W.add("causal", w["causal_T"], P, S)
    W.add("minus2", w["minus2_T"], P, S)
    W.add("window", w["window_add"], P, S)


def l1_attn(c, W, following):
    nc = c.nc
    with ExitStack() as ctx:
        xin = c.sb(ctx, "l1a_xin", [P, B, D])
        layernorm(c)
        with nc.Block() as block:
            @block.tensor
            def _(pe):
                for a, n in enumerate("qk"):
                    for j in range(KD):
                        for m in range(KD):
                            last = nc.tensor.matmul(c.bank[a][:, j * D:(j + 1) * D], W[f"w{n}T"][:, m, j * P:(j + 1) * P],
                                                    W[f"w{n}f"][:, m, :], start=m == 0, stop=m == KD - 1)
                    last.then_inc(c.h_ps.sem, 1)

            @block.scalar
            def _(act):
                for a, dst in enumerate((W["wq"], W["wk"])):
                    act.wait_ge(c.h_ps.sem, c.h_ps.at(a + 1))
                    nc.scalar.copy(dst[:, :, 0:D], c.bank[a][:, :].rearrange("p (j n) -> p j n", j=KD))

            @block.vector
            def _(dve):
                skewed(dve, [(0, lambda i, p: nc.vector.tensor_scalar(
                    xin[:, i, :], c.x[:, i, :], c.mv[:, i, 0:1], c.rstd[:, bass.ds(i, 1)],
                    ALU.subtract, ALU.mult))], span=4)
        c.passed(h_ps=2)
        layernorm(c, rms_eps=1e-6)
        attention(c, "l1a", 2, 4, 16, matrices_of(W), norm_w=W["norm_w"], q_scale=[1.0, 0.25], lin_group=0, xin=xin,
                  mask_of=lambda g, t, i: ((per_head(W["causal"]), per_head(W["minus2"])) if g == 0
                                           else (None, per_head(W["window"]))), following=following)


def first_largest(nc, chain, vals, rev, mx, tmp, mask):
    bc = mx.unsqueeze(2).to_broadcast(list(vals.shape))
    chain(nc.vector.tensor_reduce(mx, vals, AX.X, ALU.max))
    chain(nc.vector.tensor_tensor(tmp, vals, bc, ALU.is_equal))
    chain(nc.vector.tensor_tensor(tmp, tmp, rev, ALU.mult))
    chain(nc.vector.tensor_reduce(mx, tmp, AX.X, ALU.max))
    chain(nc.vector.tensor_tensor(mask, tmp, bc, ALU.is_equal))


def router_constants(c, w, W, E):
    W.add("rev", w[f"rev{E}"], P, E)
    W.add("limits", w["block_limits"], P, MOST)


def route(c, name, E, wg, W, *, xnT=None, comb=None, dispatch=None, g_bias=None, hidden=None, renorm_eps=None,
          capacity=None):
    nc = c.nc
    layernorm(c)
    with ExitStack() as ctx:
        sb = lambda n, shape, dt=F32: c.sb(ctx, f"{name}_r_{n}", shape, dt)
        xn, xT = [sb(f"xn{i}", [P, D]) for i in range(2)], [sb(f"xT{i}", [P, KD, S]) for i in range(2)]
        lg, pr, tmp, m1, m2 = (sb(n, [P, B, E]) for n in ("lg", "pr", "tmp", "m1", "m2"))
        before, before2, place = sb("before", [P, 3, B + 1, E]), sb("before2", [P, 3, B + 1, E]), sb("place", [P, B, E])
        if dispatch:
            numbers, tokens = W["numbers"], W["tokens"]
            both, ge = sb("both", [P, B, E]), sb("ge", [P, E, dispatch.most])
            each = [sb(f"each{i}", [P, E]) for i in range(3)]
            slot = sb("slot", [P, B])
            digits_int, digits = sb("digits_int", [P, 2, 2 * B], I32), sb("digits", [P, 2, 2 * B])
            in_block, at_row = sb("in_block", [P, 2 * B, BLOCKS]), sb("at_row", [P, 2 * B, WIDTH])
        r = [sb(f"r{i}", [P, B]) for i in range(3)]
        rev, limits = W["rev"], W["limits"]
        hT = [sb(f"hT{i}", [64, S]) for i in range(2)] if hidden else None
        bank_x, bank_l, bank_h = c.bank[0:2], c.bank[2:4], c.bank[4:6]
        xT_used = c.h_ps if hidden else c.l_ps
        late = 1 if hidden else 0
        with nc.Block() as block:
            @block.vector
            def _(dve):
                def normalised(i, p):
                    dve.wait_ge(c.xt_ps.sem, c.xt_ps.at(i - 1))
                    if dispatch:
                        dve.wait_ge(c.xs_ready.sem, c.xs_ready.at(i - 1))
                    nc.vector.tensor_scalar(xn[p][:, :], c.x[:, i, :], c.mv[:, i, 0:1], c.rstd[:, bass.ds(i, 1)],
                                            ALU.subtract, ALU.mult).then_inc(c.xn_ready.sem, 1)

                def transposed(i, p):
                    dve.wait_ge(c.xt_ps.sem, c.xt_ps.at(i + 1))
                    dve.wait_ge(xT_used.sem, xT_used.at(i - 1))
                    if not dispatch:
                        dve.wait_ge(c.xs_ready.sem, c.xs_ready.at(i - 1))
                    nc.vector.tensor_copy(xT[p][:, :, :], bank_x[p][:, 0:D].rearrange("p (j t) -> p j t", j=KD))\
                        .then_inc(c.xT_ready.sem, 1)

                def logits(i, p):
                    dve.wait_ge(c.l_ps.sem, c.l_ps.at(i + 1))
                    nc.vector.tensor_copy(lg[:, i, :], bank_l[p][:, 0:E]).then_inc(c.l_ready.sem, 1)

                skewed(dve, [(0, normalised), (1, transposed), (3 + late, logits)])

            @block.tensor
            def _(pe):
                def transposes(i, p):
                    pe.wait_ge(c.xn_ready.sem, c.xn_ready.at(i + 1))
                    pe.wait_ge(c.xT_ready.sem, c.xT_ready.at(i - 1))
                    for j in range(KD):
                        last = nc.tensor.transpose(bank_x[p][:, j * S:(j + 1) * S], xn[p][:, j * P:(j + 1) * P],
                                                   c.ident[:, :])
                    last.then_inc(c.xt_ps.sem, 1)

                def hiddens(i, p):
                    pe.wait_ge(c.xT_ready.sem, c.xT_ready.at(i + 1))
                    pe.wait_ge(c.h_ready.sem, c.h_ready.at(i - 1))
                    for j in range(KD):
                        last = nc.tensor.matmul(bank_h[p][0:64, 0:S], hidden[0][:, j, :], xT[p][:, j, :],
                                                start=j == 0, stop=j == KD - 1)
                    last.then_inc(c.h_ps.sem, 1)

                def logits(i, p):
                    pe.wait_ge(c.l_ready.sem, c.l_ready.at(i - 1))
                    if hidden:
                        pe.wait_ge(c.h_ready.sem, c.h_ready.at(i + 1))
                        last = nc.tensor.matmul(bank_l[p][:, 0:E], hT[p][:, :], wg[:, 0:E], start=True, stop=True)
                    else:
                        pe.wait_ge(c.xT_ready.sem, c.xT_ready.at(i + 1))
                        for j in range(KD):
                            last = nc.tensor.matmul(bank_l[p][:, 0:E], xT[p][:, j, :], wg[:, j, :],
                                                    start=j == 0, stop=j == KD - 1)
                    last.then_inc(c.l_ps.sem, 1)

                skewed(pe, [(1, transposes)] + ([(2, hiddens)] if hidden else []) + [(2 + late, logits)])

            if hidden:
                @block.scalar
                def _(act):
                    def gelus(i, p):
                        act.wait_ge(c.h_ps.sem, c.h_ps.at(i + 1))
                        act.wait_ge(c.l_ps.sem, c.l_ps.at(i - 1))
                        nc.scalar.activation(hT[p][:, :], bank_h[p][0:64, 0:S], ACT.Gelu, bias=hidden[1][:, 0:1])\
                            .then_inc(c.h_ready.sem, 1)

                    skewed(act, [(0, gelus)])

            @block.gpsimd
            def _(pool):
                def kept(i, p):
                    if dispatch:
                        pool.wait_ge(c.xn_ready.sem, c.xn_ready.at(i + 1))
                        nc.gpsimd.tensor_copy(dispatch.xn[:, i, :], xn[p][:, :]).then_inc(c.xs_ready.sem, 1)
                    else:
                        pool.wait_ge(c.xT_ready.sem, c.xT_ready.at(i + 1))
                        nc.gpsimd.tensor_copy(token_tile(xnT, i), xT[p][:, :, :]).then_inc(c.xs_ready.sem, 1)

                skewed(pool, [(0, kept)])
        c.passed(xn_ready=B, xt_ps=B, xT_ready=B, l_ps=B, l_ready=B, h_ps=B * bool(hidden), h_ready=B * bool(hidden),
                 xs_ready=B)

        steps = []
        full = lambda a: a.unsqueeze(2).to_broadcast([P, B, E])
        with nc.Block() as block:
            @block.vector
            def _(dve):
                chain = Chain(dve, c.chain_v, 0)
                v = nc.vector
                L, Q, W, M1, M2 = (a[:, :, :] for a in (lg, pr, tmp, m1, m2))
                R = [a[:, :] for a in r]
                rv = rev[:, :].unsqueeze(1).to_broadcast([P, B, E])
                if g_bias is not None:
                    chain(v.tensor_tensor(L, L, g_bias.unsqueeze(1).to_broadcast([P, B, E]), ALU.add))
                chain(v.tensor_reduce(R[0], L, AX.X, ALU.max))
                v.tensor_tensor(Q, L, full(R[0]), ALU.subtract).then_inc(c.e_ready.sem, 1)
                dve.wait_ge(c.p_ready.sem, c.p_ready.at(1))
                chain(v.tensor_reduce(R[0], Q, AX.X, ALU.add))
                chain(v.reciprocal(R[1], R[0]))
                chain(v.tensor_tensor(Q, Q, full(R[1]), ALU.mult))
                vals = L if capacity else Q
                first_largest(nc, chain, vals, rv, R[0], W, M1)
                chain(v.scalar_tensor_tensor(out=L, in0=M1, scalar=NEG if capacity else -4.0, in1=vals,
                                             op0=ALU.mult, op1=ALU.add))
                first_largest(nc, chain, L, rv, R[0], W, M2)
                if renorm_eps is not None:
                    chain(v.tensor_tensor(W, M1, M2, ALU.add))
                    chain(v.tensor_tensor(W, W, Q, ALU.mult))
                    chain(v.tensor_reduce(R[0], W, AX.X, ALU.add))
                    chain(v.tensor_scalar(R[0], R[0], renorm_eps, None, ALU.add))
                    chain(v.reciprocal(R[1], R[0]))
                    chain(v.tensor_tensor(Q, Q, full(R[1]), ALU.mult))
                sets = [None, M1, M2]
                sets_used = 3 if capacity else 1
                used = ([0] if dispatch else []) + ([1, 2] if capacity else [])
                if dispatch:
                    sets[0] = both[:, :, :]
                    chain(v.tensor_tensor(sets[0], M1, M2, ALU.add))
                if used:
                    chain(v.memset(before[:, :, 0, :], 0.0))
                    v.tensor_copy(W, M1).then_inc(c.a_ready.sem, 1)
                    dve.wait_ge(c.c_ps.sem, c.c_ps.at(1))
                    dve.wait_ge(c.a_ready.sem, c.a_ready.at(1))
                    for a in used:
                        last = v.tensor_copy(before[:, a, 1:, :],
                                             c.bank[5 + a][:, 0:B * E].rearrange("p (b e) -> p b e", b=B))
                    chain(last)
                    src, dst, d = before, before2, 1
                    while d < B:
                        v.tensor_copy(dst[:, 0:sets_used, 0:d, :], src[:, 0:sets_used, 0:d, :])
                        chain(v.tensor_tensor(dst[:, 0:sets_used, d:, :], src[:, 0:sets_used, d:, :],
                                              src[:, 0:sets_used, 0:B + 1 - d, :], ALU.add))
                        src, dst, d = dst, src, 2 * d
                    if capacity:
                        chain(v.tensor_tensor(before[:, 2, :, :], before[:, 2, :, :],
                                              before[:, 1, B, :].unsqueeze(1).to_broadcast([P, B + 1, E]), ALU.add))
                if dispatch:
                    count, blocks, start = before[:, 0, B, :], each[0][:, :], each[1][:, :]
                    chain(v.tensor_tensor(ge[:, :, :], count.unsqueeze(2).to_broadcast([P, E, dispatch.most]),
                                          limits[:, :].unsqueeze(1).to_broadcast([P, E, dispatch.most]), ALU.is_gt))
                    chain(v.tensor_reduce(blocks, ge[:, :, :], AX.X, ALU.add))
                    chain(v.memset(each[2][:, :], 1.0))
                    chain(v.tensor_tensor_scan(start, each[2][:, :], blocks, 0.0, ALU.mult, ALU.add))
                    v.tensor_copy(dispatch.ends[:, :], start).then_inc(c.ended.sem, 1)
                    dve.wait_ge(c.ended.sem, c.ended.at(1))
                    chain(v.tensor_tensor(start, start, blocks, ALU.subtract))
                    chain(v.tensor_scalar(start, start, float(dispatch.width), None, ALU.mult))
                    within = c.bank[2][:, 0:B * E].rearrange("p (b e) -> p b e", b=B)
                    chain(v.tensor_tensor(place[:, :, :], within, before[:, 0, 0:B, :], ALU.add))
                    chain(v.tensor_tensor(place[:, :, :], place[:, :, :],
                                          start.unsqueeze(1).to_broadcast([P, B, E]), ALU.add))
                    for a, M in enumerate((M1, M2)):
                        chain(v.tensor_tensor(W, place[:, :, :], M, ALU.mult))
                        chain(v.tensor_reduce(slot[:, :], W, AX.X, ALU.add))
                        chain(v.tensor_copy(dispatch.slot[:, a, :], slot[:, :]))
                    place_int = dispatch.slot[:, :, :].rearrange("p a b -> p (a b)")
                    by = lambda m, n: m.unsqueeze(2).to_broadcast([P, 2 * B, n])
                    number = numbers.unsqueeze(1)
                    v.tensor_scalar(digits_int[:, 0, :], place_int, WIDTH.bit_length() - 1, None, ALU.arith_shift_right)
                    chain(v.tensor_scalar(digits_int[:, 1, :], place_int, WIDTH - 1, None, ALU.bitwise_and))
                    chain(v.tensor_copy(digits[:, :, :], digits_int[:, :, :]))
                    chain(v.tensor_tensor(in_block[:, :, :], by(digits[:, 0, :], BLOCKS),
                                          number[:, :, 0:BLOCKS].to_broadcast([P, 2 * B, BLOCKS]), ALU.is_equal))
                    chain(v.tensor_tensor(in_block[:, :, :], in_block[:, :, :], by(tokens, BLOCKS), ALU.mult))
                    for part in range(LIST_PARTS):
                        n = 2 * B // LIST_PARTS
                        of = slice(part * n, (part + 1) * n)
                        v.tensor_tensor(at_row[:, of, :], digits[:, 1, of].unsqueeze(2).to_broadcast([P, n, WIDTH]),
                                        number.to_broadcast([P, n, WIDTH]), ALU.is_equal).then_inc(c.placed.sem, 1)
                if capacity:
                    for a, M in ((1, M1), (2, M2)):
                        within = c.bank[2 + a][:, 0:B * E].rearrange("p (b e) -> p b e", b=B)
                        chain(v.tensor_tensor(place[:, :, :], within, before[:, a, 0:B, :], ALU.add))
                        chain(v.tensor_scalar(place[:, :, :], place[:, :, :], float(capacity), None, ALU.is_lt))
                        chain(v.tensor_tensor(M, M, place[:, :, :], ALU.mult))
                if dispatch:
                    for a, M in enumerate((M1, M2)):
                        chain(v.tensor_tensor(W, Q, M, ALU.mult))
                        chain(v.tensor_reduce(dispatch.weight[:, a, :], W, AX.X, ALU.add))
                else:
                    chain(v.tensor_tensor(W, M1, M2, ALU.add))
                    chain(v.tensor_tensor(comb[:, :, :], Q, W, ALU.mult))
                steps.append(chain.n)
                if dispatch:
                    dispatch.read_ends("dve", dve)
                    dve.wait_ge(c.listed.sem, c.listed.at(1))
                    v.tensor_copy(dispatch.tokens[:, :], c.bank[1][:, 0:BLOCKS])

            @block.scalar
            def _(act):
                act.wait_ge(c.e_ready.sem, c.e_ready.at(1))
                nc.scalar.activation(pr[:, :, :], pr[:, :, :], ACT.Exp).then_inc(c.p_ready.sem, 1)
                if dispatch:
                    act.wait_ge(c.ended.sem, c.ended.at(1))
                    dispatch.read_ends("act", act)

            if dispatch:
                @block.sync
                def _(sp):
                    for s in dispatch.own.values():
                        sp.sem_inc(s.sem, START)
                    sp.dma_start(c.xn_rows.rearrange("(b p) d -> p b d", p=P), dispatch.xn[:, :, :])\
                        .then_inc(c.kept.sem, 16)
                    sp.wait_ge(c.kept.sem, c.kept.at(16))

            counted = bool(capacity or dispatch)
            if counted:
                @block.tensor
                def _(pe):
                    pe.wait_ge(c.a_ready.sem, c.a_ready.at(1))
                    for a, m in ([(0, both)] if dispatch else []) + ([(1, m1), (2, m2)] if capacity else []):
                        flat = m[:, :, :].rearrange("p b e -> p (b e)")
                        nc.tensor.matmul(c.bank[2 + a][:, 0:B * E], c.earlier[:, :], flat, start=True, stop=True)
                        last = nc.tensor.matmul(c.bank[5 + a][:, 0:B * E], c.ones[:, :], flat, start=True, stop=True)
                    last.then_inc(c.c_ps.sem, 1)
                    if dispatch:
                        pe.wait_ge(c.ended.sem, c.ended.at(1))
                        dispatch.read_ends("pe", pe)
                        for i in range(2 * B):
                            pe.wait_ge(c.placed.sem, c.placed.at(i * LIST_PARTS // (2 * B) + 1))
                            last = nc.tensor.matmul(c.bank[1][:, 0:BLOCKS], at_row[:, i, :], in_block[:, i, :],
                                                    start=i == 0, stop=i == 2 * B - 1)
                        last.then_inc(c.listed.sem, 1)
        c.passed(e_ready=1, p_ready=1, chain_v=steps[0], a_ready=counted, c_ps=counted, placed=LIST_PARTS * bool(dispatch),
                 ended=bool(dispatch),
                 listed=bool(dispatch), kept=16 * bool(dispatch))


class Dispatch:

    def __init__(self, c, ctx, name):
        sb = lambda n, shape, dt=F32: c.sb(ctx, f"{name}_{n}", shape, dt)
        self.width, self.most = WIDTH, MOST
        self.rows = sb("rows", [P, BLOCKS, D])
        self.xn = self.rows[:, 0:B, :]
        self.slot, self.weight = sb("slots", [P, 2, B], I32), sb("weights", [P, 2, B])
        self.ends, self.tokens = sb("ends", [P, 8], I32), sb("tokens", [P, BLOCKS], I32)
        self.in_registers = {}
        self.own = {n: Signal(ctx.enter_context(c.nc.semaphore(f"s_{name}_{n}")))
                    for n in ("x", "xt", "xT", "hps", "h", "yps", "y", "out")}

    def read_ends(self, engine, eng):
        self.in_registers[engine] = [0] + [eng.value_load(self.ends[0:1, e:e + 1], min_val=e + 1,
                                                          max_val=ROWS // WIDTH) for e in range(8)]


def expert_weights(c, w, W, name, g_bias):
    F = 1024
    router_constants(c, w, W, 8)
    W.add("numbers", w["numbers"], P, WIDTH)
    W.add("tokens", w["tokens"], P, 2 * B)
    W.add("wg", w[name + "_Wg"], P, KD, 8)
    W.add("b1", w[name + "_b1"], P, 8, F // P)
    W.add("b2", w[name + "_b2"], P, 8, D)
    for e in range(2):
        W.add(f"w1_{e}", w[name + "_W1"][e], P, KD, F)
        W.add(f"w2_{e}", w[name + "_W2"][e], P, F // P, D)
    if g_bias:
        W.add("g_bias", w[name + "_bg"], P, 8)


def expert_mlps(c, name, W, following, gelu, capacity, renorm_eps, g_bias):
    nc, E, F = c.nc, 8, 1024
    FC = F // P
    w = c.w
    with ExitStack() as ctx:
        sb = lambda n, shape: c.sb(ctx, f"{name}_{n}", shape)
        wg, b1, b2 = W["wg"], W["b1"], W["b2"]
        d = Dispatch(c, ctx, name)
        w1, w2 = ([W[f"w{a}_{e}"] for e in range(2)] for a in (1, 2))
        own = d.own
        x_in, xt_ps, xT_ready, h_ps = own["x"], own["xt"], own["xT"], own["hps"]
        h_ready, y_ps, y_ready, y_out = own["h"], own["yps"], own["y"], own["out"]
        route(c, name, E, wg, W, dispatch=d, g_bias=W["g_bias"] if g_bias else None, renorm_eps=renorm_eps,
              capacity=capacity)
        xs, xT = sb("xs", [P, D]), sb("xT", [P, KD, WIDTH])
        hT, ys = sb("hT", [P, FC, WIDTH]), sb("ys", [P, D])
        got = [[sb(f"got{a}{i}", [P, D]) for i in range(DEEP)] for a in range(2)]
        bank_x, banks_h, bank_y = c.bank[0], c.bank[1:5], c.bank[5]

        ends = d.in_registers
        with nc.Block() as block:
            @block.sync
            def _(sp):
                prefetch(c, sp, following)
                prefetched(c, sp, following)

            @block.tensor
            def _(pe):
                def transposes():
                    for kd in range(KD):
                        last = nc.tensor.transpose(bank_x[:, kd * WIDTH:(kd + 1) * WIDTH], xs[:, kd * P:(kd + 1) * P],
                                                   c.ident[:, :])
                    last.then_inc(xt_ps.sem, 1)

                pe.wait_ge(x_in.sem, x_in.at(1))
                transposes()
                for e in range(E):
                    with pe.Fori(ends["pe"][e], ends["pe"][e + 1]) as k:
                        if e >= 2:
                            pe.wait_ge(c.w_loaded[e % 2].sem, c.w_loaded[e % 2].at(32 * (e // 2)))
                        pe.wait_ge(xT_ready.sem, xT_ready.at(k + 1))
                        for f in range(FC):
                            pe.wait_ge(h_ready.sem, h_ready.at(k * FC + f - 3))
                            for kd in range(KD):
                                last = nc.tensor.matmul(banks_h[f % 4][:, 0:WIDTH], w1[e % 2][:, kd, f * P:(f + 1) * P],
                                                        xT[:, kd, :], start=kd == 0, stop=kd == KD - 1)
                            last.then_inc(h_ps.sem, 1)
                        pe.wait_ge(x_in.sem, x_in.at(k + 2))
                        transposes()
                        pe.wait_ge(y_ready.sem, y_ready.at(k))
                        for f in range(FC):
                            pe.wait_ge(h_ready.sem, h_ready.at(k * FC + f + 1))
                            last = nc.tensor.matmul(bank_y[:, 0:D], hT[:, f, :], w2[e % 2][:, f, :],
                                                    start=f == 0, stop=f == FC - 1)
                        last.then_inc(y_ps.sem, 1)

            @block.scalar
            def _(act):
                for e in range(E):
                    if 1 <= e < E - 1:
                        act.wait_ge(y_ps.sem, y_ps.at(ends["act"][e]))
                        act.dma_start(w1[(e + 1) % 2], w[name + "_W1"][e + 1]).then_inc(c.w_loaded[(e + 1) % 2].sem, 16)
                        act.dma_start(w2[(e + 1) % 2], w[name + "_W2"][e + 1]).then_inc(c.w_loaded[(e + 1) % 2].sem, 16)
                    with act.Fori(ends["act"][e], ends["act"][e + 1]) as k:
                        for f in range(FC):
                            act.wait_ge(h_ps.sem, h_ps.at(k * FC + f + 1))
                            if f == 0:
                                act.wait_ge(y_ps.sem, y_ps.at(k))
                            nc.scalar.activation(hT[:, f, :], banks_h[f % 4][:, 0:WIDTH], gelu,
                                                 bias=b1[:, e, f:f + 1]).then_inc(h_ready.sem, 1)
                        act.wait_ge(y_ready.sem, y_ready.at(k + 1))
                        act.dma_start(c.rows_out[bass.ds(k * WIDTH, WIDTH), :], ys[:, :]).then_inc(y_out.sem, 16)

            @block.vector
            def _(dve):
                def staged(k):
                    dve.wait_ge(c.fetched_rows.sem, c.fetched_rows.at(16 * (k + 1)))
                    nc.vector.tensor_copy(xs[:, :], d.rows[:, k, :]).then_inc(x_in.sem, 1)

                def transposed(k):
                    dve.wait_ge(xt_ps.sem, xt_ps.at(k + 1))
                    nc.vector.tensor_copy(xT[:, :, :], bank_x[:, 0:D].rearrange("p (k t) -> p k t", k=KD))\
                        .then_inc(xT_ready.sem, 1)

                staged(0)
                transposed(0)
                for e in range(E):
                    with dve.Fori(ends["dve"][e], ends["dve"][e + 1]) as k:
                        staged(k + 1)
                        transposed(k + 1)
                        dve.wait_ge(y_out.sem, y_out.at(k * 16))
                        dve.wait_ge(y_ps.sem, y_ps.at(k + 1))
                        nc.vector.tensor_tensor(ys[:, :], bank_y[:, 0:D], b2[:, e, :], ALU.add).then_inc(y_ready.sem, 1)
                for b in range(B):
                    dve.wait_ge(c.gathered[b % DEEP].sem, c.gathered[b % DEEP].at(32 * (b // DEEP + 1)))
                    for a in range(2):
                        dve.wait_ge(c.x_added.sem, c.x_added.at(2 * b + a))
                        nc.vector.scalar_tensor_tensor(out=c.x[:, b, :], in0=got[a][b % DEEP][:, :],
                                                       scalar=d.weight[:, a, b:b + 1], in1=c.x[:, b, :],
                                                       op0=ALU.mult, op1=ALU.add).then_inc(c.x_added.sem, 1)
                    dve.wait_ge(c.x_added.sem, c.x_added.at(2 * b + 2))
                    nc.vector.bn_stats(c.stats[:, b, 0, :], c.x[:, b, :])

            @block.gpsimd
            def _(pool):
                for k in range(BLOCKS):
                    nc.gpsimd.indirect_dma_start(
                        out=d.rows[:, k, :], out_offset=None, in_=c.xn_rows[:, :],
                        in_offset=bass.IndirectOffsetOnAxis(ap=d.tokens[:, k:k + 1], axis=0))\
                        .then_inc(c.fetched_rows.sem, 16)
                    pool.wait_ge(c.fetched_rows.sem, c.fetched_rows.at(16 * (k + 1)))
                pool.wait_ge(c.cleared.sem, c.cleared.at(0))
                total = pool.value_load(d.ends[0:1, E - 1:E], min_val=E, max_val=ROWS // WIDTH)
                pool.wait_ge(y_out.sem, y_out.at(total * 16))
                pool.sem_inc(c.chain_p.sem, 1)
                pool.wait_ge(c.chain_p.sem, c.chain_p.at(1))
                for b in range(B):
                    if b >= DEEP:
                        pool.wait_ge(c.x_added.sem, c.x_added.at(2 * (b - DEEP + 1)))
                    for a in range(2):
                        nc.gpsimd.indirect_dma_start(
                            out=got[a][b % DEEP][:, :], out_offset=None, in_=c.rows_out[:, :],
                            in_offset=bass.IndirectOffsetOnAxis(ap=d.slot[:, a, b:b + 1], axis=0))\
                            .then_inc(c.gathered[b % DEEP].sem, 16)

        c.passed(x_added=2 * B, chain_p=1, fetched_rows=16 * BLOCKS, fetched=16 * len(following))
        for s in c.gathered:
            s.passed(32 * B // DEEP)
        for s in c.w_loaded:
            s.passed(16 * (E - 2))


def l0_ffn_weights(c, w, W):
    expert_weights(c, w, W, "L0_ffn", True)


def l0_ffn(c, W, following):
    expert_mlps(c, "L0_ffn", W, following, ACT.Gelu_apprx_tanh, None, 1e-8, True)


def l1_ffn_weights(c, w, W):
    expert_weights(c, w, W, "L1_ffn", False)


def l1_ffn(c, W, following):
    expert_mlps(c, "L1_ffn", W, following, ACT.Gelu, 2 * 2 * B * S // 8, 1e-9, False)


def l2_ffn_weights(c, w, W):
    E = 20
    router_constants(c, w, W, E)
    W.add("wg1", w["L2_ffn_wg1"], P, KD, 64)
    W.add("bg1", w["L2_ffn_bg1"], 64, 1)
    W.add("wg2", w["L2_ffn_wg2"], 64, 2 * E)
    W.add("bg2", w["L2_ffn_bg2"], P, E)
    W.add("be", w["L2_ffn_be"], E, D)
    W.add("we", w["L2_ffn_We"], P, KD, E, D)


def l2_ffn(c, W, following):
    nc, E = c.nc, 20
    with ExitStack() as ctx:
        sb = lambda n, shape: c.sb(ctx, f"l2f_{n}", shape)
        xnT, comb = sb("xnT", [P, KD, B * S]), sb("comb", [P, B, E])
        we = W["we"]
        xs, cs, cT = sb("xs", [P, KD, S]), sb("cs", [P, E]), sb("cT", [E, S])
        route(c, "l2f", E, W["wg2"], W, xnT=xnT, comb=comb, g_bias=W["bg2"], hidden=(W["wg1"], W["bg1"]))
        PAIRS = E // 2
        banks, bank_c, bank_b = c.bank[0:5], c.bank[5], c.bank[6]
        with nc.Block() as block:
            @block.gpsimd
            def _(pool):
                with pool.Fori(0, B) as i:
                    pool.wait_ge(c.cT_ps.sem, c.cT_ps.at(i))
                    nc.gpsimd.tensor_copy(cs[:, :], comb[:, i, :])
                    pool.wait_ge(c.y_ps.sem, c.y_ps.at(i * PAIRS))
                    nc.gpsimd.tensor_copy(xs[:, :, :], token_tile(xnT, i)).then_inc(c.xs_ready.sem, 1)

            @block.scalar
            def _(act):
                with act.Fori(0, B) as i:
                    act.wait_ge(c.cT_ps.sem, c.cT_ps.at(i + 1))
                    act.wait_ge(c.b_ps.sem, c.b_ps.at(i))
                    nc.scalar.copy(cT[:, :], bank_c[0:E, 0:S]).then_inc(c.cT_ready.sem, 1)

            @block.tensor
            def _(pe):
                with pe.Fori(0, B) as i:
                    pe.wait_ge(c.xs_ready.sem, c.xs_ready.at(i + 1))
                    nc.tensor.transpose(bank_c[0:E, 0:S], cs[:, :], c.ident[:, :]).then_inc(c.cT_ps.sem, 1)
                    for e in range(PAIRS):
                        pe.wait_ge(c.x_added.sem, c.x_added.at(2 * (i * PAIRS + e - 4)))
                        for kd in range(KD):
                            last = nc.tensor.matmul(banks[e % 5][:, :], xs[:, kd, :],
                                                    we[:, kd, 2 * e:2 * e + 2, :].rearrange("p a n -> p (a n)"),
                                                    start=kd == 0, stop=kd == KD - 1)
                        last.then_inc(c.y_ps.sem, 1)
                    pe.wait_ge(c.cT_ready.sem, c.cT_ready.at(i + 1))
                    pe.wait_ge(c.b_added.sem, c.b_added.at(i))
                    nc.tensor.matmul(bank_b[:, 0:D], cT[:, :], W["be"], start=True, stop=True).then_inc(c.b_ps.sem, 1)

            @block.vector
            def _(dve):
                with dve.Fori(0, B) as i:
                    for e in range(E):
                        dve.wait_ge(c.y_ps.sem, c.y_ps.at(i * PAIRS + e // 2 + 1))
                        dve.wait_ge(c.x_added.sem, c.x_added.at(i * E + e))
                        nc.vector.scalar_tensor_tensor(out=c.x[:, i, :],
                                                       in0=banks[e // 2 % 5][:, (e % 2) * D:(e % 2 + 1) * D],
                                                       scalar=comb[:, i, e:e + 1], in1=c.x[:, i, :],
                                                       op0=ALU.mult, op1=ALU.add).then_inc(c.x_added.sem, 1)
                    dve.wait_ge(c.x_added.sem, c.x_added.at((i + 1) * E))
                    dve.wait_ge(c.b_ps.sem, c.b_ps.at(i + 1))
                    nc.vector.tensor_tensor(c.x[:, i, :], c.x[:, i, :], bank_b[:, 0:D], ALU.add)\
                        .then_inc(c.b_added.sem, 1)
                    dve.wait_ge(c.b_added.sem, c.b_added.at(i + 1))
                    nc.vector.bn_stats(c.stats[:, i, 0, :], c.x[:, i, :])

            @block.sync
            def _(sp):
                prefetch(c, sp, following)
                prefetched(c, sp, following)
        c.passed(xs_ready=B, y_ps=B * PAIRS, x_added=B * E, cT_ps=B, cT_ready=B, b_ps=B, b_added=B,
                 fetched=16 * len(following))


def l2_attn_weights(c, w, W):
    W.add("win", w["L2_attn_W_in"], P, KD, 3 * D)
    W.add("wo", w["L2_attn_W_out"], P, KD, D)
    W.add("beta", w["chebyshev_beta"], P, CHEBYSHEV, 16)


def chebyshev_beta():
    j = np.arange(CHEBYSHEV + 1, dtype=np.float32)
    tail = np.flip(np.cumsum(np.flip((j + 1.0) ** (-1.5))))
    beta = tail[1:].astype(np.float32)
    return beta / beta.sum()


def l2_attn(c, W, following):
    nc, NP, H, WD = c.nc, CHEBYSHEV, 16, D + 16
    beta = chebyshev_beta()
    lo, hi = -1.0 + 1e-6, 1.0 - 1e-6
    KA, KO = 4, 4
    with ExitStack() as ctx:
        sb = lambda n, shape: c.sb(ctx, f"l2a_{n}", shape)
        win, wo = W["win"], W["wo"]
        xn, xT = sb("xn", [P, D]), [sb(f"xT{i}", [P, KD, S]) for i in range(2)]
        v = sb("v", [P, D])
        T = [sb(f"T{i}", [P, 2, NP, WD]) for i in range(2)]
        R, CS = sb("R", [P, NP * WD]), sb("CS", [P, NP, WD])
        s8, s4, s2 = (sb(f"s{n}", [P, 2 * NP, H, n]) for n in (8, 4, 2))
        square, tmp = sb("square", [P, 2, D]), sb("tmp", [P, 2, D])
        nd, rden, minus1 = sb("nd", [P, WD]), sb("rden", [P, H]), sb("minus1", [P, 1])
        o, oT = sb("o", [P, D]), sb("oT", [P, KD, S])
        bank_x, bank_qk, bank_v, bank_c, bank_o, bank_y = c.bank[0], c.bank[1], c.bank[2], c.bank[3:6], c.bank[6], c.bank[7]
        layernorm(c)
        with nc.Block() as block:
            @block.vector
            def _(dve):
                v_ = nc.vector

                def normalised(i, p):
                    dve.wait_ge(c.xt_ps.sem, c.xt_ps.at(i))
                    v_.tensor_scalar(xn[:, :], c.x[:, i, :], c.mv[:, i, 0:1], c.rstd[:, bass.ds(i, 1)],
                                     ALU.subtract, ALU.mult).then_inc(c.xn_ready.sem, 1)

                def first_order(i, p):
                    x1 = T[p][:, :, 0, 0:D]
                    dve.wait_ge(c.k_ps.sem, c.k_ps.at(i + 1))
                    Chain(dve, c.chain_v, i * KA)(v_.tensor_scalar(
                        x1, bank_qk[:, :].rearrange("p (a n) -> p a n", a=2), 0.25, hi, ALU.mult, ALU.min))
                    v_.tensor_scalar(x1, x1, lo, None, ALU.max).then_inc(c.k_ready.sem, 1)

                def odd_orders(i, p):
                    chain = Chain(dve, c.chain_v, i * KA + 1)
                    order = lambda n: T[p][:, :, n - 1, 0:D]
                    dve.wait_ge(c.k_ready.sem, c.k_ready.at(i + 1))
                    dve.wait_ge(c.e_ready.sem, c.e_ready.at(2 * i + 1))
                    chain(v_.scalar_tensor_tensor(out=tmp[:, :, :], in0=order(1), scalar=2.0, in1=order(2),
                                                  op0=ALU.mult, op1=ALU.mult))
                    chain(v_.tensor_tensor(order(3), tmp[:, :, :], order(1), ALU.subtract))
                    dve.wait_ge(c.e_ready.sem, c.e_ready.at(2 * i + 2))
                    chain(v_.scalar_tensor_tensor(out=tmp[:, :, :], in0=order(1), scalar=2.0, in1=order(4),
                                                  op0=ALU.mult, op1=ALU.mult))
                    v_.tensor_tensor(order(5), tmp[:, :, :], order(3), ALU.subtract).then_inc(c.a_ready.sem, 1)
                    dve.wait_ge(c.a_ready.sem, c.a_ready.at(i + 1))
                    dve.wait_ge(c.v_ready.sem, c.v_ready.at(i + 1))
                    dve.wait_ge(c.c_ps.sem, c.c_ps.at(i))
                    v_.tensor_tensor(R[:, 0:NP * D].rearrange("p (n f) -> p n f", n=NP), T[p][:, 1, :, 0:D],
                                     v[:, :].unsqueeze(1).to_broadcast([P, NP, D]), ALU.mult).then_inc(c.h_ready.sem, 1)

                def summed(i, p):
                    chain = Chain(dve, c.chain_o, i * KO)
                    dve.wait_ge(c.c_ready.sem, c.c_ready.at(i + 1))
                    dve.wait_ge(c.km_ready.sem, c.km_ready.at(i + 1))
                    dve.wait_ge(c.o_ready.sem, c.o_ready.at(i))
                    TQ = T[p][:, 0, :, :]
                    chain(v_.tensor_tensor(TQ, TQ, CS[:, :, :], ALU.mult))
                    chain(v_.tensor_reduce(nd[:, :], TQ.rearrange("p n f -> p f n"), AX.X, ALU.add))
                    chain(v_.tensor_scalar(nd[:, D:WD], nd[:, D:WD], 1e-7, None, ALU.add))
                    chain(v_.reciprocal(rden[:, :], nd[:, D:WD]))

                def output(i, p):
                    dve.wait_ge(c.ot_ps.sem, c.ot_ps.at(i))
                    v_.tensor_tensor(heads_of(o[:, :], H), heads_of(nd[:, 0:D], H),
                                     rden[:, :].unsqueeze(2).to_broadcast([P, H, 16]), ALU.mult)\
                        .then_inc(c.o_ready.sem, 1)

                def residual(i, p):
                    dve.wait_ge(c.y_ps.sem, c.y_ps.at(i + 1))
                    v_.tensor_tensor(c.x[:, i, :], c.x[:, i, :], bank_y[:, 0:D], ALU.add).then_inc(c.x_added.sem, 1)

                def statistics(i, p):
                    dve.wait_ge(c.x_added.sem, c.x_added.at(i + 1))
                    v_.bn_stats(c.stats[:, i, 0, :], c.x[:, i, :])

                skewed(dve, [(1, first_order), (3, output), (0, normalised), (4, residual), (4, statistics),
                             (1, odd_orders), (2, summed)])

            @block.gpsimd
            def _(pool):
                g = nc.gpsimd

                def head_sums(i, p):
                    chain = Chain(pool, c.chain_p, i * 4)
                    pool.wait_ge(c.a_ready.sem, c.a_ready.at(i + 1))
                    src = T[p][:, :, :, 0:D].rearrange("p a n (h d) -> p (a n) h d", h=H)
                    for width, dst in ((8, s8), (4, s4), (2, s2)):
                        chain(g.tensor_tensor(dst[:, :, :, :], src[:, :, :, 0:width], src[:, :, :, width:2 * width], ALU.add))
                        src = dst[:, :, :, :]
                    chain(g.tensor_tensor(T[p][:, :, :, D:WD], src[:, :, :, 0].rearrange("p (a n) h -> p a n h", a=2),
                                          src[:, :, :, 1].rearrange("p (a n) h -> p a n h", a=2), ALU.add))
                    pool.wait_ge(c.c_ps.sem, c.c_ps.at(i))
                    g.tensor_tensor(T[p][:, 0, :, D:WD], T[p][:, 0, :, D:WD], W["beta"], ALU.mult)
                    g.tensor_copy(R[:, NP * D:].rearrange("p (n h) -> p n h", n=NP), T[p][:, 1, :, D:WD])\
                        .then_inc(c.km_ready.sem, 1)

                skewed(pool, [(0, head_sums)])

            @block.scalar
            def _(act):
                def value(i, p):
                    act.wait_ge(c.v_ps.sem, c.v_ps.at(i + 1))
                    act.wait_ge(c.h_ready.sem, c.h_ready.at(i))
                    nc.scalar.copy(v[:, :], bank_v[:, 0:D]).then_inc(c.v_ready.sem, 1)

                def even_orders(i, p):
                    for n in range(2):
                        if n == 0:
                            act.wait_ge(c.k_ready.sem, c.k_ready.at(i + 1))
                        else:
                            act.wait_ge(c.e_ready.sem, c.e_ready.at(2 * i + 1))
                        nc.scalar.activation(square[:, :, :], T[p][:, :, n, 0:D], ACT.Square).then_inc(c.chain_a.sem, 1)
                        act.wait_ge(c.chain_a.sem, c.chain_a.at(2 * i + n + 2))
                        nc.scalar.activation(T[p][:, :, 2 * n + 1, 0:D], square[:, :, :], ACT.Identity, scale=2.0,
                                             bias=minus1[:, :]).then_inc(c.e_ready.sem, 1)

                def running_sums(i, p):
                    act.wait_ge(c.c_ps.sem, c.c_ps.at(i + 1))
                    act.wait_ge(c.o_ready.sem, c.o_ready.at(i))
                    for n in range(NP):
                        nc.scalar.mul(CS[:, n, 0:D], bank_c[n // 2][:, n % 2 * D:(n % 2 + 1) * D], float(beta[n]))
                    nc.scalar.copy(CS[:, :, D:WD], bank_c[2][:, D:D + NP * H].rearrange("p (n h) -> p n h", n=NP))\
                        .then_inc(c.c_ready.sem, 1)

                def normalised(i, p):
                    act.wait_ge(c.xt_ps.sem, c.xt_ps.at(i + 1))
                    act.wait_ge(c.v_ps.sem, c.v_ps.at(i - 1))
                    nc.scalar.copy(xT[p][:, :, :], bank_x[:, 0:D].rearrange("p (j t) -> p j t", j=KD))\
                        .then_inc(c.xT_ready.sem, 1)

                def output(i, p):
                    act.wait_ge(c.ot_ps.sem, c.ot_ps.at(i + 1))
                    act.wait_ge(c.y_ps.sem, c.y_ps.at(i))
                    nc.scalar.copy(oT[:, :, :], bank_o[:, 0:D].rearrange("p (j q) -> p j q", j=KD))\
                        .then_inc(c.oT_ready.sem, 1)

                nc.scalar.activation(minus1[:, :], c.one[:, :], ACT.Identity, scale=-1.0).then_inc(c.chain_a.sem, 1)
                act.wait_ge(c.chain_a.sem, c.chain_a.at(1))
                skewed(act, [(1, value), (1, even_orders), (2, running_sums), (0, normalised), (3, output)])

            @block.tensor
            def _(pe):
                def projected(i, p):
                    pe.wait_ge(c.xT_ready.sem, c.xT_ready.at(i + 1))
                    pe.wait_ge(c.k_ready.sem, c.k_ready.at(i))
                    for kd in range(KD):
                        last = nc.tensor.matmul(bank_qk[:, :], xT[p][:, kd, :], win[:, kd, 0:2 * D],
                                                start=kd == 0, stop=kd == KD - 1)
                    last.then_inc(c.k_ps.sem, 1)
                    pe.wait_ge(c.v_ready.sem, c.v_ready.at(i))
                    for kd in range(KD):
                        last = nc.tensor.matmul(bank_v[:, 0:D], xT[p][:, kd, :], win[:, kd, 2 * D:3 * D],
                                                start=kd == 0, stop=kd == KD - 1)
                    last.then_inc(c.v_ps.sem, 1)

                def projection(i, p):
                    pe.wait_ge(c.oT_ready.sem, c.oT_ready.at(i + 1))
                    pe.wait_ge(c.x_added.sem, c.x_added.at(i))
                    for k in range(KD):
                        last = nc.tensor.matmul(bank_y[:, 0:D], oT[:, k, :], wo[:, k, :], start=k == 0, stop=k == KD - 1)
                    last.then_inc(c.y_ps.sem, 1)

                def running_sums(i, p):
                    pe.wait_ge(c.h_ready.sem, c.h_ready.at(i + 1))
                    pe.wait_ge(c.km_ready.sem, c.km_ready.at(i + 1))
                    pe.wait_ge(c.c_ready.sem, c.c_ready.at(i))
                    for n in range(3):
                        part = R[:, 512 * n:min(512 * (n + 1), NP * WD)]
                        last = nc.tensor.matmul(bank_c[n][:, 0:part.shape[1]], c.upto[:, :], part, start=True, stop=True)
                    last.then_inc(c.c_ps.sem, 1)

                def normalised(i, p):
                    pe.wait_ge(c.xn_ready.sem, c.xn_ready.at(i + 1))
                    pe.wait_ge(c.xT_ready.sem, c.xT_ready.at(i))
                    for k in range(KD):
                        last = nc.tensor.transpose(bank_x[:, k * S:(k + 1) * S], xn[:, k * P:(k + 1) * P],
                                                   c.ident[:, :])
                    last.then_inc(c.xt_ps.sem, 1)

                def output(i, p):
                    pe.wait_ge(c.o_ready.sem, c.o_ready.at(i + 1))
                    pe.wait_ge(c.oT_ready.sem, c.oT_ready.at(i))
                    for k in range(KD):
                        last = nc.tensor.transpose(bank_o[:, k * S:(k + 1) * S], o[:, k * P:(k + 1) * P],
                                                   c.ident[:, :])
                    last.then_inc(c.ot_ps.sem, 1)

                skewed(pe, [(1, projected), (4, projection), (2, running_sums), (0, normalised), (3, output)])

            @block.sync
            def _(sp):
                prefetch(c, sp, following)
                prefetched(c, sp, following)
        c.passed(chain_v=B * KA, chain_o=B * KO, chain_p=4 * B, chain_a=2 * B + 1, xn_ready=B, xt_ps=B, xT_ready=B, k_ps=B,
                 k_ready=B, v_ps=B, v_ready=B, e_ready=2 * B, a_ready=B, h_ready=B, km_ready=B, c_ps=B, c_ready=B,
                 o_ready=B, ot_ps=B, oT_ready=B, y_ps=B, x_added=B, fetched=16 * len(following))


def shift_sequence(c, sp, xin, shifted, b):
    sp.dma_start(shifted[1:P, b, :], xin[0:P - 1, b, P:D]).then_inc(c.shifted.sem, 16)


def l3_layer_weights(c, w, W, layer):
    n = "L3_ffn_"
    FC = L3_HID // P
    W.add("wqkv", w[n + "wqkv"][layer], P, KD, 3 * 512)
    W.add("wo", w[n + "wo"][layer], P, 4, D)
    W.add("scale", w[n + "qk_scale"][layer], P, 2, 64)
    W.add("cos", w["rotary_cos"], P, 2, 64)
    W.add("sin", w["rotary_sin"], P, 2, 64)
    W.add("w1", w[n + "w1"][layer], P, KD, 2 * L3_HID)
    W.add("w2", w[n + "w2"][layer], P, FC, D)
    W.add("lg", w[n + "ln_g"][layer], P, KD)
    W.add("lb", w[n + "ln_b"][layer], P, KD)
    W.add("b1", w[n + "b1"][layer], P, 2, FC)
    W.add("b2", w[n + "b2"][layer], P, D)


def l3_ffn_weights(c, w, W):
    l3_layer_weights(c, w, W, 0)


def l3_ffn(c, W, following):
    with ExitStack() as ctx:
        xin = c.sb(ctx, "l3_xin", [P, B, D])
        shifted = c.ctxT[:, 0, :].rearrange("p (b t) -> p b t", b=B)
        squares = c.ctxT[:, 1, 0:1024].rearrange("p (a h d) -> p a h d", a=2, h=8)
        second = Weights(c.arenas[0])
        l3_layer_weights(c, c.w, second, 1)
        layernorm(c, beside=lambda dve: c.nc.vector.memset(shifted[:, :, :], 0.0))
        with c.nc.Block() as block:
            @block.vector
            def _(dve):
                skewed(dve, [(0, lambda i, p: c.nc.vector.tensor_scalar(
                    xin[:, i, :], c.x[:, i, :], c.mv[:, i, 0:1], c.rstd[:, bass.ds(i, 1)],
                    ALU.subtract, ALU.mult).then_inc(c.xn_ready.sem, 1))], span=4)

            @block.sync
            def _(sp):
                with sp.Fori(0, B) as b:
                    sp.wait_ge(c.xn_ready.sem, c.xn_ready.at(b + 1))
                    shift_sequence(c, sp, xin, shifted, b)
                sp.wait_ge(c.shifted.sem, c.shifted.at(16 * B))
        c.passed(xn_ready=B, shifted=16 * B)
        for layer, weights in enumerate((W, second)):
            rotary = {n: weights[n] for n in ("wqkv", "cos", "sin", "scale")} | {"shifted": shifted, "squares": squares}
            attention(c, f"l3l{layer}", 2, 1, 64, (None, None, None, weights["wo"]), q_scale=[8.0] * 2, rotary=rotary,
                      into=xin, mask_of=lambda g, t, i: (None, per_head(c.causal_add[:, :])),
                      following=second.pairs if layer == 0 else [])
            gated_mlp(c, weights, layer, xin, shifted)
        with c.nc.Block() as block:
            @block.vector
            def _(dve):
                c.nc.vector.tensor_tensor(c.x[:, :, :], c.x[:, :, :], xin[:, :, :], ALU.add)


def gated_mlp(c, W, layer, xin, shifted):
    nc, FC, TB, TW = c.nc, L3_HID // P, 4, 512
    TT = TW // P
    name = f"l3m{layer}"
    layernorm(c, parts=2, second_half=shifted)
    with ExitStack() as ctx:
        sb = lambda n, shape: c.sb(ctx, f"{name}_{n}", shape)
        w1, w2, lg, lb, b1, b2 = (W[n] for n in ("w1", "w2", "lg", "lb", "b1", "b2"))
        hs, hT = [sb(f"hs{i}", [P, D]) for i in range(2)], sb("hT", [P, KD, B * S])
        G = [sb(f"G{i}", [P, TW]) for i in range(2)]
        u, yb = sb("u", [P, FC, TW]), sb("yb", [P, D])
        bank_x, bank_a, bank_g, bank_y = c.bank[0], c.bank[1:3], c.bank[3:5], c.bank[5:8]
        Y = len(bank_y)
        with nc.Block() as block:
            @block.vector
            def _(dve):
                def normalised(i, p):
                    dve.wait_ge(c.xt_ps.sem, c.xt_ps.at(i - 1))
                    for cols, src in ((slice(0, P), xin[:, i, 0:P]), (slice(P, D), shifted[:, i, :])):
                        last = nc.vector.tensor_scalar(hs[p][:, cols], src, c.mv[:, i, 0:1], c.rstd[:, bass.ds(i, 1)],
                                                       ALU.subtract, ALU.mult)
                    last.then_inc(c.xn_ready.sem, 1)

                def scaled(i):
                    dve.wait_ge(c.xt_ps.sem, c.xt_ps.at(i + 1))
                    for j in range(KD):
                        last = nc.vector.tensor_scalar(hT[:, j, bass.ds(i * S, S)], bank_x[:, j * S:(j + 1) * S],
                                                       lg[:, j:j + 1], lb[:, j:j + 1], ALU.mult, ALU.add)
                    last.then_inc(c.xT_ready.sem, 1)

                def gated(tb, f):
                    n = tb * FC + f
                    dve.wait_ge(c.h_ready.sem, c.h_ready.at(n + 1))
                    dve.wait_ge(c.l_ps.sem, c.l_ps.at(n + 1))
                    if f == 0:
                        dve.wait_ge(c.y_ps.sem, c.y_ps.at(tb * TT))
                    nc.vector.scalar_tensor_tensor(out=u[:, f, :], in0=bank_a[f % 2][:, :],
                                                   scalar=b1[:, 0, f:f + 1], in1=G[f % 2][:, :],
                                                   op0=ALU.add, op1=ALU.mult).then_inc(c.a_ready.sem, 1)

                def tile(tb, followed):
                    for f in range(FC):
                        if followed and f <= TT:
                            if f < TT:
                                normalised((tb + 1) * TT + f, f % 2)
                            if f > 0:
                                scaled((tb + 1) * TT + f - 1)
                        gated(tb, f)
                    chain = Chain(dve, c.chain_v, tb * TT)
                    for tt in range(TT):
                        b = tb * TT + tt
                        dve.wait_ge(c.y_ps.sem, c.y_ps.at(b + 1))
                        dve.wait_ge(c.x_added.sem, c.x_added.at(b))
                        chain(nc.vector.tensor_tensor(yb[:, :], bank_y[tt % Y][:, 0:D], b2[:, :], ALU.add))
                        nc.vector.tensor_tensor(xin[:, b, :], xin[:, b, :], yb[:, :], ALU.add)\
                            .then_inc(c.x_added.sem, 1)

                for t in range(TT + 1):
                    if t < TT:
                        normalised(t, t % 2)
                    if t > 0:
                        scaled(t - 1)
                with dve.Fori(0, TB - 1) as tb:
                    tile(tb, True)
                tile(TB - 1, False)

            @block.tensor
            def _(pe):
                def transposes(i, p):
                    pe.wait_ge(c.xn_ready.sem, c.xn_ready.at(i + 1))
                    pe.wait_ge(c.xT_ready.sem, c.xT_ready.at(i))
                    for j in range(KD):
                        last = nc.tensor.transpose(bank_x[:, j * S:(j + 1) * S], hs[p][:, j * P:(j + 1) * P],
                                                   c.ident[:, :])
                    last.then_inc(c.xt_ps.sem, 1)

                def tile(tb, followed):
                    pe.wait_ge(c.xT_ready.sem, c.xT_ready.at((tb + 1) * TT))
                    for f in range(FC):
                        n = tb * FC + f
                        pe.wait_ge(c.a_ready.sem, c.a_ready.at(n - 1))
                        for kd in range(KD):
                            last = nc.tensor.matmul(bank_g[f % 2][:, :], w1[:, kd, L3_HID + f * P:L3_HID + (f + 1) * P],
                                                    hT[:, kd, bass.ds(tb * TW, TW)], start=kd == 0, stop=kd == KD - 1)
                        last.then_inc(c.h_ps.sem, 1)
                        for kd in range(KD):
                            last = nc.tensor.matmul(bank_a[f % 2][:, :], w1[:, kd, f * P:(f + 1) * P],
                                                    hT[:, kd, bass.ds(tb * TW, TW)], start=kd == 0, stop=kd == KD - 1)
                        last.then_inc(c.l_ps.sem, 1)
                        if followed and f < TT:
                            transposes((tb + 1) * TT + f, f % 2)
                    for tt in range(TT):
                        pe.wait_ge(c.x_added.sem, c.x_added.at(tb * TT + tt - Y + 1))
                        for f in range(FC):
                            if tt == 0:
                                pe.wait_ge(c.a_ready.sem, c.a_ready.at(tb * FC + f + 1))
                            last = nc.tensor.matmul(bank_y[tt % Y][:, 0:D], u[:, f, tt * P:(tt + 1) * P], w2[:, f, :],
                                                    start=f == 0, stop=f == FC - 1)
                        last.then_inc(c.y_ps.sem, 1)

                for t in range(TT):
                    transposes(t, t % 2)
                with pe.Fori(0, TB - 1) as tb:
                    tile(tb, True)
                tile(TB - 1, False)

            @block.scalar
            def _(act):
                with act.Fori(0, TB) as tb:
                    for f in range(FC):
                        n = tb * FC + f
                        act.wait_ge(c.h_ps.sem, c.h_ps.at(n + 1))
                        act.wait_ge(c.a_ready.sem, c.a_ready.at(n - 1))
                        nc.scalar.activation(G[f % 2][:, :], bank_g[f % 2][:, :], ACT.Gelu,
                                             bias=b1[:, 1, f:f + 1]).then_inc(c.h_ready.sem, 1)

            if layer == 0:
                @block.sync
                def _(sp):
                    with sp.Fori(0, B) as b:
                        sp.wait_ge(c.x_added.sem, c.x_added.at(b + 1))
                        shift_sequence(c, sp, xin, shifted, b)
                    sp.wait_ge(c.shifted.sem, c.shifted.at(16 * B))
        c.passed(xn_ready=B, xt_ps=B, xT_ready=B)
        c.passed(h_ps=TB * FC, l_ps=TB * FC, h_ready=TB * FC, a_ready=TB * FC, y_ps=B, x_added=B, chain_v=B,
                 shifted=16 * B * (layer == 0))


STEPS = [l0_attn, l0_xattn, l0_ffn, l1_attn, l1_xattn, l1_ffn, l2_attn, l2_xattn, l2_ffn, l3_attn, l3_xattn, l3_ffn]
WEIGHTS = [l0_attn_weights, l0_xattn_weights, l0_ffn_weights, l1_attn_weights, l1_xattn_weights, l1_ffn_weights,
           l2_attn_weights, l2_xattn_weights, l2_ffn_weights, l3_attn_weights, l3_xattn_weights, l3_ffn_weights]


def decoder(nc, w, out):
    with ExitStack() as ctx:
        c = Core(nc, ctx)
        c.hm16, c.hm64 = c.sb(ctx, "hm16", [P, 8]), c.sb(ctx, "hm64", [P, 2])
        c.one = c.sb(ctx, "one", [P, 1])
        c.ones, c.earlier, c.upto = (c.sb(ctx, n, [P, P]) for n in ("ones", "earlier", "upto"))
        c.w = w
        c.xn_rows, c.rows_out = nc.dram_tensor("xn_rows", (B * S, D), F32).ap(), nc.dram_tensor("rows_out", (ROWS, D), F32).ap()
        parts = 8
        zeros = c.sb(ctx, "zeros", [P, ROWS // P // parts * D])
        c.mask_int = c.sb(ctx, "mask_int", [P, B, S], I32)
        arenas = c.arenas = [c.sb(ctx, f"arena{i}", [P, ARENA]) for i in range(2)]
        weights = {}
        for n in SUBLAYERS:
            weights[n] = Weights(arenas[n % 2])
            WEIGHTS[n](c, w, weights[n])
        first = SUBLAYERS[0]
        if first > 1:
            weights[first].pairs.append((c.ctxT[:, :, :], w["ctx_1024"]))
        with nc.Block() as block:
            @block.sync
            def _(sp):
                for s in c.sig.values():
                    if s.start:
                        sp.sem_inc(s.sem, s.start)

            @block.gpsimd
            def _(pool):
                nc.gpsimd.memset(zeros[:, :], 0.0)
        with nc.Block() as block:
            constants = [(c.one[:, :], w["one"]), (c.ones[:, :], w["ones"]), (c.earlier[:, :], w["earlier"]),
                         (c.upto[:, :], w["upto"])]
            pairs = [(c.ident[:, :], w["ident"]), (c.causal_add[:, :], w["causal_add"]), (c.hm16[:, :], w["hm16"]),
                     (c.hm64[:, :], w["hm64"])] + constants + weights[first].pairs

            @block.sync
            def _(sp):
                sp.dma_start(c.x[:, :, :], w["x"]).then_inc(c.loaded.sem, 16)
                prefetch(c, sp, pairs)
                for part, loaded in zip(weights[first].parts, c.part_loaded):
                    for dst, src in part:
                        sp.dma_start(dst, src).then_inc(loaded.sem, 16)
                prefetched(c, sp, pairs)

            @block.vector
            def _(dve):
                dve.wait_ge(c.loaded.sem, c.loaded.at(16))
                skewed(dve, [(0, lambda b, p: nc.vector.bn_stats(c.stats[:, b, 0, :], c.x[:, b, :]))], span=4)
        c.passed(loaded=16, fetched=16 * len(pairs))
        with nc.Block() as block:
            @block.sync
            def _(sp):
                part = c.rows_out.rearrange("(r p t) d -> r p (t d)", p=P, r=parts)
                for r in range(parts):
                    sp.dma_start(part[r], zeros[:, :]).then_inc(c.cleared.sem, 16)
        c.passed(cleared=16 * parts)
        for n in SUBLAYERS:
            STEPS[n](c, weights[n], weights[n + 1].pairs if n + 1 in weights else [])
        with nc.Block() as block:
            @block.sync
            def _(sp):
                sp.dma_start(out, c.x[:, :, :]).then_inc(c.stored.sem, 16)
                sp.wait_ge(c.stored.sem, c.stored.at(16))


def layout(inputs):
    a = {k: np.asarray(v) for k, v in inputs.items()}
    cont = np.ascontiguousarray

    def rows(m):
        return cont(m.reshape(-1, P, m.shape[1]).transpose(1, 0, 2))

    def column(m):
        return cont(m.reshape(-1, P).T)

    def everywhere(m):
        return cont(np.broadcast_to(m, (P,) + m.shape))

    w = {"x": cont(a["x"].transpose(1, 0, 2)), "ctx_1024": rows(a["ctx_1024"].reshape(B * S, D).T)}
    w["mask_Bx1xSxS2_ik1"] = cont(a["mask_Bx1xSxS2_ik1"][:, 0].transpose(1, 0, 2))
    w["mask_BxSxS2_if1"] = cont(a["mask_BxSxS2_if1"].transpose(1, 0, 2))
    for n in ("L0_attn_W_qkv", "L0_attn_W_out", "L0_xattn_Wq", "L0_xattn_Wkv", "L0_xattn_Wout", "L0_ffn_Wg",
              "L1_attn_Wq", "L1_attn_Wk", "L1_attn_Wv", "L1_attn_Wout", "L1_ffn_Wg", "L2_ffn_wg1"):
        w[n] = rows(a[n])
    for n in ("L1_xattn_WQ_w", "L1_xattn_WK_w", "L1_xattn_WV_w", "L1_xattn_WO_w", "L2_attn_W_in", "L2_attn_W_out",
              "L2_xattn_Wq", "L2_xattn_Wk", "L2_xattn_Wv", "L2_xattn_Wo", "L3_attn_Wq", "L3_attn_Wk", "L3_attn_Wv",
              "L3_attn_Wo", "L3_xattn_Wq", "L3_xattn_Wk", "L3_xattn_Wv", "L3_xattn_Wo"):
        w[n] = rows(a[n].T)
    for n in ("L1_attn_norm_w", "L1_xattn_WQ_b", "L1_xattn_WK_b", "L3_attn_bq", "L3_attn_bk", "L3_xattn_bq",
              "L3_xattn_bk"):
        w[n] = column(a[n])
    for n in ("L0_xattn_bout", "L1_xattn_WV_b", "L1_xattn_WO_b", "L3_attn_bv", "L3_attn_bo", "L3_xattn_bv",
              "L3_xattn_bo"):
        w[n] = everywhere(a[n])
    for n in "qk":
        w[f"L1_attn_W{n}T"] = rows(a[f"L1_attn_W{n}"].T)
        f = a[f"L1_attn_W{n}f"]
        wide = np.zeros((D, D), f.dtype)
        for h in range(D // 16):
            wide[16 * h:16 * h + 16, 16 * h:16 * h + 16] = f
        w[f"L1_attn_W{n}f"] = rows(wide)
    for n in ("L0_ffn", "L1_ffn"):
        w[n + "_W1"] = cont(a[n + "_W1"].reshape(8, KD, P, 1024).transpose(0, 2, 1, 3))
        w[n + "_W2"] = cont(a[n + "_W2"].reshape(8, 8, P, D).transpose(0, 2, 1, 3))
        w[n + "_b1"] = cont(a[n + "_b1"].reshape(8, 8, P).transpose(2, 0, 1))
        w[n + "_b2"] = everywhere(a[n + "_b2"])
    w["L0_ffn_bg"] = everywhere(a["L0_ffn_bg"])
    w["L2_ffn_bg1"] = cont(a["L2_ffn_bg1"][:, None])
    w["L2_ffn_wg2"] = a["L2_ffn_wg2"]
    w["L2_ffn_bg2"] = everywhere(a["L2_ffn_bg2"][:20])
    w["L2_ffn_We"] = cont(a["L2_ffn_We"].reshape(20, KD, P, D).transpose(2, 1, 0, 3))
    w["L2_ffn_be"] = a["L2_ffn_be"]
    n = "L3_ffn_"
    HID = int(D * 4 * 2 / 3)
    short = -HID % P
    w[n + "w1"] = np.stack([rows(np.pad(v.reshape(D, 2, HID), ((0, 0), (0, 0), (0, short))).reshape(D, -1))
                            for v in a[n + "w1"]])
    for m in ("wqkv", "wo"):
        w[n + m] = np.stack([rows(v) for v in a[n + m]])
    w[n + "w2"] = np.stack([rows(np.pad(v, ((0, short), (0, 0)))) for v in a[n + "w2"]])
    w[n + "ln_g"], w[n + "ln_b"] = (np.stack([column(v) for v in a[n + m]]) for m in ("ln_g", "ln_b"))
    w[n + "b1"] = cont(np.pad(a[n + "b1"].reshape(2, 2, HID), ((0, 0), (0, 0), (0, short)))
                       .reshape(2, 2, -1, P).transpose(0, 3, 1, 2))
    w[n + "b2"] = np.stack([everywhere(v) for v in a[n + "b2"]])
    w[n + "qk_scale"] = np.stack([everywhere(np.stack([q, k])) for q, k in zip(a[n + "q_scale"], a[n + "k_scale"])])
    f32 = np.float32
    q, k = np.arange(S)[:, None], np.arange(S)[None, :]
    w["ident"] = np.eye(P, dtype=f32)
    w["causal_T"] = (q <= k).astype(f32)
    w["causal_add"] = np.where(k <= q, 0.0, NEG).astype(f32)
    w["minus2_T"] = np.where(q <= k, 0.0, -2.0).astype(f32)
    w["window_add"] = np.where((k <= q) & (k >= q - 64), 0.0, NEG).astype(f32)
    slopes = np.array([(2 ** (-2 ** (-(math.log2(16) - 3)))) ** (i + 1) for i in range(16)], f32)
    w["alibi"] = np.where(k[:, None] <= q[:, None], slopes[None, :, None] * (k - q)[:, None].astype(f32), f32(NEG)).astype(f32)
    p = np.arange(P)[:, None]
    w["hm16"] = (p // 16 == np.arange(8)[None]).astype(f32)
    w["hm64"] = (p // 64 == np.arange(2)[None]).astype(f32)
    w["ones"] = np.ones((P, P), f32)
    w["earlier"] = (q < k).astype(f32)
    w["upto"] = (q <= k).astype(f32)
    for n in (8, 20):
        w[f"rev{n}"] = everywhere(np.arange(n, 0, -1).astype(f32))
    dh, window = 64, 128
    even = np.arange(0, dh, 2, dtype=f32)
    turn = np.arange(S, dtype=f32)[:, None] * (f32(1.0) / f32(10000.0) ** (even / f32(dh)))[None]
    grow = ((even + f32(0.4 * dh)) / f32(1.4 * dh))[None] ** ((np.arange(S, dtype=f32) - S // 2)
                                                              / f32(window // 2))[:, None]
    cos, sin = np.cos(turn), np.sin(turn)
    w["rotary_cos"] = np.stack([np.concatenate([cos * g, cos * g], 1) for g in (grow, 1 / grow)], 1).astype(f32)
    w["rotary_sin"] = np.stack([np.concatenate([-sin * g, sin * g], 1) for g in (grow, 1 / grow)], 1).astype(f32)
    w["block_limits"] = everywhere(np.array([-1.0] + [WIDTH * i for i in range(1, MOST)], f32))
    w["chebyshev_beta"] = everywhere(np.repeat(chebyshev_beta()[:, None], 16, 1))
    w["numbers"] = everywhere(np.arange(WIDTH, dtype=f32))
    w["tokens"] = (np.arange(2 * B)[None] % B * S + p).astype(f32)
    w["one"] = np.ones((P, 1), f32)
    return w


def kernel(**inputs):
    import concourse.bacc as bacc
    from concourse.bass_utils import run_bass_kernel_spmd

    nc = bacc.Bacc("TRN2", target_bir_lowering=False, num_devices=1)
    arrays = {f"in_{k}_dram": v for k, v in layout(inputs).items()}
    w = {k: nc.dram_tensor(f"in_{k}_dram", v.shape, mybir.dt.from_np(v.dtype), kind="ExternalInput").ap()
         for k, v in ((n[3:-5], v) for n, v in arrays.items())}
    out = nc.dram_tensor("out_0_dram", (S, B, D), F32, kind="ExternalOutput").ap()
    decoder(nc, w, out)
    got = run_bass_kernel_spmd(nc, [arrays], core_ids=[0]).results[0]["out_0_dram"]
    return np.ascontiguousarray(np.asarray(got).transpose(1, 0, 2))
```
